# Optimizing a Trainium2 kernel written in Bass

```python
import numpy as np
import jax
import jax.numpy as jnp

def _softmax(x, axis=-1):
    return jax.nn.softmax(x, axis=axis)

def _gelu(x):
    return jax.nn.gelu(x, approximate=True)

def _silu(x):
    return jax.nn.silu(x)

def _sigmoid(x):
    return jax.nn.sigmoid(x)

def _layernorm(x, axis=-1, eps=1e-05):
    m = jnp.mean(x, axis=axis, keepdims=True)
    v = jnp.var(x, axis=axis, keepdims=True)
    return (x - m) / jnp.sqrt(v + eps)

def _scatter_add(tgt, idx, src, axis=0):
    return tgt.at[idx].add(src)

def _segment_sum(src, seg, n):
    return jax.ops.segment_sum(src, seg, n)
kernel_name = 'mk_seq_postln_d2_jaxref_r8_d92606'

def setup_inputs(seed: int=0):
    np.random.seed(seed)
    _w = jnp.asarray

    def _L0_attn_setup():
        import jax, jax.numpy as jnp
        import numpy as np
        HEADS = 4
        DIM_HEAD = 32
        EPS = 1e-05
        key = jax.random.key(seed)
        ks = jax.random.split(key, 6)
        b, n, dim = (8, 512, 128)
        hidden = HEADS * DIM_HEAD
        x = jax.random.normal(ks[0], (b, n, dim), dtype=jnp.float32)
        gamma = jnp.ones((1, 1, dim), dtype=jnp.float32)
        beta = jnp.zeros((1, 1, dim), dtype=jnp.float32)
        w_qkv = jax.random.normal(ks[1], (dim, hidden * 3), dtype=jnp.float32) / np.sqrt(dim)
        w_out = jax.random.normal(ks[2], (hidden, dim), dtype=jnp.float32) / np.sqrt(hidden)
        b_out = jnp.zeros((dim,), dtype=jnp.float32)
        return {'x': x, 'gamma': gamma, 'beta': beta, 'w_qkv': w_qkv, 'w_out': w_out, 'b_out': b_out}
    _L0_attn_in = _L0_attn_setup()

    def _L0_ffn_setup():
        import jax, jax.numpy as jnp
        import numpy as np
        NUM_EXPERTS = 8
        TOP_K = 2
        ROUTE_SCALE = 1.0
        DIM = 128
        HID = 128
        B, S = (2, 512)
        key = jax.random.key(seed)
        ks = jax.random.split(key, 9)
        sc = 0.05
        return {'x': jax.random.normal(ks[0], (B, S, DIM), dtype=jnp.float32), 'gate_w': jax.random.normal(ks[1], (NUM_EXPERTS, DIM), dtype=jnp.float32) * sc, 'w1': jax.random.normal(ks[2], (NUM_EXPERTS, HID, DIM), dtype=jnp.float32) * sc, 'w2': jax.random.normal(ks[3], (NUM_EXPERTS, DIM, HID), dtype=jnp.float32) * sc, 'w3': jax.random.normal(ks[4], (NUM_EXPERTS, HID, DIM), dtype=jnp.float32) * sc, 'sw1': jax.random.normal(ks[5], (HID, DIM), dtype=jnp.float32) * sc, 'sw2': jax.random.normal(ks[6], (DIM, HID), dtype=jnp.float32) * sc, 'sw3': jax.random.normal(ks[7], (HID, DIM), dtype=jnp.float32) * sc, 'expert_bias': jnp.zeros((NUM_EXPERTS,), dtype=jnp.float32)}
    _L0_ffn_in = _L0_ffn_setup()

    def _L1_attn_setup():
        import jax, jax.numpy as jnp
        import numpy as np
        B, L, D_MODEL, H, HD, FD = (1, 128, 128, 16, 64, 64)
        EPS = 1e-12

        def _heads(t):
            b, l, _ = t.shape
            return t.reshape(b, l, H, HD).transpose(0, 2, 1, 3)

        def _feature_map(t, K):
            f = jnp.einsum('hdf,bhld->bhlf', K, t)
            feats = jnp.concatenate([jax.nn.softmax(f, axis=-1), jax.nn.softmax(-f, axis=-1)], axis=-1)
            return jnp.maximum(feats, EPS)
        key = jax.random.key(seed)
        ks = jax.random.split(key, 7)
        s = 1.0 / np.sqrt(D_MODEL)
        return {'x': jax.random.normal(ks[0], (B, L, D_MODEL), jnp.float32), 'Wq': jax.random.normal(ks[1], (D_MODEL, H * HD), jnp.float32) * s, 'Wk': jax.random.normal(ks[2], (D_MODEL, H * HD), jnp.float32) * s, 'Wv': jax.random.normal(ks[3], (D_MODEL, H * HD), jnp.float32) * s, 'Wo': jax.random.normal(ks[4], (H * HD, D_MODEL), jnp.float32) * s, 'Kq': jax.random.normal(ks[5], (H, HD, FD), jnp.float32) * (1.0 / np.sqrt(HD)), 'Kk': jax.random.normal(ks[6], (H, HD, FD), jnp.float32) * (1.0 / np.sqrt(HD))}
    _L1_attn_in = _L1_attn_setup()

    def _L1_ffn_setup():
        import jax, jax.numpy as jnp
        import numpy as np
        DIM = 128
        DEPTH = 6
        HEADS = 16
        DIM_HEAD = 64
        WINDOW = 32
        INNER = HEADS * DIM_HEAD
        DIM_INNER = int(DIM * 4 * 2 / 3)
        QK_SCALE = 8.0

        def shift_tokens(t):
            a, s = jnp.split(t, 2, -1)
            s = jnp.pad(s, ((0, 0), (1, 0), (0, 0)))[:, :-1]
            return jnp.concatenate([a, s], -1)

        def l2norm(t):
            return t / jnp.maximum(jnp.linalg.norm(t, axis=-1, keepdims=True), 1e-12)

        def rotate_half(x):
            x1, x2 = jnp.split(x, 2, -1)
            return jnp.concatenate([-x2, x1], -1)

        def rotary_tables(n):
            half = jnp.arange(0, DIM_HEAD, 2, dtype=jnp.float32)
            inv_freq = 1.0 / 10000.0 ** (half / DIM_HEAD)
            t = jnp.arange(n, dtype=jnp.float32)
            freqs = t[:, None] * inv_freq[None, :]
            freqs = jnp.concatenate([freqs, freqs], -1)
            base_scale = (half + 0.4 * DIM_HEAD) / (1.4 * DIM_HEAD)
            power = (t - n // 2) / (WINDOW // 2)
            scale = base_scale[None, :] ** power[:, None]
            scale = jnp.concatenate([scale, scale], -1)
            return (freqs, scale)

        def local_attention(q, k, v):
            b, h, n, d = q.shape
            w = WINDOW
            nw = n // w
            bq = q.reshape(b, h, nw, w, d)
            bk = k.reshape(b, h, nw, w, d)
            bv = v.reshape(b, h, nw, w, d)

            def look(t):
                p = jnp.pad(t, ((0, 0), (0, 0), (1, 0), (0, 0), (0, 0)))
                return jnp.concatenate([p[:, :, :nw], p[:, :, 1:]], axis=3)
            bk2, bv2 = (look(bk), look(bv))
            seq = jnp.arange(n).reshape(nw, w)
            seq_p = jnp.pad(seq, ((1, 0), (0, 0)), constant_values=-1)
            jt = jnp.concatenate([seq_p[:nw], seq_p[1:]], axis=1)
            it = seq[:, :, None]
            jb = jt[:, None, :]
            mask = (it < jb) | (it > jb + w) | (jb == -1)
            sim = jnp.einsum('bhwie,bhwje->bhwij', bq, bk2) * QK_SCALE
            sim = jnp.where(mask, -jnp.finfo(sim.dtype).max, sim)
            attn = jax.nn.softmax(sim, -1)
            out = jnp.einsum('bhwij,bhwje->bhwie', attn, bv2)
            return out.reshape(b, h, n, d)

        def attn_layer(x, Wqkv, qs, ksc, Wo):
            b, n, _ = x.shape
            qkv = x @ Wqkv
            q, k, v = jnp.split(qkv, 3, -1)
            sh = lambda t: t.reshape(b, n, HEADS, DIM_HEAD).transpose(0, 2, 1, 3)
            q, k, v = (sh(q), sh(k), sh(v))
            q = l2norm(q) * qs
            k = l2norm(k) * ksc
            freqs, scale = rotary_tables(n)
            cos, sin = (jnp.cos(freqs), jnp.sin(freqs))
            q = q * cos * scale + rotate_half(q) * sin * scale
            inv = 1.0 / scale
            k = k * cos * inv + rotate_half(k) * sin * inv
            out = local_attention(q, k, v)
            out = out.transpose(0, 2, 1, 3).reshape(b, n, INNER)
            return out @ Wo

        def ffn_layer(x, g, bln, W1, b1, W2, b2):
            mu = x.mean(-1, keepdims=True)
            var = ((x - mu) ** 2).mean(-1, keepdims=True)
            xn = (x - mu) / jnp.sqrt(var + 1e-05) * g + bln
            hg = xn @ W1 + b1
            a, gate = jnp.split(hg, 2, -1)
            return a * jax.nn.gelu(gate, approximate=False) @ W2 + b2
        key = jax.random.key(seed)
        ks = jax.random.split(key, 8)
        B, N = (2, 256)
        init = lambda k, shape: jax.random.normal(k, shape, jnp.float32) * 0.02
        return {'x': jax.random.normal(ks[0], (B, N, DIM), jnp.float32), 'Wqkv': init(ks[1], (DEPTH, DIM, 3 * INNER)), 'q_scale': jnp.ones((DEPTH, DIM_HEAD), jnp.float32), 'k_scale': jnp.ones((DEPTH, DIM_HEAD), jnp.float32), 'Wo': init(ks[2], (DEPTH, INNER, DIM)), 'ln_g': jnp.ones((DEPTH, DIM), jnp.float32), 'ln_b': jnp.zeros((DEPTH, DIM), jnp.float32), 'W1': init(ks[3], (DEPTH, DIM, 2 * DIM_INNER)), 'b1': jnp.zeros((DEPTH, 2 * DIM_INNER), jnp.float32), 'W2': init(ks[4], (DEPTH, DIM_INNER, DIM)), 'b2': jnp.zeros((DEPTH, DIM), jnp.float32)}
    _L1_ffn_in = _L1_ffn_setup()
    _d = {'L0_attn_x': _L0_attn_in['x'], 'L0_attn_gamma': _L0_attn_in['gamma'], 'L0_attn_beta': _L0_attn_in['beta'], 'L0_attn_w_qkv': _L0_attn_in['w_qkv'], 'L0_attn_w_out': _L0_attn_in['w_out'], 'L0_attn_b_out': _L0_attn_in['b_out'], 'L0_ffn_gate_w': _L0_ffn_in['gate_w'], 'L0_ffn_w1': _L0_ffn_in['w1'], 'L0_ffn_w2': _L0_ffn_in['w2'], 'L0_ffn_w3': _L0_ffn_in['w3'], 'L0_ffn_sw1': _L0_ffn_in['sw1'], 'L0_ffn_sw2': _L0_ffn_in['sw2'], 'L0_ffn_sw3': _L0_ffn_in['sw3'], 'L0_ffn_expert_bias': _L0_ffn_in['expert_bias'], 'L1_attn_Wq': _L1_attn_in['Wq'], 'L1_attn_Wk': _L1_attn_in['Wk'], 'L1_attn_Wv': _L1_attn_in['Wv'], 'L1_attn_Wo': _L1_attn_in['Wo'], 'L1_attn_Kq': _L1_attn_in['Kq'], 'L1_attn_Kk': _L1_attn_in['Kk'], 'L1_ffn_Wqkv': _L1_ffn_in['Wqkv'], 'L1_ffn_q_scale': _L1_ffn_in['q_scale'], 'L1_ffn_k_scale': _L1_ffn_in['k_scale'], 'L1_ffn_Wo': _L1_ffn_in['Wo'], 'L1_ffn_ln_g': _L1_ffn_in['ln_g'], 'L1_ffn_ln_b': _L1_ffn_in['ln_b'], 'L1_ffn_W1': _L1_ffn_in['W1'], 'L1_ffn_b1': _L1_ffn_in['b1'], 'L1_ffn_W2': _L1_ffn_in['W2'], 'L1_ffn_b2': _L1_ffn_in['b2']}
    _x0 = _d['L0_attn_x']
    _d['L0_attn_x'] = jax.random.normal(jax.random.fold_in(jax.random.key(seed), 1), (16, 256, 128), dtype=_x0.dtype)
    del _x0
    return _d

def reference(L0_attn_x, L0_attn_gamma, L0_attn_beta, L0_attn_w_qkv, L0_attn_w_out, L0_attn_b_out, L0_ffn_gate_w, L0_ffn_w1, L0_ffn_w2, L0_ffn_w3, L0_ffn_sw1, L0_ffn_sw2, L0_ffn_sw3, L0_ffn_expert_bias, L1_attn_Wq, L1_attn_Wk, L1_attn_Wv, L1_attn_Wo, L1_attn_Kq, L1_attn_Kk, L1_ffn_Wqkv, L1_ffn_q_scale, L1_ffn_k_scale, L1_ffn_Wo, L1_ffn_ln_g, L1_ffn_ln_b, L1_ffn_W1, L1_ffn_b1, L1_ffn_W2, L1_ffn_b2):

    def _L0_attn_ref(x, gamma, beta, w_qkv, w_out, b_out):
        import jax, jax.numpy as jnp
        import numpy as np
        HEADS = 4
        DIM_HEAD = 32
        EPS = 1e-05
        b, n, dim = x.shape
        mean = jnp.mean(x, axis=2, keepdims=True)
        var = jnp.var(x, axis=2, keepdims=True)
        xn = (x - mean) / jnp.sqrt(var + EPS) * gamma + beta
        qkv = jnp.einsum('bnc,ck->bnk', xn, w_qkv)
        q, k, v = jnp.split(qkv, 3, axis=2)

        def to_heads(t):
            return t.reshape(b, n, HEADS, DIM_HEAD)
        q, k, v = (to_heads(q), to_heads(k), to_heads(v))
        q = q * DIM_HEAD ** (-0.5)
        k = jax.nn.softmax(k, axis=1)
        context = jnp.einsum('bnhd,bnhe->bhde', k, v)
        out = jnp.einsum('bhde,bnhd->bnhe', context, q)
        out = out.reshape(b, n, HEADS * DIM_HEAD)
        out = jnp.einsum('bnk,kc->bnc', out, w_out) + b_out
        return out + x

    def _L0_ffn_ref(x, gate_w, w1, w2, w3, sw1, sw2, sw3, expert_bias):
        import jax, jax.numpy as jnp
        import numpy as np
        NUM_EXPERTS = 8
        TOP_K = 2
        ROUTE_SCALE = 1.0
        DIM = 128
        HID = 128
        B, S = (2, 512)
        bs, slen, dim = x.shape
        xf = x.reshape(-1, dim)
        scores = jax.nn.sigmoid((xf @ gate_w.T).astype(jnp.float32))
        _, sel = jax.lax.top_k(scores + expert_bias[None, :], TOP_K)
        top_scores = jnp.take_along_axis(scores, sel, axis=1) * ROUTE_SCALE
        flat_sel = sel.reshape(-1)
        order = jnp.argsort(flat_sel, stable=True)
        scores_sorted = top_scores.reshape(-1)[order]
        tok_idx = order // TOP_K
        expert_ids = flat_sel[order]
        routed = xf[tok_idx]
        routed = (routed.astype(jnp.float32) * scores_sorted[:, None]).astype(x.dtype)
        out_r = jnp.zeros_like(routed)
        for e in range(NUM_EXPERTS):
            m = (expert_ids == e)[:, None]
            h = jax.nn.silu(routed @ w1[e].T) * (routed @ w3[e].T)
            out_r = out_r + jnp.where(m, h @ w2[e].T, jnp.zeros((), routed.dtype))
        shared = jax.nn.silu(xf @ sw1.T) * (xf @ sw3.T) @ sw2.T
        out_r = (out_r.astype(jnp.float32) * scores_sorted[:, None]).astype(x.dtype)
        out = shared.at[tok_idx].add(out_r)
        return out.reshape(bs, slen, dim)

    def _L1_attn_ref(x, Wq, Wk, Wv, Wo, Kq, Kk):
        import jax, jax.numpy as jnp
        import numpy as np
        B, L, D_MODEL, H, HD, FD = (1, 128, 128, 16, 64, 64)
        EPS = 1e-12

        def _heads(t):
            b, l, _ = t.shape
            return t.reshape(b, l, H, HD).transpose(0, 2, 1, 3)

        def _feature_map(t, K):
            f = jnp.einsum('hdf,bhld->bhlf', K, t)
            feats = jnp.concatenate([jax.nn.softmax(f, axis=-1), jax.nn.softmax(-f, axis=-1)], axis=-1)
            return jnp.maximum(feats, EPS)
        q = _heads(x @ Wq)
        k = _heads(x @ Wk)
        v = _heads(x @ Wv)
        qf = _feature_map(q, Kq)
        kf = _feature_map(k, Kk)
        kv = jnp.cumsum(kf[:, :, :, None, :] * v[..., None], axis=2)
        o = jnp.einsum('bhlf,bhldf->bhld', qf, kv)
        z = jnp.einsum('bhlf,bhlf->bhl', qf, jnp.cumsum(kf, axis=2)) + EPS
        o = o / z[..., None]
        y = o.transpose(0, 2, 1, 3).reshape(x.shape[0], x.shape[1], H * HD)
        return y @ Wo

    def _L1_ffn_ref(x, Wqkv, q_scale, k_scale, Wo, ln_g, ln_b, W1, b1, W2, b2):
        import jax, jax.numpy as jnp
        import numpy as np
        DIM = 128
        DEPTH = 6
        HEADS = 16
        DIM_HEAD = 64
        WINDOW = 32
        INNER = HEADS * DIM_HEAD
        DIM_INNER = int(DIM * 4 * 2 / 3)
        QK_SCALE = 8.0

        def shift_tokens(t):
            a, s = jnp.split(t, 2, -1)
            s = jnp.pad(s, ((0, 0), (1, 0), (0, 0)))[:, :-1]
            return jnp.concatenate([a, s], -1)

        def l2norm(t):
            return t / jnp.maximum(jnp.linalg.norm(t, axis=-1, keepdims=True), 1e-12)

        def rotate_half(x):
            x1, x2 = jnp.split(x, 2, -1)
            return jnp.concatenate([-x2, x1], -1)

        def rotary_tables(n):
            half = jnp.arange(0, DIM_HEAD, 2, dtype=jnp.float32)
            inv_freq = 1.0 / 10000.0 ** (half / DIM_HEAD)
            t = jnp.arange(n, dtype=jnp.float32)
            freqs = t[:, None] * inv_freq[None, :]
            freqs = jnp.concatenate([freqs, freqs], -1)
            base_scale = (half + 0.4 * DIM_HEAD) / (1.4 * DIM_HEAD)
            power = (t - n // 2) / (WINDOW // 2)
            scale = base_scale[None, :] ** power[:, None]
            scale = jnp.concatenate([scale, scale], -1)
            return (freqs, scale)

        def local_attention(q, k, v):
            b, h, n, d = q.shape
            w = WINDOW
            nw = n // w
            bq = q.reshape(b, h, nw, w, d)
            bk = k.reshape(b, h, nw, w, d)
            bv = v.reshape(b, h, nw, w, d)

            def look(t):
                p = jnp.pad(t, ((0, 0), (0, 0), (1, 0), (0, 0), (0, 0)))
                return jnp.concatenate([p[:, :, :nw], p[:, :, 1:]], axis=3)
            bk2, bv2 = (look(bk), look(bv))
            seq = jnp.arange(n).reshape(nw, w)
            seq_p = jnp.pad(seq, ((1, 0), (0, 0)), constant_values=-1)
            jt = jnp.concatenate([seq_p[:nw], seq_p[1:]], axis=1)
            it = seq[:, :, None]
            jb = jt[:, None, :]
            mask = (it < jb) | (it > jb + w) | (jb == -1)
            sim = jnp.einsum('bhwie,bhwje->bhwij', bq, bk2) * QK_SCALE
            sim = jnp.where(mask, -jnp.finfo(sim.dtype).max, sim)
            attn = jax.nn.softmax(sim, -1)
            out = jnp.einsum('bhwij,bhwje->bhwie', attn, bv2)
            return out.reshape(b, h, n, d)

        def attn_layer(x, Wqkv, qs, ksc, Wo):
            b, n, _ = x.shape
            qkv = x @ Wqkv
            q, k, v = jnp.split(qkv, 3, -1)
            sh = lambda t: t.reshape(b, n, HEADS, DIM_HEAD).transpose(0, 2, 1, 3)
            q, k, v = (sh(q), sh(k), sh(v))
            q = l2norm(q) * qs
            k = l2norm(k) * ksc
            freqs, scale = rotary_tables(n)
            cos, sin = (jnp.cos(freqs), jnp.sin(freqs))
            q = q * cos * scale + rotate_half(q) * sin * scale
            inv = 1.0 / scale
            k = k * cos * inv + rotate_half(k) * sin * inv
            out = local_attention(q, k, v)
            out = out.transpose(0, 2, 1, 3).reshape(b, n, INNER)
            return out @ Wo

        def ffn_layer(x, g, bln, W1, b1, W2, b2):
            mu = x.mean(-1, keepdims=True)
            var = ((x - mu) ** 2).mean(-1, keepdims=True)
            xn = (x - mu) / jnp.sqrt(var + 1e-05) * g + bln
            hg = xn @ W1 + b1
            a, gate = jnp.split(hg, 2, -1)
            return a * jax.nn.gelu(gate, approximate=False) @ W2 + b2
        for i in range(DEPTH):
            x = attn_layer(shift_tokens(x), Wqkv[i], q_scale[i], k_scale[i], Wo[i]) + x
            x = ffn_layer(shift_tokens(x), ln_g[i], ln_b[i], W1[i], b1[i], W2[i], b2[i]) + x
        return x
    x = L0_attn_x
    x = _layernorm(x + _L0_attn_ref(x, L0_attn_gamma, L0_attn_beta, L0_attn_w_qkv, L0_attn_w_out, L0_attn_b_out), axis=-1)
    x = _layernorm(x + _L0_ffn_ref(x, L0_ffn_gate_w, L0_ffn_w1, L0_ffn_w2, L0_ffn_w3, L0_ffn_sw1, L0_ffn_sw2, L0_ffn_sw3, L0_ffn_expert_bias), axis=-1)
    x = _layernorm(x + _L1_attn_ref(x, L1_attn_Wq, L1_attn_Wk, L1_attn_Wv, L1_attn_Wo, L1_attn_Kq, L1_attn_Kk), axis=-1)
    x = _layernorm(x + _L1_ffn_ref(x, L1_ffn_Wqkv, L1_ffn_q_scale, L1_ffn_k_scale, L1_ffn_Wo, L1_ffn_ln_g, L1_ffn_ln_b, L1_ffn_W1, L1_ffn_b1, L1_ffn_W2, L1_ffn_b2), axis=-1)
    return x

_drawn_inputs = setup_inputs


def setup_inputs(seed=0):
    import zlib

    import numpy as np

    out = dict(_drawn_inputs(seed))
    spreads = {'L0_attn_gamma': (1.0, 0.2),
     'L0_attn_beta': (0.0, 0.1),
     'L0_attn_b_out': (0.0, 0.1),
     'L0_ffn_expert_bias': (0.0, 0.294),
     'L1_ffn_q_scale': (1.0, 0.6),
     'L1_ffn_k_scale': (1.0, 0.6),
     'L1_ffn_ln_g': (1.0, 0.6),
     'L1_ffn_ln_b': (0.0, 0.8),
     'L1_ffn_b1': (0.0, 0.8),
     'L1_ffn_b2': (0.0, 0.1)}
    factors = {'L1_ffn_W1': 3.69, 'L1_ffn_W2': 3.629}
    for name, (base, spread) in spreads.items():
        noise = np.random.default_rng([zlib.crc32(name.encode()), seed]).standard_normal(out[name].shape)
        drawn = base * np.exp(spread * noise) if base else spread * noise
        out[name] = jnp.asarray(drawn.astype(out[name].dtype))
    for name, factor in factors.items():
        out[name] = (out[name] * factor).astype(out[name].dtype)
    return out
```

```python
from contextlib import ExitStack

import numpy as np

import concourse.bass as bass
from concourse import mybir

F32 = mybir.dt.float32
BF16 = mybir.dt.bfloat16
ACT = mybir.ActivationFunctionType
ALU = mybir.AluOpType
AX = mybir.AxisListType

P = 128
D = 128
NBLK = 32
NSEQ = 16
SEQ = 256
H = 16
HD = 64
INNER = H * HD
PAIRS = H // 2
DEPTH = 6
WIN = 32
FH = 341
FT = [(0, 128), (128, 128), (256, 85)]
EPS_LN = 1e-5
NEG = -1.0e30


def count(n):
    return n + 1


def norm_stats(nc, ctx, X, tag, residual=None):
    def sb(name, shape):
        return ctx.enter_context(nc.sbuf_tensor(name + tag, shape, F32))

    mean = sb("mean", [P, NBLK])
    rstd = sb("rstd", [P, NBLK])
    with ExitStack() as inner:
        counters = []

        def sem(name):
            counters.append(inner.enter_context(nc.semaphore(name + tag)))
            return counters[-1]

        st = inner.enter_context(nc.sbuf_tensor("lst" + tag, [P, 4, 6], F32))
        mv = inner.enter_context(nc.sbuf_tensor("lmv" + tag, [P, 4, 2], F32))
        ve = inner.enter_context(nc.sbuf_tensor("lve" + tag, [P, NBLK], F32))
        tick = inner.enter_context(nc.sbuf_tensor("ltick" + tag, [P, 1], F32))
        cleared = sem("cleared")
        half = inner.enter_context(nc.sbuf_tensor("lhalf" + tag, [P, NBLK], F32))
        stats = sem("stats")
        with_residual = sem("with_residual")
        means = sem("means")
        kept = sem("kept")
        half_set = sem("half_set")
        powered = sem("powered")
        block = inner.enter_context(nc.Block())

        @block.sync
        def _(sp):
            for s in counters:
                sp.sem_inc(s, 1)

        @block.vector
        def _(dve):
            dve.memset(half[:], -0.5).then_inc(half_set, 1)
            if residual is not None:
                with dve.Fori(0, NBLK // 4) as g:
                    x = X[:, bass.ds(4 * g, 4), :]
                    dve.tensor_tensor(x, x, residual[:, bass.ds(4 * g, 4), :], ALU.add).then_inc(with_residual, 1)
                dve.wait_ge(with_residual, count(NBLK // 4))
            with dve.Fori(0, NBLK // 4) as g:
                dve.wait_ge(kept, count(2 * g))
                for k in range(4):
                    i = dve.bn_stats(st[:, k], X[:, bass.ds(4 * g + k, 1), :].rearrange("p o d -> p (o d)"))
                i.then_inc(stats, 1)
                dve.wait_ge(cleared, count(g))
                dve.wait_ge(stats, count(g + 1))
                dve.memset(tick[:], 0.0).then_inc(cleared, 1)
                for k in range(4):
                    i = dve.bn_aggr(mv[:, k], st[:, k])
                i.then_inc(means, 1)
                dve.wait_ge(means, count(g + 1))
                dve.tensor_copy(mean[:, bass.ds(4 * g, 4)], mv[:, :, 0]).then_inc(kept, 1)
                dve.tensor_scalar(ve[:, bass.ds(4 * g, 4)], mv[:, :, 1], EPS_LN, None, ALU.add).then_inc(kept, 1)

        @block.gpsimd
        def _(pool):
            pool.wait_ge(half_set, count(1))
            pool.wait_ge(kept, count(2 * (NBLK // 4)))
            pool.tensor_tensor(rstd[:], ve[:], half[:], ALU.pow).then_inc(powered, 1)
            pool.wait_ge(powered, count(1))
    return mean, rstd


def norm_stage(nc, X, tag, residual=None, keep=None):
    with ExitStack() as ctx:
        mean, rstd = norm_stats(nc, ctx, X, tag, residual)
        applied = ctx.enter_context(nc.semaphore("applied" + tag))
        block = ctx.enter_context(nc.Block())

        @block.vector
        def _(dve):
            with dve.Fori(0, NBLK // 4) as g:
                for k in range(4):
                    x = X[:, bass.ds(4 * g + k, 1), :].rearrange("p o d -> p (o d)")
                    dve.tensor_scalar(x, x, mean[:, bass.ds(4 * g + k, 1)], rstd[:, bass.ds(4 * g + k, 1)],
                                      ALU.subtract, ALU.mult).then_inc(applied, 1)
                if keep is not None:
                    dve.wait_ge(applied, 4 * g + 4)
                    dve.tensor_copy(keep[:, bass.ds(4 * g, 4), :], X[:, bass.ds(4 * g, 4), :])


def linear_stage(nc, X, c, w):
    with ExitStack() as ctx:
        def sb(name, shape, dt=F32):
            return ctx.enter_context(nc.sbuf_tensor(name, shape, dt))

        counters = []

        def sem(name):
            counters.append(ctx.enter_context(nc.semaphore(name)))
            return counters[-1]

        def psum(name):
            return ctx.enter_context(nc.psum_tensor(name, [P, 512], F32))

        mean, rstd = norm_stats(nc, ctx, X, "_in")
        GS = 4
        wqkv = sb("a_wqkv", [P, 3 * D])
        wout = sb("a_wout", [P, D])
        gamma = sb("a_gamma", [P, 1])
        beta = sb("a_beta", [P, 1])
        bout = sb("a_bout", [P, D])
        bd = sb("a_bd", [P, P])
        xn = sb("a_xn", [P, 2 * GS, D])
        xnT = sb("a_xnT", [P, GS, SEQ])
        nmax = sb("a_nmax", [P, GS])
        ke = sb("a_ke", [P, GS, SEQ])
        ksum = sb("a_ksum", [P, GS])
        krec = sb("a_krec", [P, GS])
        kscale = sb("a_kscale", [P, GS])
        q = sb("a_q", [P, GS, SEQ])
        v = sb("a_v", [P, GS, SEQ])
        ket = sb("a_ket", [P, GS, SEQ])
        cx = sb("a_cx", [P, GS, P])
        oT = sb("a_oT", [P, GS, SEQ])
        A = [psum("a_A0"), psum("a_A1")]
        K = [psum("a_K0"), psum("a_K1")]
        VB = [psum("a_V0"), psum("a_V1")]
        R = [psum("a_R0"), psum("a_R1")]

        loaded = ctx.enter_context(nc.semaphore("a_loaded"))
        normed = sem("a_normed")
        turn_full = sem("a_turn_full")
        turn_drained = sem("a_turn_drained")
        kq_full = sem("a_kq_full")
        v_full = sem("a_v_full")
        k_max = sem("a_k_max")
        k_exp = sem("a_k_exp")
        q_drained = sem("a_q_drained")
        v_drained = sem("a_v_drained")
        k_rec = sem("a_k_rec")
        k_scale = sem("a_k_scale")
        cx_full = sem("a_cx_full")
        cx_drained = sem("a_cx_drained")
        o_full = sem("a_o_full")
        o_drained = sem("a_o_drained")
        y_full = sem("a_y_full")
        y_summed = sem("a_y_summed")
        y_added = sem("a_y_added")
        block = ctx.enter_context(nc.Block())

        @block.sync
        def _(sp):
            for s in counters:
                sp.sem_inc(s, 1)
            sp.dma_start(wqkv[:], w["w_qkv"]).then_inc(loaded, 16)
            sp.dma_start(wout[:], w["w_out"]).then_inc(loaded, 16)
            sp.dma_start(gamma[:], w["gamma"].rearrange("a b d -> d (a b)")).then_inc(loaded, 16)
            sp.dma_start(beta[:], w["beta"].rearrange("a b d -> d (a b)")).then_inc(loaded, 16)
            sp.dma_start(bout[:], w["b_out"].rearrange("(o d) -> o d", o=1).to_broadcast([P, D])).then_inc(loaded, 16)
            sp.dma_start(bd[:], c["heads32"]).then_inc(loaded, 16)

        LOADED = 96

        @block.tensor
        def _(pe):
            pe.wait_ge(loaded, LOADED)
            with pe.Fori(0, NSEQ // GS) as g:
                for u in range(GS):
                    pe.wait_ge(normed, count(2 * GS * g + 2 * u + 2))
                    if u >= 2:
                        pe.wait_ge(turn_drained, count(2 * GS * g + u - 1))
                    else:
                        pe.wait_ge(turn_drained, count(2 * GS * g))
                    for k in range(2):
                        t = pe.transpose(A[u % 2][:, k * P:(k + 1) * P], xn[:, 2 * u + k], c["ident"][:])
                    t.then_inc(turn_full, 1)
                for u in range(GS):
                    pe.wait_ge(turn_drained, count(2 * GS * g + u + 1))
                    if u >= 2:
                        pe.wait_ge(q_drained, count(GS * g + u - 1))
                        pe.wait_ge(v_drained, count(GS * g + u - 1))
                    else:
                        pe.wait_ge(q_drained, count(GS * g))
                        pe.wait_ge(v_drained, count(GS * g))
                    pe.matmul(K[u % 2][:, 0:SEQ], wqkv[:, D:2 * D], xnT[:, u], start=True, stop=True)
                    pe.matmul(K[u % 2][:, SEQ:2 * SEQ], wqkv[:, 0:D], xnT[:, u], start=True, stop=True)\
                        .then_inc(kq_full, 1)
                    for k in range(2):
                        t = pe.matmul(VB[u % 2][:, k * P:(k + 1) * P], xnT[:, u, k * P:(k + 1) * P],
                                      wqkv[:, 2 * D:3 * D], start=True, stop=True)
                    t.then_inc(v_full, 1)
                for u in range(GS):
                    pe.wait_ge(k_exp, count(GS * g + u + 1))
                    pe.wait_ge(turn_drained, count(2 * GS * g + GS + u - 1))
                    for k in range(2):
                        t = pe.transpose(A[u % 2][:, k * P:(k + 1) * P], ke[:, u, k * P:(k + 1) * P], c["ident"][:])
                    t.then_inc(turn_full, 1)
                for u in range(GS):
                    pe.wait_ge(turn_drained, count(2 * GS * g + GS + u + 1))
                    pe.wait_ge(v_drained, count(GS * g + u + 1))
                    if u >= 2:
                        pe.wait_ge(cx_drained, count(GS * g + u - 1))
                    else:
                        pe.wait_ge(y_summed, count(GS * g))
                    for k in range(2):
                        t = pe.matmul(R[u % 2][:, 0:P], ket[:, u, k * P:(k + 1) * P], v[:, u, k * P:(k + 1) * P],
                                      start=(k == 0), stop=(k == 1))
                    t.then_inc(cx_full, 1)
                for u in range(GS):
                    pe.wait_ge(q_drained, count(GS * g + u + 1))
                    if u >= 2:
                        pe.wait_ge(cx_drained, count(GS * g + u + 1))
                        pe.wait_ge(o_drained, count(GS * g + u - 1))
                    else:
                        pe.wait_ge(cx_drained, count(GS * g + u + 3))
                    pe.matmul(R[u % 2][:, 0:SEQ], cx[:, u], q[:, u], start=True, stop=True).then_inc(o_full, 1)
                for u in range(GS):
                    if u >= 2:
                        pe.wait_ge(o_drained, count(GS * g + u + 1))
                        pe.wait_ge(y_summed, count(GS * g + u - 1))
                    else:
                        pe.wait_ge(o_drained, count(GS * g + u + 3))
                    for k in range(2):
                        t = pe.matmul(R[u % 2][:, k * P:(k + 1) * P], oT[:, u, k * P:(k + 1) * P], wout[:],
                                      start=True, stop=True)
                    t.then_inc(y_full, 1)

        @block.scalar
        def _(act):
            act.wait_ge(loaded, LOADED)
            with act.Fori(0, NSEQ // GS) as g:
                for u in range(GS):
                    act.wait_ge(turn_full, count(2 * GS * g + u + 1))
                    act.activation(xnT[:, u], A[u % 2][:, 0:SEQ], ACT.Identity, bias=beta[:],
                                   scale=gamma[:]).then_inc(turn_drained, 1)
                for u in range(GS):
                    act.wait_ge(k_max, count(GS * g + u + 1))
                    act.activation(ke[:, u], K[u % 2][:, 0:SEQ], ACT.Exp, bias=nmax[:, u:u + 1],
                                   accum_out=ksum[:, u:u + 1]).then_inc(k_exp, 1)
                    act.activation(q[:, u], K[u % 2][:, SEQ:2 * SEQ], ACT.Copy).then_inc(q_drained, 1)
                for u in range(GS):
                    act.wait_ge(turn_full, count(2 * GS * g + GS + u + 1))
                    act.activation(ket[:, u], A[u % 2][:, 0:SEQ], ACT.Copy).then_inc(turn_drained, 1)
                for u in range(GS):
                    act.wait_ge(o_full, count(GS * g + u + 1))
                    act.activation(oT[:, u], R[u % 2][:, 0:SEQ], ACT.Copy).then_inc(o_drained, 1)

        @block.vector
        def _(dve):
            dve.wait_ge(loaded, LOADED)
            with dve.Fori(0, NSEQ // GS) as g:
                dve.wait_ge(turn_full, count(2 * GS * g))
                for u in range(2 * GS):
                    b = 2 * GS * g + u
                    dve.tensor_scalar(xn[:, u], X[:, bass.ds(b, 1), :].rearrange("p o d -> p (o d)"),
                                      mean[:, bass.ds(b, 1)], rstd[:, bass.ds(b, 1)],
                                      ALU.subtract, ALU.mult).then_inc(normed, 1)
                for u in range(GS):
                    dve.wait_ge(kq_full, count(GS * g + u + 1))
                    dve.tensor_reduce(nmax[:, u:u + 1], K[u % 2][:, 0:SEQ], AX.X, ALU.max,
                                      negate=True).then_inc(k_max, 1)
                    dve.wait_ge(v_full, count(GS * g + u + 1))
                    dve.tensor_copy(v[:, u], VB[u % 2][:, 0:SEQ]).then_inc(v_drained, 1)
                for u in range(GS):
                    dve.wait_ge(k_exp, count(GS * g + u + 1))
                    dve.reciprocal(krec[:, u:u + 1], ksum[:, u:u + 1]).then_inc(k_rec, 1)
                    dve.wait_ge(k_rec, count(GS * g + u + 1))
                    dve.tensor_scalar(kscale[:, u:u + 1], krec[:, u:u + 1], float(32) ** -0.5, None,
                                      ALU.mult).then_inc(k_scale, 1)
                for u in range(GS):
                    dve.wait_ge(cx_full, count(GS * g + u + 1))
                    dve.wait_ge(k_scale, count(GS * g + u + 1))
                    dve.scalar_tensor_tensor(out=cx[:, u], in0=R[u % 2][:, 0:P], scalar=kscale[:, u:u + 1],
                                             in1=bd[:], op0=ALU.mult, op1=ALU.mult).then_inc(cx_drained, 1)
                for u in range(GS):
                    dve.wait_ge(y_full, count(GS * g + u + 1))
                    x = X[:, bass.ds(2 * GS * g + 2 * u, 2), :]
                    dve.scalar_tensor_tensor(out=x, in0=x, scalar=2.0,
                                             in1=R[u % 2][:, 0:SEQ].rearrange("p (k d) -> p k d", k=2),
                                             op0=ALU.mult, op1=ALU.add).then_inc(y_summed, 1)
                    dve.wait_ge(y_summed, count(GS * g + u + 1))
                    dve.tensor_tensor(x, x, bout[:, None, :].to_broadcast([P, 2, D]), ALU.add).then_inc(y_added, 1)
                dve.wait_ge(y_added, count(GS * g + GS))


def expert_stage(nc, X, c, w):
    NE = 8
    with ExitStack() as ctx:
        def sb(name, shape, dt=F32):
            return ctx.enter_context(nc.sbuf_tensor(name, shape, dt))

        counters = []

        def sem(name):
            counters.append(ctx.enter_context(nc.semaphore(name)))
            return counters[-1]

        def psum(name):
            return ctx.enter_context(nc.psum_tensor(name, [P, 512], F32))

        w13 = sb("e_w13", [P, NE + 1, 2, P])
        w2 = sb("e_w2", [P, NE + 1, D])
        gw = sb("e_gw", [P, NE])
        bias = sb("e_bias", [P, NE])
        rank = sb("e_rank", [P, NE])
        xs = sb("e_xs", [P, 4, D])
        xT = sb("e_xT", [P, 4, P])
        score = sb("e_score", [P, NBLK, NE])
        key = sb("e_key", [P, NBLK, NE])
        top = sb("e_top", [P, NBLK])
        hit = sb("e_hit", [P, NBLK, NE])
        place = sb("e_place", [P, NBLK, NE])
        first = sb("e_first", [P, NBLK])
        one = sb("e_one", [P, 2, NBLK, NE])
        key2 = sb("e_key2", [P, NBLK, NE])
        both = sb("e_both", [P, NBLK, NE])
        cf = sb("e_cf", [P, NBLK, NE + 1])
        cf2 = sb("e_cf2", [P, NBLK, NE + 1])
        cfs = sb("e_cfs", [P, 2, 4, NE + 1])
        sl = sb("e_sl", [P, 3, P])
        gg = sb("e_gg", [P, 3, P])
        ggT = sb("e_ggT", [P, 2, P])
        hb = [psum(f"e_hb{i}") for i in range(3)]
        tb = [psum(f"e_tb{i}") for i in range(2)]
        ob = [psum(f"e_ob{i}") for i in range(2)]
        xb = psum("e_xb")

        loaded = ctx.enter_context(nc.semaphore("e_loaded"))
        staged = sem("e_staged")
        x_turned = sem("e_x_turned")
        x_ready = sem("e_x_ready")
        logits = sem("e_logits")
        scored = sem("e_scored")
        chain = sem("e_chain")
        routed = sem("e_routed")
        coeffs = sem("e_coeffs")
        h_full = sem("e_h_full")
        silued = sem("e_silued")
        gated = sem("e_gated")
        g_turned = sem("e_g_turned")
        gT_ready = sem("e_gT_ready")
        o_full = sem("e_o_full")
        mixed = sem("e_mixed")
        added = sem("e_added")
        block = ctx.enter_context(nc.Block())
        NI = NBLK // 4
        UN = 4 * (NE + 1)

        @block.sync
        def _(sp):
            for s in counters:
                sp.sem_inc(s, 1)
            sp.dma_start(gw[:], w["gate_w"]).then_inc(loaded, 16)
            sp.dma_start(bias[:], w["expert_bias"].rearrange("(o d) -> o d", o=1).to_broadcast([P, NE]))\
                .then_inc(loaded, 16)
            sp.dma_start(rank[:], c["rank8"]).then_inc(loaded, 16)
            sp.dma_start(w13[:, 0:NE, 0], w["w1"]).then_inc(loaded, 16)
            sp.dma_start(w13[:, 0:NE, 1], w["w3"]).then_inc(loaded, 16)
            sp.dma_start(w2[:, 0:NE], w["w2"]).then_inc(loaded, 16)
            sp.dma_start(w13[:, NE, 0], w["sw1"]).then_inc(loaded, 16)
            sp.dma_start(w13[:, NE, 1], w["sw3"]).then_inc(loaded, 16)
            sp.dma_start(w2[:, NE], w["sw2"]).then_inc(loaded, 16)

        LOADED = 144

        @block.gpsimd
        def _(pool):
            with pool.Fori(0, 2 * NI) as i:
                pool.wait_ge(x_turned, count(i))
                pool.tensor_copy(xs[:], X[:, bass.ds(4 * (i % NI), 4), :]).then_inc(staged, 1)

        @block.tensor
        def _(pe):
            def turn_x(i):
                pe.wait_ge(staged, count(i + 1))
                for k in range(4):
                    t = pe.transpose(xb[:, k * P:(k + 1) * P], xs[:, k], c["ident"][:])
                t.then_inc(x_turned, 1)
                pe.wait_ge(x_ready, count(i + 1))

            pe.wait_ge(loaded, LOADED)
            with pe.Fori(0, NI) as i:
                turn_x(i)
                pe.wait_ge(scored, count(i))
                for k in range(4):
                    t = pe.matmul(hb[0][:, k * NE:(k + 1) * NE], xT[:, k], gw[:], start=True, stop=True)
                t.then_inc(logits, 1)
            pe.wait_ge(scored, count(NI))

            with pe.Fori(0, NI) as i:
                turn_x(NI + i)
                for s in range(UN + 4):
                    if s < UN:
                        u = UN * i + s
                        if s >= 3:
                            pe.wait_ge(gated, count(u - 2))
                        else:
                            pe.wait_ge(gated, count(UN * i))
                        k, e = divmod(s, NE + 1)
                        pe.matmul(hb[s % 3][:, 0:2 * P], xT[:, k], w13[:, e].rearrange("p a h -> p (a h)"),
                                  start=True, stop=True).then_inc(h_full, 1)
                    if 2 <= s < UN + 2:
                        u = UN * i + s - 2
                        pe.wait_ge(gated, count(u + 1))
                        if s >= 4:
                            pe.wait_ge(gT_ready, count(u - 1))
                        pe.transpose(tb[s % 2][:, 0:P], gg[:, (s - 2) % 3], c["ident"][:]).then_inc(g_turned, 1)
                    if s >= 4:
                        r = s - 4
                        u = UN * i + r
                        k, e = divmod(r, NE + 1)
                        pe.wait_ge(gT_ready, count(u + 1))
                        if e == 0:
                            if k >= 2:
                                pe.wait_ge(added, count(4 * i + k - 1))
                            else:
                                pe.wait_ge(added, count(4 * i))
                        pe.matmul(ob[k % 2][:, 0:P], ggT[:, r % 2], w2[:, e], start=(e == 0),
                                  stop=(e == NE)).then_inc(mixed, 1)

        @block.scalar
        def _(act):
            def take_x(i):
                act.wait_ge(x_turned, count(i + 1))
                act.activation(xT[:].rearrange("p k t -> p (k t)"), xb[:], ACT.Copy).then_inc(x_ready, 1)

            act.preload_act_table(ACT.Sigmoid)
            with act.Fori(0, NI) as i:
                act.wait_ge(logits, count(i))
                take_x(i)
                act.wait_ge(logits, count(i + 1))
                act.activation(score[:, bass.ds(4 * i, 4), :], hb[0][:, 0:4 * NE].rearrange("p (k e) -> p k e", k=4),
                               ACT.Sigmoid).then_inc(scored, 1)
            act.preload_act_table(ACT.Silu)
            with act.Fori(0, NI) as i:
                take_x(NI + i)
                act.wait_ge(coeffs, count(2 * i + 2))
                for s in range(UN + 3):
                    if s < UN:
                        u = UN * i + s
                        k, e = divmod(s, NE + 1)
                        act.wait_ge(h_full, count(u + 1))
                        act.activation(sl[:, s % 3], hb[s % 3][:, 0:P], ACT.Silu,
                                       scale=cfs[:, 0, k, e:e + 1]).then_inc(silued, 1)
                    if s >= 3:
                        r = s - 3
                        u = UN * i + r
                        act.wait_ge(g_turned, count(u + 1))
                        if r >= 2:
                            act.wait_ge(mixed, count(u - 1))
                        act.activation(ggT[:, r % 2], tb[r % 2][:, 0:P], ACT.Copy).then_inc(gT_ready, 1)

        @block.vector
        def _(dve):
            dve.wait_ge(loaded, LOADED)
            dve.wait_ge(scored, count(NI))
            done = [0]

            def link(i):
                done[0] += 1
                i.then_inc(chain, 1)
                dve.wait_ge(chain, count(done[0]))

            def per_block(ap):
                return ap[:, :, None].to_broadcast([P, NBLK, NE])

            def every_block(ap):
                return ap[:, None, :].to_broadcast([P, NBLK, NE])

            link(dve.tensor_tensor(key[:], score[:], every_block(bias), ALU.add))
            keys = key
            for n in range(2):
                link(dve.tensor_reduce(top[:], keys[:], AX.X, ALU.max))
                link(dve.tensor_tensor(hit[:], keys[:], per_block(top), ALU.is_equal))
                link(dve.tensor_tensor(place[:], hit[:], every_block(rank), ALU.mult))
                link(dve.tensor_reduce(first[:], place[:], AX.X, ALU.max))
                link(dve.tensor_tensor(one[:, n], place[:], per_block(first), ALU.is_equal))
                if n == 0:
                    link(dve.scalar_tensor_tensor(out=key2[:], in0=one[:, 0], scalar=-3.0e38, in1=key[:],
                                                  op0=ALU.mult, op1=ALU.add))
                    keys = key2
            link(dve.tensor_tensor(both[:], one[:, 0], one[:, 1], ALU.add))
            link(dve.memset(cf[:, :, NE:NE + 1], 1.0))
            link(dve.tensor_tensor(cf[:, :, 0:NE], both[:], score[:], ALU.mult))
            link(dve.tensor_tensor(cf2[:], cf[:], cf[:], ALU.mult))
            with dve.Fori(0, NI) as i:
                dve.wait_ge(gated, count(UN * i))
                dve.tensor_copy(cfs[:, 0], cf[:, bass.ds(4 * i, 4), :]).then_inc(coeffs, 1)
                dve.tensor_copy(cfs[:, 1], cf2[:, bass.ds(4 * i, 4), :]).then_inc(coeffs, 1)
                dve.wait_ge(coeffs, count(2 * i + 2))
                for s in range(UN + 5):
                    if s < UN:
                        u = UN * i + s
                        k, e = divmod(s, NE + 1)
                        dve.wait_ge(silued, count(u + 1))
                        if s >= 3:
                            dve.wait_ge(g_turned, count(u - 2))
                        dve.scalar_tensor_tensor(out=gg[:, s % 3], in0=hb[s % 3][:, P:2 * P],
                                                 scalar=cfs[:, 1, k, e:e + 1], in1=sl[:, s % 3],
                                                 op0=ALU.mult, op1=ALU.mult).then_inc(gated, 1)
                    if s >= 13 and (s - 13) % (NE + 1) == 0:
                        k = (s - 13) // (NE + 1)
                        dve.wait_ge(mixed, count(UN * i + (k + 1) * (NE + 1)))
                        x = X[:, bass.ds(4 * i + k, 1), :].rearrange("p o d -> p (o d)")
                        dve.tensor_tensor(x, x, ob[k % 2][:, 0:P], ALU.add).then_inc(added, 1)
FSLOTS = 15
FSTEPS = (1, 2, 3, 4, 5, 6, 7, 8, 9, 10, 11, 12, 13, 14, 15)
FTURN = 7


def feature_stage(nc, X, c, w):
    with ExitStack() as ctx:
        def sb(name, shape, dt=F32):
            return ctx.enter_context(nc.sbuf_tensor(name, shape, dt))

        counters = []

        def sem(name):
            counters.append(ctx.enter_context(nc.semaphore(name)))
            return counters[-1]

        def psum(name, n=512):
            return ctx.enter_context(nc.psum_tensor(name, [P, n], F32))

        wT = sb("g_wT", [P, 2, PAIRS, D])
        kern = sb("g_kern", [P, 2, PAIRS, HD])
        wf = sb("g_wf", [P, 3 * INNER])
        wo = sb("g_wo", [P, PAIRS, D])
        tri = sb("g_tri", [P, 3 * P])
        xs = sb("g_xs", [P, 2, D])
        xT = sb("g_xT", [P, SEQ])
        raw = sb("g_raw", [P, 2, INNER])
        hi = sb("g_hi", [P, 2, 2, H])
        shifted = sb("g_shifted", [P, 2, H, 2, HD])
        ex = sb("g_ex", [P, 2, H, 2, HD])
        es = sb("g_es", [P, 2, H, 2])
        er = sb("g_er", [P, 2, H, 2])
        V = sb("g_V", [P, 2, 2, H, HD + 1])
        qT = sb("g_qT", [P, 2, H, SEQ])
        kT = sb("g_kT", [P, 2, H, SEQ])
        at = sb("g_at", [P, 2, 3 * P])
        zs = sb("g_zs", [P, 2, 4])
        zr = sb("g_zr", [P, 2, 4])
        on = sb("g_on", [P, 2, H, HD])
        oT = sb("g_oT", [P, PAIRS, SEQ])
        sco = [psum("g_sco0"), psum("g_sco1")]
        tur = psum("g_tur", 1024)
        acc = psum("g_acc")
        wop = psum("g_wop")
        G = psum("g_gen", 1024)

        loaded = ctx.enter_context(nc.semaphore("g_loaded"))
        ones_set = sem("g_ones_set")
        folded = sem("g_folded")
        fold_kept = sem("g_fold_kept")
        staged = sem("g_staged")
        slot_full = sem("g_slot_full")
        slot_drained = sem("g_slot_drained")
        largest = sem("g_largest")
        smallest = sem("g_smallest")
        shift_done = sem("g_shift_done")
        exped = sem("g_exped")
        summed = sem("g_summed")
        recips = sem("g_recips")
        pos_ready = sem("g_pos_ready")
        neg_ready = sem("g_neg_ready")
        scored = sem("g_scored")
        masked = sem("g_masked")
        mixed = sem("g_mixed")
        z_kept = sem("g_z_kept")
        z_recip = sem("g_z_recip")
        head_out = sem("g_head_out")
        o_turned = sem("g_o_turned")
        oT_ready = sem("g_oT_ready")
        projected = sem("g_projected")
        added = sem("g_added")
        block = ctx.enter_context(nc.Block())

        def slot_qkv(k, part):
            return 1 + 3 * k + part

        def slot_turn(k, part, sgn):
            return FTURN + 4 * k + 2 * part + sgn

        @block.sync
        def _(sp):
            for s in counters:
                sp.sem_inc(s, 1)
            sp.dma_start(wT[:, 0], w["WqT"].rearrange("(r p) d -> p r d", p=P)).then_inc(loaded, 16)
            sp.dma_start(wT[:, 1], w["WkT"].rearrange("(r p) d -> p r d", p=P)).then_inc(loaded, 16)
            sp.dma_start(kern[:, 0], w["Kq"].rearrange("(r h) d f -> (h d) r f", h=2)).then_inc(loaded, 16)
            sp.dma_start(kern[:, 1], w["Kk"].rearrange("(r h) d f -> (h d) r f", h=2)).then_inc(loaded, 16)
            sp.dma_start(wf[:, 2 * INNER:3 * INNER], w["Wv"]).then_inc(loaded, 16)
            sp.dma_start(wo[:], w["Wo"].rearrange("(r p) n -> p r n", p=P)).then_inc(loaded, 16)
            sp.dma_start(tri[:], c["causal"]).then_inc(loaded, 16)

        LOADED = 112

        @block.tensor
        def _(pe):
            def project(n, step):
                if step not in FSTEPS:
                    return
                slot = FSTEPS.index(step)
                pe.wait_ge(slot_drained, count(n * FSLOTS + slot))
                if slot == 0:
                    pe.wait_ge(staged, count(n + 1))
                    for k in range(2):
                        t = pe.transpose(G[:, k * P:(k + 1) * P], xs[:, k], c["ident"][:])
                elif slot < FTURN:
                    k, part = divmod(slot - 1, 3)
                    for a in range(2):
                        t = pe.matmul(G[:, a * 512:a * 512 + 512], xT[:, k * P:(k + 1) * P],
                                      wf[:, part * INNER + a * 512:part * INNER + a * 512 + 512],
                                      start=True, stop=True)
                else:
                    k, rest = divmod(slot - FTURN, 4)
                    part, a = divmod(rest, 2)
                    pe.wait_ge(pos_ready, count(n * 4 + 2 * k + part + 1))
                    pe.wait_ge(neg_ready, count(n * 4 + 2 * k + part + 1))
                    for h in range(8):
                        t = pe.transpose(G[:, h * P:(h + 1) * P],
                                         ex[:, part, 8 * a + h].rearrange("p s f -> p (s f)"),
                                         c["ident"][:])
                t.then_inc(slot_full, 1)

            def scores(n, par, h, first):
                N = n * H + h
                if h == 0:
                    pe.wait_ge(slot_drained, count(n * FSLOTS + FSLOTS))
                if not (first and h < 2):
                    pe.wait_ge(masked, count(N - 1))
                s = sco[h % 2]
                pe.matmul(s[:, 0:SEQ], kT[:, par, h, 0:P], qT[:, par, h], start=True, stop=True)
                pe.matmul(s[:, SEQ:SEQ + P], kT[:, par, h, P:SEQ], qT[:, par, h, P:SEQ],
                          start=True, stop=True).then_inc(scored, 1)

            def mix(n, par, h):
                N = n * H + h
                pe.wait_ge(masked, count(N + 1))
                if h % 2 == 0:
                    pe.wait_ge(head_out, count(n * PAIRS + h // 2))
                a, o = at[:, h % 2], (h % 2) * 130
                pe.matmul(acc[:, o:o + 65], a[:, 0:P], V[:, par, 0, h], start=True, stop=True)
                pe.matmul(acc[:, o + 65:o + 130], a[:, P:SEQ], V[:, par, 0, h], start=True, stop=False)
                pe.matmul(acc[:, o + 65:o + 130], a[:, SEQ:SEQ + P], V[:, par, 1, h],
                          start=False, stop=True).then_inc(mixed, 1)

            def turn_out(n):
                pe.wait_ge(head_out, count(n * PAIRS + PAIRS))
                for k in range(2):
                    pe.wait_ge(oT_ready, count(2 * n + k))
                    for r in range(PAIRS):
                        t = pe.transpose(tur[:, r * P:(r + 1) * P],
                                         on[:, k, 2 * r:2 * r + 2].rearrange("p h d -> p (h d)"), c["ident"][:])
                    t.then_inc(o_turned, 1)

            def out_product(n):
                pe.wait_ge(oT_ready, count(2 * n + 2))
                pe.wait_ge(added, count(n))
                for k in range(2):
                    for r in range(PAIRS):
                        t = pe.matmul(wop[:, k * P:(k + 1) * P], oT[:, r, k * P:(k + 1) * P], wo[:, r],
                                      start=(r == 0), stop=(r == PAIRS - 1))
                t.then_inc(projected, 1)

            def heads(n, par, first=False, last=False):
                for h in range(H):
                    scores(n, par, h, first)
                    if not last:
                        project(n + 1, h)
                    if h >= 1:
                        mix(n, par, h - 1)
                    elif not first:
                        mix(n - 1, 1 - par, H - 1)
                    if h == 1 and not first:
                        turn_out(n - 1)
                    if h == 3 and not first:
                        out_product(n - 1)

            pe.wait_ge(loaded, LOADED)
            for part in range(2):
                for h in range(H):
                    j = part * H + h
                    if j >= 2:
                        pe.wait_ge(fold_kept, count(j - 1))
                    lo = 64 * (h % 2)
                    pe.matmul(sco[j % 2][:, 0:HD], wT[lo:lo + 64, part, h // 2], kern[lo:lo + 64, part, h // 2],
                              start=True, stop=True).then_inc(folded, 1)
            pe.wait_ge(fold_kept, count(2 * H))
            for h in range(17):
                project(0, h)
            heads(0, 0, first=True)
            with pe.Fori(0, NSEQ // 2 - 1) as i:
                heads(2 * i + 1, 1)
                heads(2 * i + 2, 0)
            n = NSEQ - 1
            heads(n, 1, last=True)
            mix(n, 1, H - 1)
            turn_out(n)
            out_product(n)

        @block.scalar
        def _(act):
            def exps(n, k, part, first):
                j = n * 4 + 2 * k + part
                act.wait_ge(shift_done, count(2 * j + 2))
                if k == 1:
                    act.wait_ge(slot_full, count(n * FSLOTS + slot_turn(0, part, 1) + 1))
                elif not first:
                    act.wait_ge(slot_full, count(n * FSLOTS - FSLOTS + slot_turn(1, part, 1) + 1))
                act.activation(ex[:, part].rearrange("p h s f -> p (h s f)"),
                               shifted[:, part].rearrange("p h s f -> p (h s f)"), ACT.Exp).then_inc(exped, 1)

            def project(n, par, step, first=False):
                if step in FSTEPS:
                    slot = FSTEPS.index(step)
                    if slot < FTURN:
                        act.wait_ge(slot_full, count(n * FSLOTS + slot + 1))
                        k, part = divmod(slot - 1, 3)
                        if slot == 0:
                            t = act.activation(xT[:], G[:, 0:SEQ], ACT.Copy)
                        elif part == 2:
                            t = act.activation(V[:, par, k, :, 0:HD], G[:].rearrange("p (h d) -> p h d", h=H), ACT.Copy)
                        else:
                            if k == 1:
                                act.wait_ge(shift_done, count(2 * (n * 4 + part) + 2))
                                act.wait_ge(smallest, count(n * 4 + part + 1))
                            elif not first:
                                act.wait_ge(shift_done, count(2 * (n * 4 - 2 + part) + 2))
                            t = act.activation(raw[:, part], G[:], ACT.Copy)
                        t.then_inc(slot_drained, 1)
                if step == 4:
                    exps(n, 0, 0, first)
                if step == 5:
                    exps(n, 0, 1, first)
                if step == 11:
                    exps(n, 1, 0, first)
                if step == 13:
                    exps(n, 1, 1, first)

            def drain_out(n):
                for k in range(2):
                    act.wait_ge(o_turned, count(2 * n + k + 1))
                    act.activation(oT[:, :, k * P:(k + 1) * P], tur[:].rearrange("p (r t) -> p r t", t=P),
                                   ACT.Copy).then_inc(oT_ready, 1)

            def heads(n, par, first=False, last=False):
                for h in range(H):
                    if not last:
                        project(n + 1, 1 - par, h)
                    if h == 1 and not first:
                        drain_out(n - 1)

            act.preload_act_table(ACT.Exp)
            act.wait_ge(ones_set, count(1))
            for h in range(16):
                project(0, 0, h, True)
            heads(0, 0, first=True)
            with act.Fori(0, NSEQ // 2 - 1) as i:
                heads(2 * i + 1, 1)
                heads(2 * i + 2, 0)
            heads(NSEQ - 1, 1, last=True)
            drain_out(NSEQ - 1)

        @block.vector
        def _(dve):
            def heads_of(ap):
                return ap.rearrange("p (h f) -> p h f", f=HD)

            def extremes(n, k, part, first):
                j = n * 4 + 2 * k + part
                dve.wait_ge(slot_drained, count(n * FSLOTS + slot_qkv(k, part) + 1))
                if not (first and k == 0):
                    dve.wait_ge(shift_done, count(2 * (j - 2) + 2))
                dve.tensor_reduce(hi[:, part, 0], heads_of(raw[:, part]), AX.X, ALU.max).then_inc(largest, 1)
                dve.tensor_reduce(hi[:, part, 1], heads_of(raw[:, part]), AX.X, ALU.min).then_inc(smallest, 1)

            def sums(n, k, part, first):
                j = n * 4 + 2 * k + part
                dve.wait_ge(exped, count(j + 1))
                if not (first and k == 0):
                    dve.wait_ge(neg_ready, count(j - 1))
                dve.tensor_reduce(es[:, part], ex[:, part], AX.X,
                                  ALU.add).then_inc(summed, 1)
                dve.wait_ge(summed, count(j + 1))
                dve.reciprocal(er[:, part], es[:, part]).then_inc(recips, 1)
                dve.wait_ge(recips, count(j + 1))
                e = ex[:, part, :, 0]
                dve.tensor_tensor(e, e, er[:, part, :, 0][:, :, None].to_broadcast([P, H, HD]),
                                  ALU.mult).then_inc(pos_ready, 1)

            def drain_turn(n, par, slot):
                k, rest = divmod(slot - FTURN, 4)
                part, a = divmod(rest, 2)
                dve.wait_ge(slot_full, count(n * FSLOTS + slot + 1))
                to = (qT, kT)[part]
                dve.tensor_scalar(to[:, par, 8 * a:8 * a + 8, k * P:(k + 1) * P],
                                  G[:].rearrange("p (h t) -> p h t", t=P), 1e-12, None,
                                  ALU.max).then_inc(slot_drained, 1)

            def project(n, par, step, first=False):
                for k in range(2):
                    if step == (3, 9)[k]:
                        extremes(n, k, 0, first)
                    if step == (4, 10)[k]:
                        extremes(n, k, 1, first)
                    if step == (5, 11)[k]:
                        sums(n, k, 0, first)
                    if step == (6, 13)[k]:
                        sums(n, k, 1, first)
                if step in FSTEPS and FSTEPS.index(step) >= FTURN:
                    drain_turn(n, par, FSTEPS.index(step))

            def mask(n, h, first):
                N = n * H + h
                dve.wait_ge(scored, count(N + 1))
                if not (first and h < 2):
                    dve.wait_ge(mixed, count(N - 1))
                dve.tensor_tensor(at[:, h % 2], sco[h % 2][:, 0:3 * P], tri[:], ALU.mult).then_inc(masked, 1)

            def drain_pair(n, r):
                Q = n * PAIRS + r
                dve.wait_ge(mixed, count(n * H + 2 * r + 2))
                a = acc[:, 0:260].rearrange("p (h k d) -> p h k d", h=2, k=2)
                z, zi = zs[:, r % 2], zr[:, r % 2]
                dve.tensor_scalar(z.rearrange("p (h k) -> p h k", h=2), a[:, :, :, HD], 1e-12, None,
                                  ALU.add).then_inc(z_kept, 1)
                dve.wait_ge(z_kept, count(Q + 1))
                dve.reciprocal(zi, z).then_inc(z_recip, 1)
                dve.wait_ge(z_recip, count(Q + 1))
                if r == 0:
                    dve.wait_ge(o_turned, count(2 * n))
                dve.tensor_tensor(on[:, :, 2 * r:2 * r + 2].rearrange("p k h d -> p h k d"), a[:, :, :, 0:HD],
                                  zi.rearrange("p (h k) -> p h k", h=2)[:, :, :, None].to_broadcast([P, 2, 2, HD]),
                                  ALU.mult).then_inc(head_out, 1)

            def add_attn(n):
                dve.wait_ge(projected, count(n + 1))
                x = X[:, bass.ds(2 * n, 2), :]
                dve.tensor_tensor(x, x, wop[:, 0:SEQ].rearrange("p (k d) -> p k d", k=2), ALU.add).then_inc(added, 1)

            def heads(n, par, first=False, last=False):
                for h in range(H):
                    mask(n, h, first)
                    if h == 0 and not first:
                        drain_pair(n - 1, PAIRS - 1)
                    if h >= 2 and h % 2 == 0:
                        drain_pair(n, h // 2 - 1)
                    if not last:
                        project(n + 1, 1 - par, h)
                    if h == 4 and not first:
                        add_attn(n - 1)

            dve.memset(V[:].rearrange("p a k h d -> p (a k h) d")[:, :, HD:HD + 1], 1.0).then_inc(ones_set, 1)
            dve.wait_ge(loaded, LOADED)
            for j in range(2 * H):
                dve.wait_ge(folded, count(j + 1))
                dve.tensor_copy(wf[:, j * HD:(j + 1) * HD], sco[j % 2][:, 0:HD]).then_inc(fold_kept, 1)
            for h in range(16):
                project(0, 0, h, True)
            heads(0, 0, first=True)
            with dve.Fori(0, NSEQ // 2 - 1) as i:
                heads(2 * i + 1, 1)
                heads(2 * i + 2, 0)
            heads(NSEQ - 1, 1, last=True)
            drain_pair(NSEQ - 1, PAIRS - 1)
            add_attn(NSEQ - 1)

        @block.gpsimd
        def _(pool):
            def heads_of(ap):
                return ap.rearrange("p (h f) -> p h f", f=HD)

            def shift(n, k, part, first):
                j = n * 4 + 2 * k + part
                pool.wait_ge(smallest, count(j + 1))
                if not (first and k == 0):
                    pool.wait_ge(exped, count(j - 1))
                f = heads_of(raw[:, part])
                pool.tensor_tensor(shifted[:, part, :, 0], f,
                                   hi[:, part, 0][:, :, None].to_broadcast([P, H, HD]), ALU.subtract)\
                    .then_inc(shift_done, 1)
                pool.tensor_tensor(shifted[:, part, :, 1],
                                   hi[:, part, 1][:, :, None].to_broadcast([P, H, HD]), f, ALU.subtract)\
                    .then_inc(shift_done, 1)

            def scale(n, k, part):
                j = n * 4 + 2 * k + part
                pool.wait_ge(recips, count(j + 1))
                e = ex[:, part, :, 1]
                pool.tensor_tensor(e, e, er[:, part, :, 1][:, :, None].to_broadcast([P, H, HD]), ALU.mult)\
                    .then_inc(neg_ready, 1)

            def project(n, first=False):
                if not first:
                    pool.wait_ge(slot_full, count(n * FSLOTS - FSLOTS + 1))
                pool.tensor_copy(xs[:], X[:, bass.ds(2 * n, 2), :]).then_inc(staged, 1)
                shift(n, 0, 0, first)
                shift(n, 0, 1, first)
                scale(n, 0, 0)
                scale(n, 0, 1)
                shift(n, 1, 0, first)
                shift(n, 1, 1, first)
                scale(n, 1, 0)
                scale(n, 1, 1)

            project(0, True)
            with pool.Fori(1, NSEQ) as s:
                project(s)
PROJ = 13
TURN = 8
PROJ_ORDER = [(k, part, a) for k, part in ((0, 0), (0, 1), (1, 0), (1, 1), (0, 2), (1, 2)) for a in range(2)]
PROJ_STEPS = range(-6, 7)
TURN_STEPS = (1, 2, 5, 6, 8, 9, 12, 13)
FIRST_STEP = -6


def slot_qkv(k, part):
    return 1 + PROJ_ORDER.index((k, part, 1))


def slot_turn(k, part):
    return 4 * k + 2 * part + 1


def deep_stage(nc, X, c, w):
    with ExitStack() as ctx:
        def sb(name, shape, dt=F32):
            return ctx.enter_context(nc.sbuf_tensor(name, shape, dt))

        counters = []

        def sem(name):
            counters.append(ctx.enter_context(nc.semaphore(name)))
            return counters[-1]

        wqkv = sb("wqkv", [P, 3 * INNER])
        wo = sb("wo", [P, PAIRS, D])
        w1 = sb("w1", [P, 2 * FH])
        w2 = sb("w2", [P, 3, D])
        b1 = sb("b1", [P, 6])
        lng = sb("lng", [P, 1])
        lnb = sb("lnb", [P, 1])
        b2 = sb("b2", [P, D])
        qks = sb("qks", [P, 2, HD])
        rope = sb("rope", [P, 2, 2, 2, HD])
        table = sb("table", [P, 2, 2, 2, HD])
        band32 = sb("band32", [P, 320])
        band = sb("band", [P, 320], BF16)
        identb = sb("identb", [P, P], BF16)
        xs = sb("xs", [P, 2, D])
        xT = sb("xT", [P, SEQ + 1])
        raw = sb("raw", [P, 2, 2, INNER])
        sq = sb("sq", [P, 2, INNER])
        t1 = sb("t1", [P, 2, INNER])
        t2 = sb("t2", [P, 2, INNER])
        rot = sb("rot", [P, 2, INNER])
        ss = sb("ss", [P, 2, 2 * H])
        ssc = sb("ssc", [P, 2, 2 * H])
        rs = sb("rs", [P, 2, 2 * H])
        half = sb("half", [P, 2 * H])
        rq8 = sb("rq8", [P, 2, 2, H])
        V = sb("V", [P, 2, 2, INNER])
        qT = sb("qT", [P, 2, PAIRS, SEQ])
        kT = sb("kT", [P, 2, PAIRS, SEQ])
        mx = sb("mx", [P, 4, 2])
        nb = sb("nb", [P, 4, 2])
        den = sb("den", [P, 4, 2])
        rden = sb("rden", [P, 4, 2])
        pr = sb("pr", [P, 4, 3 * P])
        prT = sb("prT", [P, 2, 288])
        oT = sb("oT", [P, 2, PAIRS, SEQ])
        xs4 = sb("xs4", [P, 4, D])
        xT4 = sb("xT4", [P, 2, SEQ + 1])
        st = sb("st", [P, 4, 6])
        mv = sb("mv", [P, 4, 2])
        zero = sb("zero", [P, D])
        tick = sb("tick", [P, 1])
        ve = sb("ve", [P, 4])
        rstd = sb("rstd", [P, 4])
        xn = sb("xn", [P, 4, D])
        xnT = sb("xnT", [P, 4 * P])
        gl = sb("gl", [P, 2, 4 * P])
        hT = sb("hT", [P, 3, 4 * P])

        def psum(name):
            return ctx.enter_context(nc.psum_tensor(name, [P, 512], F32))

        sco = [psum("sco0"), psum("sco1")]
        tur = [psum("tur0"), psum("tur1")]
        acc = psum("acc")
        wop = psum("wop")
        gen = psum("gen")
        trn = psum("trn")
        gate_ps, up_ps, out_ps = sco, tur, acc
        trn_ps = wop
        back_ps = gen

        const_in = ctx.enter_context(nc.semaphore("const_in"))
        attn_w_in = ctx.enter_context(nc.semaphore("attn_w_in"))
        ffn_w_in = ctx.enter_context(nc.semaphore("ffn_w_in"))
        filled = sem("filled")
        tables = sem("tables")
        staged = sem("staged")
        proj_full = sem("proj_full")
        proj_drained = sem("proj_drained")
        turn_full = sem("turn_full")
        turn_kept = sem("turn_kept")
        squared = sem("squared")
        reduced = sem("reduced")
        clamped = sem("clamped")
        inv_norm = sem("inv_norm")
        cos_part = sem("cos_part")
        sin_part = sem("sin_part")
        summed = sem("summed")
        rotated = sem("rotated")
        q_scaled = sem("q_scaled")
        scored = sem("scored")
        maxed = sem("maxed")
        bias_ready = sem("bias_ready")
        exped = sem("exped")
        recips = sem("recips")
        normed = sem("normed")
        turned = sem("turned")
        turn_drained = sem("turn_drained")
        mixed = sem("mixed")
        head_out = sem("head_out")
        projected = sem("projected")
        attn_added = sem("attn_added")
        f_staged = sem("f_staged")
        f_bias = sem("f_bias")
        f_t1 = sem("f_t1")
        f_shifted = sem("f_shifted")
        f_back = sem("f_back")
        f_stats = sem("f_stats")
        f_mv = sem("f_mv")
        f_cleared = sem("f_cleared")
        f_ve = sem("f_ve")
        f_rstd = sem("f_rstd")
        f_xn = sem("f_xn")
        f_t3 = sem("f_t3")
        f_xnT = sem("f_xnT")
        f_gate = sem("f_gate")
        f_up = sem("f_up")
        f_gelu = sem("f_gelu")
        f_h = sem("f_h")
        f_out = sem("f_out")
        f_added = sem("f_added")

        block = ctx.enter_context(nc.Block())


        @block.sync
        def _(sp):
            for s in counters:
                sp.sem_inc(s, 1)
            sp.dma_start(rope[:], c["rope"]).then_inc(const_in, 16)
            sp.dma_start(band32[:], c["band"]).then_inc(const_in, 16)
            with sp.Fori(0, DEPTH) as l:
                sp.wait_ge(projected, count(l * NSEQ))
                sp.wait_ge(const_in, 32)
                sp.dma_start(wqkv[:], w["Wqkv"][bass.ds(l, 1)].rearrange("o d n -> (o d) n")).then_inc(attn_w_in, 16)
                sp.dma_start(wo[:], w["Wo"][bass.ds(l, 1)].rearrange("o (r p) n -> p (o r) n", p=P)).then_inc(attn_w_in, 16)
                sp.wait_ge(tables, count(l))
                sp.wait_ge(const_in, 32)
                sp.dma_start(qks[:, 0], w["q_scale"][bass.ds(l, 1)].to_broadcast([P, HD])).then_inc(attn_w_in, 16)
                sp.dma_start(qks[:, 1], w["k_scale"][bass.ds(l, 1)].to_broadcast([P, HD])).then_inc(attn_w_in, 16)
                sp.wait_ge(f_added, count(l * 8))
                sp.wait_ge(const_in, 32)
                sp.dma_start(w1[:], w["W1"][bass.ds(l, 1)].rearrange("o d n -> (o d) n")).then_inc(ffn_w_in, 16)
                sp.dma_start(w2[:, 0:2], w["W2"][bass.ds(l, 1), 0:256].rearrange("o (r p) n -> p (o r) n", p=P)).then_inc(ffn_w_in, 16)
                sp.dma_start(w2[0:85, 2], w["W2"][bass.ds(l, 1), 256:FH].rearrange("o p n -> (o p) n")).then_inc(ffn_w_in, 16)
                sp.dma_start(b1[:], w["b1"][bass.ds(l, 1)].rearrange("o p t -> (o p) t")).then_inc(ffn_w_in, 16)
                sp.dma_start(lng[:], w["ln_g"][bass.ds(l, 1)].rearrange("o (p i) -> (o p) i", i=1)).then_inc(ffn_w_in, 16)
                sp.dma_start(lnb[:], w["ln_b"][bass.ds(l, 1)].rearrange("o (p i) -> (o p) i", i=1)).then_inc(ffn_w_in, 16)
                sp.dma_start(b2[:], w["b2"][bass.ds(l, 1)].to_broadcast([P, D])).then_inc(ffn_w_in, 16)

        ATTN_W, FFN_W = 64, 112

        @block.tensor
        def _(pe):
            def project(n, step):
                if step not in PROJ_STEPS:
                    return
                slot = PROJ_STEPS.index(step)
                pe.wait_ge(proj_drained, count(n * PROJ + slot))
                if slot == 0:
                    pe.wait_ge(staged, count(n + 1))
                    for k in range(2):
                        t = pe.transpose(gen[:, k * P:(k + 1) * P], xs[:, k], c["ident"][:])
                else:
                    k, part, a = PROJ_ORDER[slot - 1]
                    at = part * INNER + a * 512
                    t = pe.matmul(gen[:], xT[:, k * P:(k + 1) * P], wqkv[:, at:at + 512], start=True, stop=True)
                t.then_inc(proj_full, 1)

            def turn_qk(n, step):
                if step not in TURN_STEPS:
                    return
                slot = TURN_STEPS.index(step)
                k, rest = divmod(slot, 4)
                part, a = divmod(rest, 2)
                pe.wait_ge(turn_kept, count(n * TURN + slot))
                pe.wait_ge(rotated, count(n * 4 + 2 * k + part + 1))
                for r in range(4):
                    at = (4 * a + r) * P
                    t = pe.transpose(trn[:, r * P:(r + 1) * P], rot[:, part, at:at + P], c["ident"][:])
                t.then_inc(turn_full, 1)

            def scores(n, par, h, first):
                N = n * H + h
                if h == 0:
                    pe.wait_ge(turn_kept, count(n * TURN + TURN))
                    pe.wait_ge(proj_drained, count(n * PROJ + PROJ))
                if not (first and h < 2):
                    pe.wait_ge(exped, count(N - 1))
                r, lo = h // 2, 64 * (h % 2)
                s = sco[h % 2]
                pe.matmul(s[:, 0:320], identb[:], band[:], start=True, stop=True)
                pe.matmul(s[:, 32:160], qT[lo:lo + 64, par, r, 0:P], kT[lo:lo + 64, par, r, 0:P],
                          start=False, stop=True, skip_group_check=True)
                pe.matmul(s[:, 160:320], qT[lo:lo + 64, par, r, P:SEQ], kT[lo:lo + 64, par, r, P - WIN:SEQ],
                          start=False, stop=True, skip_group_check=True).then_inc(scored, 1)

            def turn(n, h, first):
                N = n * H + h
                pe.wait_ge(normed, count(N + 1))
                if not (first and h < 2):
                    pe.wait_ge(turn_drained, count(N - 1))
                p = pr[:, h % 4]
                t = tur[h % 2]
                pe.transpose(t[:, 0:P], p[:, 0:P], c["ident"][:])
                pe.transpose(t[:, P:P + WIN], p[0:WIN, P:2 * P], c["ident"][0:WIN, 0:WIN])
                pe.transpose(t[:, P + WIN:288], p[:, 2 * P:3 * P], c["ident"][:]).then_inc(turned, 1)

            def mix(n, par, h):
                N = n * H + h
                pe.wait_ge(turn_drained, count(N + 1))
                if h % 2 == 0:
                    pe.wait_ge(head_out, count(n * PAIRS + h // 2))
                lo = 64 * (h % 2)
                pe.matmul(acc[lo:lo + 64, 0:160], V[:, par, 0, h * HD:(h + 1) * HD], prT[:, h % 2, 0:160],
                          start=True, stop=True)
                pe.matmul(acc[lo:lo + 64, P:SEQ], V[:, par, 1, h * HD:(h + 1) * HD], prT[:, h % 2, 160:288],
                          start=False, stop=True, skip_group_check=True).then_inc(mixed, 1)

            def out_product(n, par, k):
                if k == 0:
                    pe.wait_ge(head_out, count(n * PAIRS + PAIRS))
                    pe.wait_ge(attn_added, count(n))
                for r in range(PAIRS):
                    t = pe.matmul(wop[:, k * P:(k + 1) * P], oT[:, par, r, k * P:(k + 1) * P], wo[:, r],
                                  start=(r == 0), stop=(r == PAIRS - 1))
                if k == 1:
                    t.then_inc(projected, 1)

            def heads(n, par, first=False, ahead=2):
                for h in range(H):
                    scores(n, par, h, first)
                    if ahead >= 1:
                        project(n + 1, h)
                    if ahead >= 2:
                        project(n + 2, h - H)
                    if h >= 2:
                        turn(n, h - 2, first)
                    elif not first:
                        turn(n - 1, h + H - 2, False)
                    if ahead >= 1:
                        turn_qk(n + 1, h)
                    if h >= 3:
                        mix(n, par, h - 3)
                    elif not first:
                        mix(n - 1, 1 - par, h + H - 3)
                    if h in (7, 9) and not first:
                        out_product(n - 1, 1 - par, (h - 7) // 2)

            def attention(l):
                pe.wait_ge(attn_w_in, (l + 1) * ATTN_W)
                pe.wait_ge(f_added, count(l * 8))
                n = l * NSEQ
                for step in range(FIRST_STEP, H):
                    project(n, step)
                    project(n + 1, step - H)
                    turn_qk(n, step)
                heads(n, 0, first=True)
                with pe.Fori(0, NSEQ // 2 - 2) as i:
                    heads(n + 2 * i + 1, 1)
                    heads(n + 2 * i + 2, 0)
                heads(n + NSEQ - 3, 1)
                heads(n + NSEQ - 2, 0, ahead=1)
                heads(n + NSEQ - 1, 1, ahead=0)
                n = n + NSEQ - 1
                for h in range(H - 2, H):
                    turn(n, h, False)
                    mix(n, 1, h - 1)
                mix(n, 1, H - 1)
                out_product(n, 1, 0)
                out_product(n, 1, 1)

            def f_in(m):
                pe.wait_ge(f_staged, count(m + 1))
                for k in range(4):
                    t = pe.transpose(trn_ps[:, k * P:(k + 1) * P], xs4[:, k], c["ident"][:])
                t.then_inc(f_t1, 1)

            def f_return(m):
                pe.wait_ge(f_shifted, count(m + 1))
                for k in range(4):
                    t = pe.transpose(back_ps[:, k * P:(k + 1) * P],
                                     xT4[:, k // 2, (k % 2) * P:(k % 2) * P + P], c["ident"][:])
                t.then_inc(f_back, 1)

            def f_norm(m):
                pe.wait_ge(f_xn, count(4 * m + 4))
                for k in range(4):
                    t = pe.transpose(trn_ps[:, k * P:(k + 1) * P], xn[:, k], c["ident"][:])
                t.then_inc(f_t3, 1)

            def f_hidden(m, t):
                at, rows = FT[t]
                if t == 0:
                    pe.wait_ge(f_xnT, count(m + 1))
                u = 3 * m + t
                if t >= 2:
                    pe.wait_ge(f_gelu, count(u - 1))
                    pe.wait_ge(f_h, count(u - 1))
                else:
                    pe.wait_ge(f_h, count(3 * m))
                pe.matmul(gate_ps[t % 2][0:rows, :], w1[:, FH + at:FH + at + rows], xnT[:],
                          start=True, stop=True).then_inc(f_gate, 1)
                pe.matmul(up_ps[t % 2][0:rows, :], w1[:, at:at + rows], xnT[:],
                          start=True, stop=True).then_inc(f_up, 1)

            def f_output(m):
                pe.wait_ge(f_h, count(3 * m + 3))
                pe.wait_ge(f_added, count(m))
                for k in range(4):
                    for t, (at, rows) in enumerate(FT):
                        i = pe.matmul(out_ps[:, k * P:(k + 1) * P], hT[0:rows, t, k * P:(k + 1) * P],
                                      w2[0:rows, t], start=(t == 0), stop=(t == 2))
                i.then_inc(f_out, 1)

            def feed(m, front):
                f_hidden(m, 0)
                if front:
                    f_in(m + 1)
                f_hidden(m, 1)
                if front:
                    f_return(m + 1)
                f_hidden(m, 2)
                if front:
                    f_norm(m + 1)
                f_output(m)

            pe.wait_ge(filled, count(9))
            with pe.Fori(0, DEPTH) as l:
                attention(l)
                pe.wait_ge(attn_added, count((l + 1) * NSEQ))
                pe.wait_ge(ffn_w_in, (l + 1) * FFN_W)
                f_in(8 * l)
                f_return(8 * l)
                f_norm(8 * l)
                with pe.Fori(0, 7) as g:
                    feed(8 * l + g, True)
                feed(8 * l + 7, False)

        @block.scalar
        def _(act):
            def project(n, par, step, first=False):
                if step not in PROJ_STEPS:
                    return
                slot = PROJ_STEPS.index(step)
                act.wait_ge(proj_full, count(n * PROJ + slot + 1))
                if slot == 0:
                    act.activation(xT[0:64, 0:SEQ], gen[0:64, 0:SEQ], ACT.Copy)
                    t = act.activation(xT[64:128, 1:SEQ + 1], gen[64:128, 0:SEQ], ACT.Copy)
                else:
                    k, part, a = PROJ_ORDER[slot - 1]
                    cols = slice(a * 512, a * 512 + 512)
                    if part == 2:
                        t = act.activation(V[:, par, k, cols], gen[:], ACT.Copy)
                    else:
                        if a == 0 and not first:
                            act.wait_ge(rotated, count(n * 4 - 4 + 2 * k + part + 1))
                        t = act.activation(raw[:, part, k, cols], gen[:], ACT.Copy)
                t.then_inc(proj_drained, 1)

            def keep_turn(n, par, step):
                if step not in TURN_STEPS:
                    return
                slot = TURN_STEPS.index(step)
                k, rest = divmod(slot, 4)
                part, a = divmod(rest, 2)
                act.wait_ge(turn_full, count(n * TURN + slot + 1))
                act.activation((qT, kT)[part][:, par, 4 * a:4 * a + 4, k * P:(k + 1) * P],
                               trn[:].rearrange("p (r t) -> p r t", t=P), ACT.Copy).then_inc(turn_kept, 1)

            def exps(n, par, h, first):
                N = n * H + h
                act.wait_ge(bias_ready, count(N + 1))
                if not (first and h < 4):
                    act.wait_ge(turned, count(N - 3))
                p, s = pr[:, h % 4], sco[h % 2]
                act.activation(p[:, 0:P], s[:, 32:160], ACT.Exp, bias=nb[:, h % 4, 0:1],
                               scale=rq8[:, par, 0, h:h + 1], accum_out=den[:, h % 4, 0:1])
                act.activation(p[:, 2 * P - WIN:3 * P], s[:, 160:320], ACT.Exp, bias=nb[:, h % 4, 1:2],
                               scale=rq8[:, par, 1, h:h + 1], accum_out=den[:, h % 4, 1:2]).then_inc(exped, 1)

            def drain_turn(n, h, first):
                N = n * H + h
                act.wait_ge(turned, count(N + 1))
                if not (first and h < 2):
                    act.wait_ge(mixed, count(N - 1))
                act.activation(prT[:, h % 2], tur[h % 2][:, 0:288], ACT.Copy).then_inc(turn_drained, 1)

            def heads(n, par, first=False, ahead=2):
                for h in range(H):
                    exps(n, par, h, first)
                    if ahead >= 1:
                        project(n + 1, 1 - par, h)
                    if ahead >= 2:
                        project(n + 2, par, h - H)
                    if h >= 2:
                        drain_turn(n, h - 2, first)
                    elif not first:
                        drain_turn(n - 1, h + H - 2, False)
                    if ahead >= 1:
                        keep_turn(n + 1, 1 - par, h)

            def attention(l):
                act.wait_ge(f_added, count(l * 8))
                n = l * NSEQ
                for step in range(FIRST_STEP, H):
                    project(n, 0, step, True)
                    project(n + 1, 1, step - H)
                    keep_turn(n, 0, step)
                heads(n, 0, first=True)
                with act.Fori(0, NSEQ // 2 - 2) as i:
                    heads(n + 2 * i + 1, 1)
                    heads(n + 2 * i + 2, 0)
                heads(n + NSEQ - 3, 1)
                heads(n + NSEQ - 2, 0, ahead=1)
                heads(n + NSEQ - 1, 1, ahead=0)
                drain_turn(n + NSEQ - 1, H - 2, False)
                drain_turn(n + NSEQ - 1, H - 1, False)

            def f_shift(m):
                act.wait_ge(f_t1, count(m + 1))
                for s in range(2):
                    act.activation(xT4[0:64, s, 0:SEQ], trn_ps[0:64, s * SEQ:(s + 1) * SEQ], ACT.Copy)
                    t = act.activation(xT4[64:128, s, 1:SEQ + 1], trn_ps[64:128, s * SEQ:(s + 1) * SEQ], ACT.Copy)
                t.then_inc(f_shifted, 1)

            def f_affine(m):
                act.wait_ge(f_t3, count(m + 1))
                act.activation(xnT[:], trn_ps[:], ACT.Identity, bias=lnb[:], scale=lng[:]).then_inc(f_xnT, 1)

            def f_gelus(m, t):
                rows = FT[t][1]
                u = 3 * m + t
                act.wait_ge(f_gate, count(u + 1))
                if t == 2:
                    act.wait_ge(f_h, count(u - 1))
                act.activation(gl[0:rows, t % 2], gate_ps[t % 2][0:rows, :], ACT.Gelu,
                               bias=b1[0:rows, 3 + t:4 + t]).then_inc(f_gelu, 1)

            def feed(m, front):
                f_gelus(m, 0)
                if front:
                    f_shift(m + 1)
                f_gelus(m, 1)
                f_gelus(m, 2)
                if front:
                    f_affine(m + 1)

            act.wait_ge(filled, count(7))
            with act.Fori(0, DEPTH) as l:
                act.preload_act_table(ACT.Exp)
                attention(l)
                act.preload_act_table(ACT.Gelu)
                act.wait_ge(attn_added, count((l + 1) * NSEQ))
                act.wait_ge(ffn_w_in, (l + 1) * FFN_W)
                f_shift(8 * l)
                f_affine(8 * l)
                with act.Fori(0, 7) as g:
                    feed(8 * l + g, True)
                feed(8 * l + 7, False)

        @block.vector
        def _(dve):
            def heads_of(ap):
                return ap.rearrange("p (h d) -> p h d", d=HD)

            def reduce_sq(n, k, part):
                j = n * 4 + 2 * k + part
                dve.wait_ge(squared, count(j + 1))
                dve.tensor_reduce(ss[:, k, part * H:(part + 1) * H], heads_of(sq[:, part]), AX.X,
                                  ALU.add).then_inc(reduced, 1)

            def cosine(n, k, part, first):
                j = n * 4 + 2 * k + part
                dve.wait_ge(proj_drained, count(n * PROJ + slot_qkv(k, part) + 1))
                if not (first and k == 0):
                    dve.wait_ge(rotated, count(j - 1))
                dve.tensor_tensor(heads_of(t1[:, part]), heads_of(raw[:, part, k]),
                                  table[:, part, 0, k][:, None, :].to_broadcast([P, H, HD]),
                                  ALU.mult).then_inc(cos_part, 1)

            def add_parts(n, k, part, first):
                j = n * 4 + 2 * k + part
                dve.wait_ge(cos_part, count(j + 1))
                dve.wait_ge(sin_part, count(2 * j + 2))
                if k == 1:
                    dve.wait_ge(turn_full, count(n * TURN + slot_turn(0, part) + 1))
                elif not first:
                    dve.wait_ge(turn_full, count(n * TURN - TURN + slot_turn(1, part) + 1))
                dve.tensor_tensor(rot[:, part], t1[:, part], t2[:, part],
                                  ALU.add).then_inc(rotated if part == 0 else summed, 1)

            def clamp(n, k):
                dve.wait_ge(reduced, count(n * 4 + 2 * k + 2))
                dve.tensor_scalar(ssc[:, k], ss[:, k], 1e-24, None, ALU.max).then_inc(clamped, 1)

            def scale_block(n, par, k):
                dve.wait_ge(inv_norm, count(2 * n + k + 1))
                dve.tensor_scalar(rq8[:, par, k], rs[:, k, 0:H], 8.0, None, ALU.mult).then_inc(q_scaled, 1)
                dve.wait_ge(summed, count(2 * n + k + 1))
                dve.tensor_tensor(heads_of(rot[:, 1]), heads_of(rot[:, 1]),
                                  rs[:, k, H:2 * H][:, :, None].to_broadcast([P, H, HD]),
                                  ALU.mult).then_inc(rotated, 1)

            def project(n, par, step, first=False):
                for k in range(2):
                    if step == (-3, 4)[k]:
                        reduce_sq(n, k, 0)
                    if step == (-2, 5)[k]:
                        cosine(n, k, 0, first)
                    if step == (-1, 7)[k]:
                        add_parts(n, k, 0, first)
                    if step == (0, 6)[k]:
                        reduce_sq(n, k, 1)
                        clamp(n, k)
                    if step == (1, 8)[k]:
                        cosine(n, k, 1, first)
                    if step == (2, 9)[k]:
                        add_parts(n, k, 1, first)
                    if step == (3, 11)[k]:
                        scale_block(n, par, k)

            def maxima(n, par, h, first):
                N = n * H + h
                dve.wait_ge(scored, count(N + 1))
                if h == 0:
                    dve.wait_ge(q_scaled, count(2 * n + 2))
                if not (first and h < 4):
                    dve.wait_ge(exped, count(N - 3))
                dve.tensor_reduce(mx[:, h % 4], sco[h % 2][:, 0:320].rearrange("p (k j) -> p k j", k=2),
                                  AX.X, ALU.max).then_inc(maxed, 1)
                dve.wait_ge(maxed, count(N + 1))
                dve.scalar_tensor_tensor(out=nb[:, h % 4], in0=mx[:, h % 4], scalar=-1.0,
                                         in1=rq8[:, par, :, h], op0=ALU.mult, op1=ALU.mult).then_inc(bias_ready, 1)

            def normalise(n, h):
                N = n * H + h
                dve.wait_ge(exped, count(N + 1))
                dve.reciprocal(rden[:, h % 4], den[:, h % 4]).then_inc(recips, 1)
                dve.wait_ge(recips, count(N + 1))
                p = pr[:, h % 4]
                dve.tensor_scalar(p[:, 0:P], p[:, 0:P], rden[:, h % 4, 0:1], None, ALU.mult)
                dve.tensor_scalar(p[:, 2 * P - WIN:3 * P], p[:, 2 * P - WIN:3 * P], rden[:, h % 4, 1:2], None,
                                  ALU.mult).then_inc(normed, 1)

            def drain_pair(n, par, r):
                dve.wait_ge(mixed, count(n * H + 2 * r + 2))
                dve.tensor_copy(oT[:, par, r], acc[:, 0:SEQ]).then_inc(head_out, 1)

            def add_attn(n, l, s):
                dve.wait_ge(projected, count(n + 1))
                x = X[:, bass.ds(2 * s, 2), :]
                dve.tensor_tensor(x, x, wop[:, 0:SEQ].rearrange("p (k d) -> p k d", k=2),
                                  ALU.add).then_inc(attn_added, 1)

            def heads(l, s, par, first=False, ahead=2):
                n = l * NSEQ + s
                for h in range(H):
                    maxima(n, par, h, first)
                    if ahead >= 1:
                        project(n + 1, 1 - par, h)
                    if ahead >= 2:
                        project(n + 2, par, h - H)
                    if h >= 1:
                        normalise(n, h - 1)
                    elif not first:
                        normalise(n - 1, H - 1)
                    if h >= 4 and h % 2 == 0:
                        drain_pair(n, par, h // 2 - 2)
                    elif not first and h in (0, 2):
                        drain_pair(n - 1, 1 - par, PAIRS - 2 + h // 2)
                    if h == 12 and not first:
                        add_attn(n - 1, l, s - 1)

            def attention(l):
                dve.wait_ge(attn_w_in, (l + 1) * ATTN_W)
                dve.wait_ge(f_added, count(l * 8))
                for part in range(2):
                    for k in range(2):
                        dve.tensor_tensor(table[:, part, 0, k], rope[:, part, 0, k], qks[:, part], ALU.mult)
                        for a in range(2):
                            i = dve.tensor_tensor(table[:, part, 1, k, 32 * a:32 * a + 32],
                                                  rope[:, part, 1, k, 32 * a:32 * a + 32],
                                                  qks[:, part, 32 - 32 * a:64 - 32 * a], ALU.mult)
                i.then_inc(tables, 1)
                dve.wait_ge(tables, count(l + 1))
                n = l * NSEQ
                for step in range(FIRST_STEP, H):
                    project(n, 0, step, True)
                    project(n + 1, 1, step - H)
                heads(l, 0, 0, first=True)
                with dve.Fori(0, NSEQ // 2 - 2) as i:
                    heads(l, 2 * i + 1, 1)
                    heads(l, 2 * i + 2, 0)
                heads(l, NSEQ - 3, 1)
                heads(l, NSEQ - 2, 0, ahead=1)
                heads(l, NSEQ - 1, 1, ahead=0)
                n = n + NSEQ - 1
                normalise(n, H - 1)
                drain_pair(n, 1, PAIRS - 2)
                drain_pair(n, 1, PAIRS - 1)
                add_attn(n, l, NSEQ - 1)

            def f_stat(m):
                dve.wait_ge(f_back, count(m + 1))
                dve.wait_ge(f_xn, count(4 * m))
                for k in range(4):
                    i = dve.bn_stats(st[:, k], back_ps[:, k * P:(k + 1) * P])
                i.then_inc(f_stats, 1)
                dve.wait_ge(f_cleared, count(m))
                dve.wait_ge(f_stats, count(m + 1))
                dve.memset(tick[:], 0.0).then_inc(f_cleared, 1)
                for k in range(4):
                    i = dve.bn_aggr(mv[:, k], st[:, k])
                i.then_inc(f_mv, 1)
                dve.wait_ge(f_mv, count(m + 1))
                dve.tensor_scalar(ve[:], mv[:, :, 1], EPS_LN, None, ALU.add).then_inc(f_ve, 1)

            def f_normal(m):
                dve.wait_ge(f_rstd, count(m + 1))
                for k in range(4):
                    dve.tensor_scalar(xn[:, k], back_ps[:, k * P:(k + 1) * P], mv[:, k, 0:1], rstd[:, k:k + 1],
                                      ALU.subtract, ALU.mult).then_inc(f_xn, 1)

            def f_gated(m, t):
                rows = FT[t][1]
                u = 3 * m + t
                dve.wait_ge(f_up, count(u + 1))
                dve.wait_ge(f_gelu, count(u + 1))
                if t == 0:
                    dve.wait_ge(f_out, count(m))
                dve.scalar_tensor_tensor(out=hT[0:rows, t], in0=up_ps[t % 2][0:rows, :],
                                         scalar=b1[0:rows, t:t + 1], in1=gl[0:rows, t % 2],
                                         op0=ALU.add, op1=ALU.mult).then_inc(f_h, 1)

            def f_add(m, g):
                dve.wait_ge(f_out, count(m + 1))
                dve.wait_ge(f_bias, count(m + 1))
                x = X[:, bass.ds(4 * g, 4), :]
                dve.tensor_tensor(x, x, out_ps[:].rearrange("p (k d) -> p k d", k=4), ALU.add).then_inc(f_added, 1)

            def feed(l, g, front):
                m = 8 * l + g
                f_gated(m, 0)
                f_gated(m, 1)
                if front:
                    f_stat(m + 1)
                f_gated(m, 2)
                if front:
                    f_normal(m + 1)
                f_add(m, g)

            dve.memset(half[:], -0.5).then_inc(filled, 1)
            dve.memset(xT[64:128, 0:1], 0.0).then_inc(filled, 1)
            dve.memset(xT4[64:128, :, 0:1], 0.0).then_inc(filled, 1)
            dve.memset(pr[:, :, P:2 * P], 0.0).then_inc(filled, 1)
            dve.memset(zero[:], 0.0).then_inc(filled, 1)
            dve.memset(den[:], 0.0).then_inc(filled, 1)
            dve.memset(mx[:], 0.0).then_inc(filled, 1)
            dve.wait_ge(filled, count(7))
            dve.wait_ge(const_in, 32)
            dve.tensor_copy(band[:], band32[:]).then_inc(filled, 1)
            dve.tensor_copy(identb[:], c["ident"][:]).then_inc(filled, 1)
            with dve.Fori(0, DEPTH) as l:
                attention(l)
                dve.wait_ge(ffn_w_in, (l + 1) * FFN_W)
                f_stat(8 * l)
                f_normal(8 * l)
                with dve.Fori(0, 7) as g:
                    feed(l, g, True)
                feed(l, 7, False)

        @block.gpsimd
        def _(pool):
            def square(n, k, part, first):
                j = n * 4 + 2 * k + part
                pool.wait_ge(proj_drained, count(n * PROJ + slot_qkv(k, part) + 1))
                if not (first and k == 0):
                    pool.wait_ge(reduced, count(j - 1))
                pool.tensor_tensor(sq[:, part], raw[:, part, k], raw[:, part, k], ALU.mult).then_inc(squared, 1)

            def sine(n, k, part, first):
                j = n * 4 + 2 * k + part
                if not (first and k == 0):
                    pool.wait_ge(rotated, count(j - 1))
                src = raw[:, part, k].rearrange("p (h a d) -> p h a d", h=H, a=2)
                dst = t2[:, part].rearrange("p (h a d) -> p h a d", h=H, a=2)
                for a in range(2):
                    pool.tensor_tensor(dst[:, :, a], src[:, :, 1 - a],
                                       table[:, part, 1, k, 32 * a:32 * a + 32][:, None, :].to_broadcast([P, H, 32]),
                                       ALU.mult).then_inc(sin_part, 1)

            def inverse(n, k):
                pool.wait_ge(clamped, count(2 * n + k + 1))
                pool.tensor_tensor(rs[:, k], ssc[:, k], half[:], ALU.pow).then_inc(inv_norm, 1)

            def stage(l, s):
                if isinstance(s, int):
                    if s > 0:
                        pool.wait_ge(proj_full, count((l * NSEQ + s - 1) * PROJ + 1))
                    pool.tensor_tensor(xs[:], X[:, 2 * s:2 * s + 2], zero[:, None, :].to_broadcast([P, 2, D]),
                                       ALU.add).then_inc(staged, 1)
                else:
                    pool.wait_ge(proj_full, count((l * NSEQ + s - 1) * PROJ + 1))
                    pool.tensor_copy(xs[:], X[:, bass.ds(2 * s, 2), :]).then_inc(staged, 1)

            def project(l, s, first=False, last=False):
                n = l * NSEQ + s
                square(n, 0, 0, first)
                sine(n, 0, 0, first)
                square(n, 0, 1, first)
                sine(n, 0, 1, first)
                inverse(n, 0)
                square(n, 1, 0, first)
                sine(n, 1, 0, first)
                if not last:
                    stage(l, s + 1)
                square(n, 1, 1, first)
                sine(n, 1, 1, first)
                inverse(n, 1)

            def f_stage(l, g):
                m = 8 * l + g
                pool.wait_ge(f_t1, count(m))
                x = X[:, bass.ds(4 * g, 4), :]
                if isinstance(g, int):
                    pool.tensor_tensor(xs4[:], x, zero[:, None, :].to_broadcast([P, 4, D]), ALU.add).then_inc(f_staged, 1)
                else:
                    pool.tensor_copy(xs4[:], x).then_inc(f_staged, 1)
                pool.wait_ge(f_ve, count(m + 1))
                pool.tensor_tensor(rstd[:], ve[:], half[:, 0:4], ALU.pow).then_inc(f_rstd, 1)
                pool.tensor_tensor(x, x, b2[:, None, :].to_broadcast([P, 4, D]), ALU.add).then_inc(f_bias, 1)

            pool.wait_ge(filled, count(7))
            with pool.Fori(0, DEPTH) as l:
                pool.wait_ge(f_added, count(l * 8))
                pool.wait_ge(tables, count(l + 1))
                stage(l, 0)
                project(l, 0, True)
                with pool.Fori(1, NSEQ - 1) as s:
                    project(l, s)
                project(l, NSEQ - 1, last=True)
                pool.wait_ge(attn_added, count((l + 1) * NSEQ))
                pool.wait_ge(ffn_w_in, (l + 1) * FFN_W)
                f_stage(l, 0)
                with pool.Fori(1, 8) as g:
                    f_stage(l, g)

def network(nc, c, w, out):
    with ExitStack() as ctx:
        X = ctx.enter_context(nc.sbuf_tensor("X", [P, NBLK, D], F32))
        X0 = ctx.enter_context(nc.sbuf_tensor("X0", [P, NBLK, D], F32))
        ident = ctx.enter_context(nc.sbuf_tensor("ident", [P, P], F32))
        x_in = ctx.enter_context(nc.semaphore("x_in"))
        x_out = ctx.enter_context(nc.semaphore("x_out"))
        with nc.Block() as block:
            @block.sync
            def _(sp):
                for s in range(NSEQ):
                    sp.dma_start(X[:, 2 * s:2 * s + 2, :],
                                 w["L0_attn_x"][s].rearrange("(k p) d -> p k d", p=P)).then_inc(x_in, 16)
                sp.dma_start(ident[:], c["ident"]).then_inc(x_in, 16)
                sp.wait_ge(x_in, 16 * (NSEQ + 1))
        c = dict(c, ident=ident)

        def part(prefix):
            return {k[len(prefix):]: v for k, v in w.items() if k.startswith(prefix)}

        linear_stage(nc, X, c, part("L0_attn_"))
        norm_stage(nc, X, "_n0")
        expert_stage(nc, X, c, part("L0_ffn_"))
        norm_stage(nc, X, "_n1")
        feature_stage(nc, X, c, part("L1_attn_"))
        norm_stage(nc, X, "_n2", keep=X0)
        deep_stage(nc, X, c, part("L1_ffn_"))
        norm_stage(nc, X, "_n3", residual=X0)
        with nc.Block() as block:
            @block.sync
            def _(sp):
                for s in range(NSEQ):
                    sp.dma_start(out[s].rearrange("(k p) d -> p k d", p=P),
                                 X[:, 2 * s:2 * s + 2, :]).then_inc(x_out, 16)
                sp.wait_ge(x_out, 16 * NSEQ)


def shape_constants():
    f = np.float32
    half = np.arange(0, HD, 2, dtype=f)
    inv_freq = (f(1.0) / f(10000.0) ** (half / f(HD))).astype(f)
    t = np.arange(SEQ, dtype=f)
    freqs = t[:, None] * inv_freq[None, :]
    base = (half + f(0.4 * HD)) / f(1.4 * HD)
    scale = (base[None, :] ** ((t - SEQ // 2) / f(WIN // 2))[:, None]).astype(f)
    cos, sin = np.cos(freqs), np.sin(freqs)
    rope = np.zeros((P, 2, 2, 2, HD), f)
    for part, s in enumerate((scale, f(1.0) / scale)):
        for kind, table in enumerate(([cos * s, cos * s], [-sin * s, sin * s])):
            rope[:, part, kind] = np.concatenate(table, 1).reshape(2, P, HD).transpose(1, 0, 2)
    i = np.arange(P)[:, None]
    band = np.full((P, 320), NEG, f)
    for at, j in ((WIN, np.arange(P)), (P + WIN, np.arange(P + WIN) - WIN)):
        band[:, at:at + len(j)] = np.where((i >= j) & (i <= j + WIN), 0.0, NEG)
    j = np.arange(P)[None, :]
    upper = (i <= j).astype(f)
    return {
        "ident": np.eye(P, dtype=f),
        "rope": rope,
        "band": band,
        "causal": np.concatenate([upper, np.ones((P, P), f), upper], 1),
        "heads32": (i // 32 == j // 32).astype(f),
        "rank8": np.tile(np.arange(8, 0, -1, dtype=f), (P, 1)),
    }


def laid_out(inputs):
    a = {k: np.asarray(v) for k, v in inputs.items()}
    turn = {"L0_ffn_gate_w": (1, 0), "L0_ffn_sw1": (1, 0), "L0_ffn_sw2": (1, 0), "L0_ffn_sw3": (1, 0),
            "L0_ffn_w1": (2, 0, 1), "L0_ffn_w2": (2, 0, 1), "L0_ffn_w3": (2, 0, 1)}
    for k, axes in turn.items():
        a[k] = a[k].transpose(axes)
    a["L1_attn_WqT"] = a.pop("L1_attn_Wq").T
    a["L1_attn_WkT"] = a.pop("L1_attn_Wk").T
    b1 = a["L1_ffn_b1"]
    tiles = np.zeros((DEPTH, P, 6), b1.dtype)
    for side in range(2):
        for t, (at, rows) in enumerate(FT):
            tiles[:, :rows, 3 * side + t] = b1[:, FH * side + at:FH * side + at + rows]
    a["L1_ffn_b1"] = tiles
    return {k: np.ascontiguousarray(v) for k, v in a.items()}


def kernel(**inputs):
    import concourse.bacc as bacc
    from concourse.bass_utils import run_bass_kernel_spmd

    nc = bacc.Bacc("TRN2", target_bir_lowering=False, num_devices=1)
    arrays = {}

    def declare(name, a):
        arrays["in_" + name] = a
        return nc.dram_tensor("in_" + name, a.shape, mybir.dt.from_np(a.dtype), kind="ExternalInput").ap()

    w = {k: declare(k, a) for k, a in laid_out(inputs).items()}
    c = {k: declare("const_" + k, a) for k, a in shape_constants().items()}
    out = nc.dram_tensor("out_0", (NSEQ, SEQ, D), F32, kind="ExternalOutput").ap()
    network(nc, c, w, out)
    r = run_bass_kernel_spmd(nc, [arrays], core_ids=[0])
    return r.results[0]["out_0"]
```

```python
from contextlib import ExitStack

import numpy as np

import concourse.bass as bass
from concourse import mybir

F32 = mybir.dt.float32
F32R = mybir.dt.float32r
BF16 = mybir.dt.bfloat16
ACT = mybir.ActivationFunctionType
ALU = mybir.AluOpType
AX = mybir.AxisListType

P = 128
D = 128
NBLK = 32
NSEQ = 16
SEQ = 256
H = 16
HD = 64
INNER = H * HD
PAIRS = H // 2
DEPTH = 6
WIN = 32
FH = 341
FT = [(0, 128), (128, 128), (256, 85)]
EPS_LN = 1e-5
NEG = -1.0e30


def count(n):
    return n + 1


def norm_stats(nc, ctx, X, tag, residual=None):
    def sb(name, shape):
        return ctx.enter_context(nc.sbuf_tensor(name + tag, shape, F32))

    mean = sb("mean", [P, NBLK])
    rstd = sb("rstd", [P, NBLK])
    with ExitStack() as inner:
        def sem(name):
            return inner.enter_context(nc.semaphore(name + tag))

        st = inner.enter_context(nc.sbuf_tensor("lst" + tag, [P, NBLK, 6], F32))
        mv = inner.enter_context(nc.sbuf_tensor("lmv" + tag, [P, NBLK, 2], F32))
        ve = inner.enter_context(nc.sbuf_tensor("lve" + tag, [P, NBLK], F32))
        half = inner.enter_context(nc.sbuf_tensor("lhalf" + tag, [P, NBLK], F32))
        half_set = sem("half_set")
        with_residual = sem("with_residual")
        stats = sem("stats")
        means = sem("means")
        kept = sem("kept")
        powered = sem("powered")
        block = inner.enter_context(nc.Block())
        parts = [slice(0, NBLK // 2), slice(NBLK // 2, NBLK)]

        @block.vector
        def _(dve):
            dve.memset(half[:], -0.5).then_inc(half_set, 1)
            if residual is not None:
                for part in parts:
                    dve.tensor_tensor(X[:, part], X[:, part], residual[:, part], ALU.add).then_inc(with_residual, 1)
            for a, part in enumerate(parts):
                if residual is not None:
                    dve.wait_ge(with_residual, a + 1)
                for b in range(part.start, part.stop):
                    i = dve.bn_stats(st[:, b], X[:, b])
                i.then_inc(stats, 1)
                dve.wait_ge(stats, a + 1)
                for b in range(part.start, part.stop):
                    i = dve.bn_aggr(mv[:, b], st[:, b])
                i.then_inc(means, 1)
                dve.wait_ge(means, a + 1)
                dve.tensor_scalar(ve[:, part], mv[:, part, 1], EPS_LN, None, ALU.add).then_inc(kept, 1)
                dve.tensor_copy(mean[:, part], mv[:, part, 0])

        @block.gpsimd
        def _(pool):
            pool.wait_ge(half_set, 1)
            for a, part in enumerate(parts):
                pool.wait_ge(kept, a + 1)
                pool.tensor_tensor(rstd[:, part], ve[:, part], half[:, part], ALU.pow).then_inc(powered, 1)
            pool.wait_ge(powered, len(parts))
    return mean, rstd


def norm_stage(nc, X, tag, residual=None, keep=None):
    with ExitStack() as ctx:
        mean, rstd = norm_stats(nc, ctx, X, tag, residual)
        applied = ctx.enter_context(nc.semaphore("applied" + tag))
        block = ctx.enter_context(nc.Block())

        @block.vector
        def _(dve):
            for b in range(NBLK):
                dve.tensor_scalar(X[:, b], X[:, b], mean[:, b:b + 1], rstd[:, b:b + 1],
                                  ALU.subtract, ALU.mult).then_inc(applied, 1)

        if keep is not None:
            @block.scalar
            def _(act):
                for b in range(0, NBLK, 8):
                    act.wait_ge(applied, b + 8)
                    act.activation(keep[:, b:b + 8].rearrange("p b d -> p (b d)"),
                                   X[:, b:b + 8].rearrange("p b d -> p (b d)"), ACT.Copy)


def linear_stage(nc, X, c, w):
    with ExitStack() as ctx:
        def sb(name, shape, dt=F32):
            return ctx.enter_context(nc.sbuf_tensor(name, shape, dt))

        counters = []

        def sem(name):
            counters.append(ctx.enter_context(nc.semaphore(name)))
            return counters[-1]

        def psum(name):
            return ctx.enter_context(nc.psum_tensor(name, [P, 512], F32))

        mean, rstd = norm_stats(nc, ctx, X, "_in")
        GS = 4
        wqkv = sb("a_wqkv", [P, 3 * D])
        wout = sb("a_wout", [P, D])
        gamma = sb("a_gamma", [P, 1])
        beta = sb("a_beta", [P, 1])
        bout = sb("a_bout", [P, D])
        bd = sb("a_bd", [P, P])
        xn = sb("a_xn", [P, 2 * GS, D])
        xnT = sb("a_xnT", [P, GS, SEQ])
        nmax = sb("a_nmax", [P, GS])
        ke = sb("a_ke", [P, GS, SEQ])
        ksum = sb("a_ksum", [P, GS])
        krec = sb("a_krec", [P, GS])
        kscale = sb("a_kscale", [P, GS])
        q = sb("a_q", [P, GS, SEQ])
        v = sb("a_v", [P, GS, SEQ])
        ket = sb("a_ket", [P, GS, SEQ])
        cx = sb("a_cx", [P, GS, P])
        oT = sb("a_oT", [P, GS, SEQ])
        A = [psum("a_A0"), psum("a_A1")]
        K = [psum("a_K0"), psum("a_K1")]
        VB = [psum("a_V0"), psum("a_V1")]
        R = [psum("a_R0"), psum("a_R1")]

        loaded = ctx.enter_context(nc.semaphore("a_loaded"))
        normed = sem("a_normed")
        turn_full = sem("a_turn_full")
        turn_drained = sem("a_turn_drained")
        kq_full = sem("a_kq_full")
        v_full = sem("a_v_full")
        k_max = sem("a_k_max")
        k_exp = sem("a_k_exp")
        q_drained = sem("a_q_drained")
        v_drained = sem("a_v_drained")
        k_rec = sem("a_k_rec")
        k_scale = sem("a_k_scale")
        cx_full = sem("a_cx_full")
        cx_drained = sem("a_cx_drained")
        o_full = sem("a_o_full")
        o_drained = sem("a_o_drained")
        y_full = sem("a_y_full")
        y_summed = sem("a_y_summed")
        y_added = sem("a_y_added")
        block = ctx.enter_context(nc.Block())

        @block.sync
        def _(sp):
            for s in counters:
                sp.sem_inc(s, 1)
            sp.dma_start(wqkv[:], w["w_qkv"]).then_inc(loaded, 16)
            sp.dma_start(wout[:], w["w_out"]).then_inc(loaded, 16)
            sp.dma_start(gamma[:], w["gamma"].rearrange("a b d -> d (a b)")).then_inc(loaded, 16)
            sp.dma_start(beta[:], w["beta"].rearrange("a b d -> d (a b)")).then_inc(loaded, 16)
            sp.dma_start(bout[:], w["b_out"].rearrange("(o d) -> o d", o=1).to_broadcast([P, D])).then_inc(loaded, 16)
            sp.dma_start(bd[:], c["heads32"]).then_inc(loaded, 16)

        LOADED = 96

        @block.tensor
        def _(pe):
            pe.wait_ge(loaded, LOADED)
            with pe.Fori(0, NSEQ // GS) as g:
                for u in range(GS):
                    pe.wait_ge(normed, count(2 * GS * g + 2 * u + 2))
                    if u >= 2:
                        pe.wait_ge(turn_drained, count(2 * GS * g + u - 1))
                    else:
                        pe.wait_ge(turn_drained, count(2 * GS * g))
                    for k in range(2):
                        t = pe.transpose(A[u % 2][:, k * P:(k + 1) * P], xn[:, 2 * u + k], c["ident"][:])
                    t.then_inc(turn_full, 1)
                for u in range(GS):
                    pe.wait_ge(turn_drained, count(2 * GS * g + u + 1))
                    if u >= 2:
                        pe.wait_ge(q_drained, count(GS * g + u - 1))
                        pe.wait_ge(v_drained, count(GS * g + u - 1))
                    else:
                        pe.wait_ge(q_drained, count(GS * g))
                        pe.wait_ge(v_drained, count(GS * g))
                    pe.matmul(K[u % 2][:, 0:SEQ], wqkv[:, D:2 * D], xnT[:, u], start=True, stop=True)
                    pe.matmul(K[u % 2][:, SEQ:2 * SEQ], wqkv[:, 0:D], xnT[:, u], start=True, stop=True)\
                        .then_inc(kq_full, 1)
                    for k in range(2):
                        t = pe.matmul(VB[u % 2][:, k * P:(k + 1) * P], xnT[:, u, k * P:(k + 1) * P],
                                      wqkv[:, 2 * D:3 * D], start=True, stop=True)
                    t.then_inc(v_full, 1)
                for u in range(GS):
                    pe.wait_ge(k_exp, count(GS * g + u + 1))
                    pe.wait_ge(turn_drained, count(2 * GS * g + GS + u - 1))
                    for k in range(2):
                        t = pe.transpose(A[u % 2][:, k * P:(k + 1) * P], ke[:, u, k * P:(k + 1) * P], c["ident"][:])
                    t.then_inc(turn_full, 1)
                for u in range(GS):
                    pe.wait_ge(turn_drained, count(2 * GS * g + GS + u + 1))
                    pe.wait_ge(v_drained, count(GS * g + u + 1))
                    if u >= 2:
                        pe.wait_ge(cx_drained, count(GS * g + u - 1))
                    else:
                        pe.wait_ge(y_summed, count(GS * g))
                    for k in range(2):
                        t = pe.matmul(R[u % 2][:, 0:P], ket[:, u, k * P:(k + 1) * P], v[:, u, k * P:(k + 1) * P],
                                      start=(k == 0), stop=(k == 1))
                    t.then_inc(cx_full, 1)
                for u in range(GS):
                    pe.wait_ge(q_drained, count(GS * g + u + 1))
                    if u >= 2:
                        pe.wait_ge(cx_drained, count(GS * g + u + 1))
                        pe.wait_ge(o_drained, count(GS * g + u - 1))
                    else:
                        pe.wait_ge(cx_drained, count(GS * g + u + 3))
                    pe.matmul(R[u % 2][:, 0:SEQ], cx[:, u], q[:, u], start=True, stop=True).then_inc(o_full, 1)
                for u in range(GS):
                    if u >= 2:
                        pe.wait_ge(o_drained, count(GS * g + u + 1))
                        pe.wait_ge(y_summed, count(GS * g + u - 1))
                    else:
                        pe.wait_ge(o_drained, count(GS * g + u + 3))
                    for k in range(2):
                        t = pe.matmul(R[u % 2][:, k * P:(k + 1) * P], oT[:, u, k * P:(k + 1) * P], wout[:],
                                      start=True, stop=True)
                    t.then_inc(y_full, 1)

        @block.scalar
        def _(act):
            act.wait_ge(loaded, LOADED)
            with act.Fori(0, NSEQ // GS) as g:
                for u in range(GS):
                    act.wait_ge(turn_full, count(2 * GS * g + u + 1))
                    act.activation(xnT[:, u], A[u % 2][:, 0:SEQ], ACT.Identity, bias=beta[:],
                                   scale=gamma[:]).then_inc(turn_drained, 1)
                for u in range(GS):
                    act.wait_ge(k_max, count(GS * g + u + 1))
                    act.activation(ke[:, u], K[u % 2][:, 0:SEQ], ACT.Exp, bias=nmax[:, u:u + 1],
                                   accum_out=ksum[:, u:u + 1]).then_inc(k_exp, 1)
                    act.activation(q[:, u], K[u % 2][:, SEQ:2 * SEQ], ACT.Copy).then_inc(q_drained, 1)
                for u in range(GS):
                    act.wait_ge(turn_full, count(2 * GS * g + GS + u + 1))
                    act.activation(ket[:, u], A[u % 2][:, 0:SEQ], ACT.Copy).then_inc(turn_drained, 1)
                for u in range(GS):
                    act.wait_ge(o_full, count(GS * g + u + 1))
                    act.activation(oT[:, u], R[u % 2][:, 0:SEQ], ACT.Copy).then_inc(o_drained, 1)

        @block.vector
        def _(dve):
            dve.wait_ge(loaded, LOADED)
            with dve.Fori(0, NSEQ // GS) as g:
                dve.wait_ge(turn_full, count(2 * GS * g))
                for u in range(2 * GS):
                    b = 2 * GS * g + u
                    dve.tensor_scalar(xn[:, u], X[:, bass.ds(b, 1), :].rearrange("p o d -> p (o d)"),
                                      mean[:, bass.ds(b, 1)], rstd[:, bass.ds(b, 1)],
                                      ALU.subtract, ALU.mult).then_inc(normed, 1)
                for u in range(GS):
                    dve.wait_ge(kq_full, count(GS * g + u + 1))
                    dve.tensor_reduce(nmax[:, u:u + 1], K[u % 2][:, 0:SEQ], AX.X, ALU.max,
                                      negate=True).then_inc(k_max, 1)
                    dve.wait_ge(v_full, count(GS * g + u + 1))
                    dve.tensor_copy(v[:, u], VB[u % 2][:, 0:SEQ]).then_inc(v_drained, 1)
                for u in range(GS):
                    dve.wait_ge(k_exp, count(GS * g + u + 1))
                    dve.reciprocal(krec[:, u:u + 1], ksum[:, u:u + 1]).then_inc(k_rec, 1)
                    dve.wait_ge(k_rec, count(GS * g + u + 1))
                    dve.tensor_scalar(kscale[:, u:u + 1], krec[:, u:u + 1], float(32) ** -0.5, None,
                                      ALU.mult).then_inc(k_scale, 1)
                for u in range(GS):
                    dve.wait_ge(cx_full, count(GS * g + u + 1))
                    dve.wait_ge(k_scale, count(GS * g + u + 1))
                    dve.scalar_tensor_tensor(out=cx[:, u], in0=R[u % 2][:, 0:P], scalar=kscale[:, u:u + 1],
                                             in1=bd[:], op0=ALU.mult, op1=ALU.mult).then_inc(cx_drained, 1)
                for u in range(GS):
                    dve.wait_ge(y_full, count(GS * g + u + 1))
                    x = X[:, bass.ds(2 * GS * g + 2 * u, 2), :]
                    dve.scalar_tensor_tensor(out=x, in0=x, scalar=2.0,
                                             in1=R[u % 2][:, 0:SEQ].rearrange("p (k d) -> p k d", k=2),
                                             op0=ALU.mult, op1=ALU.add).then_inc(y_summed, 1)
                    dve.wait_ge(y_summed, count(GS * g + u + 1))
                    dve.tensor_tensor(x, x, bout[:, None, :].to_broadcast([P, 2, D]), ALU.add).then_inc(y_added, 1)
                dve.wait_ge(y_added, count(GS * g + GS))


def expert_stage(nc, X, c, w):
    NE = 8
    with ExitStack() as ctx:
        def sb(name, shape, dt=F32):
            return ctx.enter_context(nc.sbuf_tensor(name, shape, dt))

        counters = []

        def sem(name):
            counters.append(ctx.enter_context(nc.semaphore(name)))
            return counters[-1]

        def psum(name):
            return ctx.enter_context(nc.psum_tensor(name, [P, 512], F32))

        w13 = sb("e_w13", [P, NE + 1, 2, P])
        w2 = sb("e_w2", [P, NE + 1, D])
        gw = sb("e_gw", [P, NE])
        bias = sb("e_bias", [P, NE])
        rank = sb("e_rank", [P, NE])
        xs = sb("e_xs", [P, 4, D])
        xT = sb("e_xT", [P, 4, P])
        score = sb("e_score", [P, NBLK, NE])
        key = sb("e_key", [P, NBLK, NE])
        top = sb("e_top", [P, NBLK])
        hit = sb("e_hit", [P, NBLK, NE])
        place = sb("e_place", [P, NBLK, NE])
        first = sb("e_first", [P, NBLK])
        one = sb("e_one", [P, 2, NBLK, NE])
        key2 = sb("e_key2", [P, NBLK, NE])
        both = sb("e_both", [P, NBLK, NE])
        cf = sb("e_cf", [P, NBLK, NE + 1])
        cf2 = sb("e_cf2", [P, NBLK, NE + 1])
        cfs = sb("e_cfs", [P, 2, 4, NE + 1])
        sl = sb("e_sl", [P, 3, P])
        gg = sb("e_gg", [P, 3, P])
        ggT = sb("e_ggT", [P, 2, P])
        hb = [psum(f"e_hb{i}") for i in range(3)]
        tb = [psum(f"e_tb{i}") for i in range(2)]
        ob = [psum(f"e_ob{i}") for i in range(2)]
        xb = psum("e_xb")

        loaded = ctx.enter_context(nc.semaphore("e_loaded"))
        staged = sem("e_staged")
        x_turned = sem("e_x_turned")
        x_ready = sem("e_x_ready")
        logits = sem("e_logits")
        scored = sem("e_scored")
        chain = sem("e_chain")
        routed = sem("e_routed")
        coeffs = sem("e_coeffs")
        h_full = sem("e_h_full")
        silued = sem("e_silued")
        gated = sem("e_gated")
        g_turned = sem("e_g_turned")
        gT_ready = sem("e_gT_ready")
        o_full = sem("e_o_full")
        mixed = sem("e_mixed")
        added = sem("e_added")
        block = ctx.enter_context(nc.Block())
        NI = NBLK // 4
        UN = 4 * (NE + 1)

        @block.sync
        def _(sp):
            for s in counters:
                sp.sem_inc(s, 1)
            sp.dma_start(gw[:], w["gate_w"]).then_inc(loaded, 16)
            sp.dma_start(bias[:], w["expert_bias"].rearrange("(o d) -> o d", o=1).to_broadcast([P, NE]))\
                .then_inc(loaded, 16)
            sp.dma_start(rank[:], c["rank8"]).then_inc(loaded, 16)
            sp.dma_start(w13[:, 0:NE, 0], w["w1"]).then_inc(loaded, 16)
            sp.dma_start(w13[:, 0:NE, 1], w["w3"]).then_inc(loaded, 16)
            sp.dma_start(w2[:, 0:NE], w["w2"]).then_inc(loaded, 16)
            sp.dma_start(w13[:, NE, 0], w["sw1"]).then_inc(loaded, 16)
            sp.dma_start(w13[:, NE, 1], w["sw3"]).then_inc(loaded, 16)
            sp.dma_start(w2[:, NE], w["sw2"]).then_inc(loaded, 16)

        LOADED = 144

        @block.gpsimd
        def _(pool):
            with pool.Fori(0, 2 * NI) as i:
                pool.wait_ge(x_turned, count(i))
                pool.tensor_copy(xs[:], X[:, bass.ds(4 * (i % NI), 4), :]).then_inc(staged, 1)

        @block.tensor
        def _(pe):
            def turn_x(i):
                pe.wait_ge(staged, count(i + 1))
                for k in range(4):
                    t = pe.transpose(xb[:, k * P:(k + 1) * P], xs[:, k], c["ident"][:])
                t.then_inc(x_turned, 1)
                pe.wait_ge(x_ready, count(i + 1))

            pe.wait_ge(loaded, LOADED)
            with pe.Fori(0, NI) as i:
                turn_x(i)
                pe.wait_ge(scored, count(i))
                for k in range(4):
                    t = pe.matmul(hb[0][:, k * NE:(k + 1) * NE], xT[:, k], gw[:], start=True, stop=True)
                t.then_inc(logits, 1)
            pe.wait_ge(scored, count(NI))

            with pe.Fori(0, NI) as i:
                turn_x(NI + i)
                for s in range(UN + 4):
                    if s < UN:
                        u = UN * i + s
                        if s >= 3:
                            pe.wait_ge(gated, count(u - 2))
                        else:
                            pe.wait_ge(gated, count(UN * i))
                        k, e = divmod(s, NE + 1)
                        pe.matmul(hb[s % 3][:, 0:2 * P], xT[:, k], w13[:, e].rearrange("p a h -> p (a h)"),
                                  start=True, stop=True).then_inc(h_full, 1)
                    if 2 <= s < UN + 2:
                        u = UN * i + s - 2
                        pe.wait_ge(gated, count(u + 1))
                        if s >= 4:
                            pe.wait_ge(gT_ready, count(u - 1))
                        pe.transpose(tb[s % 2][:, 0:P], gg[:, (s - 2) % 3], c["ident"][:]).then_inc(g_turned, 1)
                    if s >= 4:
                        r = s - 4
                        u = UN * i + r
                        k, e = divmod(r, NE + 1)
                        pe.wait_ge(gT_ready, count(u + 1))
                        if e == 0:
                            if k >= 2:
                                pe.wait_ge(added, count(4 * i + k - 1))
                            else:
                                pe.wait_ge(added, count(4 * i))
                        pe.matmul(ob[k % 2][:, 0:P], ggT[:, r % 2], w2[:, e], start=(e == 0),
                                  stop=(e == NE)).then_inc(mixed, 1)

        @block.scalar
        def _(act):
            def take_x(i):
                act.wait_ge(x_turned, count(i + 1))
                act.activation(xT[:].rearrange("p k t -> p (k t)"), xb[:], ACT.Copy).then_inc(x_ready, 1)

            act.preload_act_table(ACT.Sigmoid)
            with act.Fori(0, NI) as i:
                act.wait_ge(logits, count(i))
                take_x(i)
                act.wait_ge(logits, count(i + 1))
                act.activation(score[:, bass.ds(4 * i, 4), :], hb[0][:, 0:4 * NE].rearrange("p (k e) -> p k e", k=4),
                               ACT.Sigmoid).then_inc(scored, 1)
            act.preload_act_table(ACT.Silu)
            with act.Fori(0, NI) as i:
                take_x(NI + i)
                act.wait_ge(coeffs, count(2 * i + 2))
                for s in range(UN + 3):
                    if s < UN:
                        u = UN * i + s
                        k, e = divmod(s, NE + 1)
                        act.wait_ge(h_full, count(u + 1))
                        act.activation(sl[:, s % 3], hb[s % 3][:, 0:P], ACT.Silu,
                                       scale=cfs[:, 0, k, e:e + 1]).then_inc(silued, 1)
                    if s >= 3:
                        r = s - 3
                        u = UN * i + r
                        act.wait_ge(g_turned, count(u + 1))
                        if r >= 2:
                            act.wait_ge(mixed, count(u - 1))
                        act.activation(ggT[:, r % 2], tb[r % 2][:, 0:P], ACT.Copy).then_inc(gT_ready, 1)

        @block.vector
        def _(dve):
            dve.wait_ge(loaded, LOADED)
            dve.wait_ge(scored, count(NI))
            done = [0]

            def link(i):
                done[0] += 1
                i.then_inc(chain, 1)
                dve.wait_ge(chain, count(done[0]))

            def per_block(ap):
                return ap[:, :, None].to_broadcast([P, NBLK, NE])

            def every_block(ap):
                return ap[:, None, :].to_broadcast([P, NBLK, NE])

            link(dve.tensor_tensor(key[:], score[:], every_block(bias), ALU.add))
            keys = key
            for n in range(2):
                link(dve.tensor_reduce(top[:], keys[:], AX.X, ALU.max))
                link(dve.tensor_tensor(hit[:], keys[:], per_block(top), ALU.is_equal))
                link(dve.tensor_tensor(place[:], hit[:], every_block(rank), ALU.mult))
                link(dve.tensor_reduce(first[:], place[:], AX.X, ALU.max))
                link(dve.tensor_tensor(one[:, n], place[:], per_block(first), ALU.is_equal))
                if n == 0:
                    link(dve.scalar_tensor_tensor(out=key2[:], in0=one[:, 0], scalar=-3.0e38, in1=key[:],
                                                  op0=ALU.mult, op1=ALU.add))
                    keys = key2
            link(dve.tensor_tensor(both[:], one[:, 0], one[:, 1], ALU.add))
            link(dve.memset(cf[:, :, NE:NE + 1], 1.0))
            link(dve.tensor_tensor(cf[:, :, 0:NE], both[:], score[:], ALU.mult))
            link(dve.tensor_tensor(cf2[:], cf[:], cf[:], ALU.mult))
            with dve.Fori(0, NI) as i:
                dve.wait_ge(gated, count(UN * i))
                dve.tensor_copy(cfs[:, 0], cf[:, bass.ds(4 * i, 4), :]).then_inc(coeffs, 1)
                dve.tensor_copy(cfs[:, 1], cf2[:, bass.ds(4 * i, 4), :]).then_inc(coeffs, 1)
                dve.wait_ge(coeffs, count(2 * i + 2))
                for s in range(UN + 5):
                    if s < UN:
                        u = UN * i + s
                        k, e = divmod(s, NE + 1)
                        dve.wait_ge(silued, count(u + 1))
                        if s >= 3:
                            dve.wait_ge(g_turned, count(u - 2))
                        dve.scalar_tensor_tensor(out=gg[:, s % 3], in0=hb[s % 3][:, P:2 * P],
                                                 scalar=cfs[:, 1, k, e:e + 1], in1=sl[:, s % 3],
                                                 op0=ALU.mult, op1=ALU.mult).then_inc(gated, 1)
                    if s >= 13 and (s - 13) % (NE + 1) == 0:
                        k = (s - 13) // (NE + 1)
                        dve.wait_ge(mixed, count(UN * i + (k + 1) * (NE + 1)))
                        x = X[:, bass.ds(4 * i + k, 1), :].rearrange("p o d -> p (o d)")
                        dve.tensor_tensor(x, x, ob[k % 2][:, 0:P], ALU.add).then_inc(added, 1)
F_PROJ_ORDER = [(k, part, a) for k, part in ((0, 0), (0, 1), (1, 0), (1, 1), (0, 2), (1, 2)) for a in range(2)]
F_PROJ = 1 + len(F_PROJ_ORDER)
F_PROJ_STEPS = (-11, -10, -9, -8, -7, -6, -5, -4, -3, 1, 2, 3, 4)
F_TURN = 16
F_TURN_STEPS = (0, 1, 2, 3, 4, 5, 6, 7, 8, 9, 10, 11, 12, 13, 14, 15)
F_MAX_STEPS = (-8, -5, 0, 4)
F_MIN_STEPS = (-7, -3, 1, 5)
F_EXP_STEPS = (-5, 0, 4, 8)
F_SUM_STEPS = (-3, 2, 6, 10)
F_OUT_TURN_STEPS = (6, 10, 15, 18)
F_OUT_STEPS = (3, 4)
F_ADD_STEP = 5
F_FIRST = -11
F_MIX_LAG = 1
F_DRAIN_LAG = 3


def f_slot_qkv(k, part):
    return 1 + F_PROJ_ORDER.index((k, part, 1))


def feature_stage(nc, X, c, w):
    with ExitStack() as ctx:
        def sb(name, shape, dt=F32):
            return ctx.enter_context(nc.sbuf_tensor(name, shape, dt))

        counters = []

        def sem(name):
            counters.append(ctx.enter_context(nc.semaphore(name)))
            return counters[-1]

        def psum(name, n=512):
            return ctx.enter_context(nc.psum_tensor(name, [P, n], F32))

        wT = sb("g_wT", [P, 2, PAIRS, D])
        kern = sb("g_kern", [P, 2, PAIRS, HD])
        wf = sb("g_wf", [P, 3 * INNER])
        wo = sb("g_wo", [P, PAIRS, D])
        tri = sb("g_tri", [P, 3 * P])
        xs = sb("g_xs", [P, 2, D])
        xT = sb("g_xT", [P, SEQ])
        raw = sb("g_raw", [P, 2, 2, INNER])
        hi = sb("g_hi", [P, 2, 2, H])
        ex = sb("g_ex", [P, 2, H, 2, HD])
        shifted = sb("g_shifted", [P, 2, H, 2, HD])
        es = sb("g_es", [P, 2, H, 2])
        er = sb("g_er", [P, 2, H, 2])
        V = sb("g_V", [P, 2, 2, H, HD + 1])
        qT = sb("g_qT", [P, 2, H, SEQ])
        kT = sb("g_kT", [P, 2, H, SEQ])
        at = sb("g_at", [P, 2, 3 * P])
        zs = sb("g_zs", [P, 2, 4])
        zr = sb("g_zr", [P, 2, 4])
        on = sb("g_on", [P, 2, H, HD])
        oT = sb("g_oT", [P, PAIRS, SEQ])
        sco = [psum("g_sco0"), psum("g_sco1")]
        tur = psum("g_tur")
        wop = tur
        acc = [psum("g_acc0"), psum("g_acc1")]
        gen = psum("g_gen")
        trn = [psum("g_trn0"), psum("g_trn1")]

        loaded = ctx.enter_context(nc.semaphore("g_loaded"))
        ones_set = sem("g_ones_set")
        folded = sem("g_folded")
        fold_kept = sem("g_fold_kept")
        staged = sem("g_staged")
        proj_full = sem("g_proj_full")
        proj_drained = sem("g_proj_drained")
        turn_full = sem("g_turn_full")
        turn_kept = sem("g_turn_kept")
        largest = sem("g_largest")
        smallest = sem("g_smallest")
        shift_done = sem("g_shift_done")
        exped = sem("g_exped")
        summed = sem("g_summed")
        recips = sem("g_recips")
        featured = sem("g_featured")
        scored = sem("g_scored")
        masked = sem("g_masked")
        mixed = sem("g_mixed")
        z_kept = sem("g_z_kept")
        z_recip = sem("g_z_recip")
        head_out = sem("g_head_out")
        o_turned = sem("g_o_turned")
        oT_ready = sem("g_oT_ready")
        projected = sem("g_projected")
        added = sem("g_added")
        block = ctx.enter_context(nc.Block())

        @block.sync
        def _(sp):
            for s in counters:
                sp.sem_inc(s, 1)
            sp.dma_start(wT[:, 0], w["WqT"].rearrange("(r p) d -> p r d", p=P)).then_inc(loaded, 16)
            sp.dma_start(wT[:, 1], w["WkT"].rearrange("(r p) d -> p r d", p=P)).then_inc(loaded, 16)
            sp.dma_start(kern[:, 0], w["Kq"].rearrange("(r h) d f -> (h d) r f", h=2)).then_inc(loaded, 16)
            sp.dma_start(kern[:, 1], w["Kk"].rearrange("(r h) d f -> (h d) r f", h=2)).then_inc(loaded, 16)
            sp.dma_start(wf[:, 2 * INNER:3 * INNER], w["Wv"]).then_inc(loaded, 16)
            sp.dma_start(wo[:], w["Wo"].rearrange("(r p) n -> p r n", p=P)).then_inc(loaded, 16)
            sp.dma_start(tri[:], c["causal"]).then_inc(loaded, 16)

        LOADED = 112

        @block.tensor
        def _(pe):
            def project(n, step):
                for slot in [i for i, at_step in enumerate(F_PROJ_STEPS) if at_step == step]:
                    pe.wait_ge(proj_drained, count(n * F_PROJ + slot))
                    if slot == 0:
                        pe.wait_ge(staged, count(n + 1))
                        for k in range(2):
                            t = pe.transpose(gen[:, k * P:(k + 1) * P], xs[:, k], c["ident"][:])
                    else:
                        k, part, a = F_PROJ_ORDER[slot - 1]
                        col = part * INNER + a * 512
                        t = pe.matmul(gen[:], xT[:, k * P:(k + 1) * P], wf[:, col:col + 512],
                                      start=True, stop=True)
                    t.then_inc(proj_full, 1)

            def turn_features(n, step, first=False):
                for slot in [i for i, at_step in enumerate(F_TURN_STEPS) if at_step == step]:
                    unit, a = divmod(slot, 4)
                    if not (first and slot < 2):
                        pe.wait_ge(turn_kept, count(n * F_TURN + slot - 1))
                    pe.wait_ge(featured, count(n * 4 + unit + 1))
                    for i in range(4):
                        t = pe.transpose(trn[slot % 2][:, i * P:(i + 1) * P],
                                         ex[:, unit % 2, 4 * a + i].rearrange("p s f -> p (s f)"), c["ident"][:])
                    t.then_inc(turn_full, 1)

            def scores(n, par, h, first):
                N = n * H + h
                if h == 0:
                    pe.wait_ge(turn_kept, count(n * F_TURN + F_TURN))
                    pe.wait_ge(proj_drained, count(n * F_PROJ + F_PROJ))
                if not (first and h < 2):
                    pe.wait_ge(masked, count(N - 1))
                s = sco[h % 2]
                pe.matmul(s[:, 0:SEQ], kT[:, par, h, 0:P], qT[:, par, h], start=True, stop=True)
                pe.matmul(s[:, SEQ:SEQ + P], kT[:, par, h, P:SEQ], qT[:, par, h, P:SEQ],
                          start=True, stop=True).then_inc(scored, 1)

            def mix(n, par, h, first=False):
                N = n * H + h
                pe.wait_ge(masked, count(N + 1))
                if h % 2 == 0 and not (first and h < 4):
                    pe.wait_ge(head_out, count(n * PAIRS + h // 2 - 1))
                a, o = at[:, h % 2], (h % 2) * 130
                bank = acc[h // 2 % 2]
                pe.matmul(bank[:, o:o + 65], a[:, 0:P], V[:, par, 0, h], start=True, stop=True)
                pe.matmul(bank[:, o + 65:o + 130], a[:, P:SEQ], V[:, par, 0, h], start=True, stop=False)
                pe.matmul(bank[:, o + 65:o + 130], a[:, SEQ:SEQ + P], V[:, par, 1, h],
                          start=False, stop=True).then_inc(mixed, 1)

            def turn_out(n, q):
                pe.wait_ge(head_out, count(n * PAIRS + 2 * q + 2))
                pe.wait_ge(oT_ready, count(4 * n + q))
                if q == 0:
                    pe.wait_ge(added, count(n))
                for i in range(4):
                    r, k = 2 * q + i // 2, i % 2
                    t = pe.transpose(tur[:, i * P:(i + 1) * P],
                                     on[:, k, 2 * r:2 * r + 2].rearrange("p h d -> p (h d)"), c["ident"][:])
                t.then_inc(o_turned, 1)

            def out_product(n, k):
                if k == 0:
                    pe.wait_ge(oT_ready, count(4 * n + 4))
                for r in range(PAIRS):
                    t = pe.matmul(wop[:, k * P:(k + 1) * P], oT[:, r, k * P:(k + 1) * P], wo[:, r],
                                  start=(r == 0), stop=(r == PAIRS - 1))
                if k == 1:
                    t.then_inc(projected, 1)

            def heads(n, par, first=False, ahead=2):
                for h in range(H):
                    scores(n, par, h, first)
                    if ahead >= 1:
                        project(n + 1, h)
                    if ahead >= 2:
                        project(n + 2, h - H)
                    if ahead >= 1:
                        turn_features(n + 1, h)
                    if ahead >= 2:
                        turn_features(n + 2, h - H)
                    if h >= F_MIX_LAG:
                        mix(n, par, h - F_MIX_LAG, first)
                    elif not first:
                        mix(n - 1, 1 - par, h + H - F_MIX_LAG)
                    if h in F_OUT_TURN_STEPS:
                        turn_out(n, F_OUT_TURN_STEPS.index(h))
                    if h + H in F_OUT_TURN_STEPS and not first:
                        turn_out(n - 1, F_OUT_TURN_STEPS.index(h + H))
                    if h in F_OUT_STEPS and not first:
                        out_product(n - 1, F_OUT_STEPS.index(h))

            pe.wait_ge(loaded, LOADED)
            for j in range(4):
                part, a = divmod(j, 2)
                if j >= 2:
                    pe.wait_ge(fold_kept, count(j - 1))
                for r in range(PAIRS):
                    t = pe.matmul(sco[a][:, r * HD:(r + 1) * HD], wT[64 * a:64 * a + 64, part, r],
                                  kern[64 * a:64 * a + 64, part, r], start=True, stop=True)
                t.then_inc(folded, 1)
            pe.wait_ge(fold_kept, count(4))
            for step in range(F_FIRST, H):
                project(0, step)
                project(1, step - H)
                turn_features(0, step, True)
            heads(0, 0, first=True)
            with pe.Fori(0, NSEQ // 2 - 2) as i:
                heads(2 * i + 1, 1)
                heads(2 * i + 2, 0)
            heads(NSEQ - 3, 1)
            heads(NSEQ - 2, 0, ahead=1)
            heads(NSEQ - 1, 1, ahead=0)
            n = NSEQ - 1
            for h in range(H - F_MIX_LAG, H):
                mix(n, 1, h)
            for q, step in enumerate(F_OUT_TURN_STEPS):
                if step >= H:
                    turn_out(n, q)
            out_product(n, 0)
            out_product(n, 1)

        @block.scalar
        def _(act):
            def exps(n, unit, first):
                j = n * 4 + unit
                act.wait_ge(shift_done, count(2 * j + 2))
                if not (first and unit < 2):
                    act.wait_ge(turn_full, count(4 * (j - 1)))
                act.activation(ex[:, unit % 2].rearrange("p h s f -> p (h s f)"),
                               shifted[:, unit % 2].rearrange("p h s f -> p (h s f)"), ACT.Exp).then_inc(exped, 1)

            def project(n, par, step, first=False):
                for slot in [i for i, at_step in enumerate(F_PROJ_STEPS) if at_step == step]:
                    act.wait_ge(proj_full, count(n * F_PROJ + slot + 1))
                    if slot == 0:
                        t = act.activation(xT[:], gen[:, 0:SEQ], ACT.Copy)
                    else:
                        k, part, a = F_PROJ_ORDER[slot - 1]
                        if part == 2:
                            t = act.activation(V[:, par, k, 8 * a:8 * a + 8, 0:HD],
                                               gen[:].rearrange("p (h d) -> p h d", d=HD), ACT.Copy)
                        else:
                            if a == 0 and not first:
                                act.wait_ge(shift_done, count(2 * (n * 4 - 4 + 2 * k + part) + 2))
                            t = act.activation(raw[:, k, part, a * 512:a * 512 + 512], gen[:], ACT.Copy)
                    t.then_inc(proj_drained, 1)

            def exponentials(n, step, first=False):
                if step in F_EXP_STEPS:
                    exps(n, F_EXP_STEPS.index(step), first)

            def drain_out(n, q):
                act.wait_ge(o_turned, count(4 * n + q + 1))
                if q == 0:
                    act.wait_ge(projected, count(n))
                act.activation(oT[:, 2 * q:2 * q + 2], tur[:].rearrange("p (r t) -> p r t", t=SEQ),
                               ACT.Copy).then_inc(oT_ready, 1)

            def heads(n, par, first=False, ahead=2):
                for h in range(H):
                    if ahead >= 1:
                        project(n + 1, 1 - par, h)
                    if ahead >= 2:
                        project(n + 2, par, h - H)
                    if ahead >= 1:
                        exponentials(n + 1, h)
                    if ahead >= 2:
                        exponentials(n + 2, h - H)
                    if h in F_OUT_TURN_STEPS:
                        drain_out(n, F_OUT_TURN_STEPS.index(h))
                    if h + H in F_OUT_TURN_STEPS and not first:
                        drain_out(n - 1, F_OUT_TURN_STEPS.index(h + H))

            act.preload_act_table(ACT.Exp)
            act.wait_ge(ones_set, count(1))
            for step in range(F_FIRST, H):
                project(0, 0, step, True)
                project(1, 1, step - H)
                exponentials(0, step, True)
                exponentials(1, step - H)
            heads(0, 0, first=True)
            with act.Fori(0, NSEQ // 2 - 2) as i:
                heads(2 * i + 1, 1)
                heads(2 * i + 2, 0)
            heads(NSEQ - 3, 1)
            heads(NSEQ - 2, 0, ahead=1)
            heads(NSEQ - 1, 1, ahead=0)
            for q, step in enumerate(F_OUT_TURN_STEPS):
                if step >= H:
                    drain_out(NSEQ - 1, q)

        @block.vector
        def _(dve):
            def maxima(n, unit, first):
                j = n * 4 + unit
                k, part = divmod(unit, 2)
                dve.wait_ge(proj_drained, count(n * F_PROJ + f_slot_qkv(k, part) + 1))
                if not (first and k == 0):
                    dve.wait_ge(shift_done, count(2 * (j - 2) + 2))
                f = raw[:, k, part].rearrange("p (h f) -> p h f", f=HD)
                dve.tensor_reduce(hi[:, part, 0], f, AX.X, ALU.max).then_inc(largest, 1)

            def minima(n, unit, first):
                j = n * 4 + unit
                k, part = divmod(unit, 2)
                if not (first and k == 0):
                    dve.wait_ge(shift_done, count(2 * (j - 2) + 2))
                f = raw[:, k, part].rearrange("p (h f) -> p h f", f=HD)
                dve.tensor_reduce(hi[:, part, 1], f, AX.X, ALU.min).then_inc(smallest, 1)

            def sums(n, unit, first):
                j = n * 4 + unit
                part = unit % 2
                dve.wait_ge(exped, count(j + 1))
                if not (first and unit < 2):
                    dve.wait_ge(featured, count(j - 1))
                dve.tensor_reduce(es[:, part], ex[:, part], AX.X, ALU.add).then_inc(summed, 1)
                dve.wait_ge(summed, count(j + 1))
                dve.reciprocal(er[:, part], es[:, part]).then_inc(recips, 1)

            def keep_features(n, par, step):
                for slot in [i for i, at_step in enumerate(F_TURN_STEPS) if at_step == step]:
                    unit, a = divmod(slot, 4)
                    k, part = divmod(unit, 2)
                    dve.wait_ge(turn_full, count(n * F_TURN + slot + 1))
                    dve.tensor_scalar((qT, kT)[part][:, par, 4 * a:4 * a + 4, k * P:(k + 1) * P],
                                      trn[slot % 2][:].rearrange("p (h t) -> p h t", t=P), 1e-12, None,
                                      ALU.max).then_inc(turn_kept, 1)

            def softmaxes(n, step, first=False):
                if step in F_MAX_STEPS:
                    maxima(n, F_MAX_STEPS.index(step), first)
                if step in F_MIN_STEPS:
                    minima(n, F_MIN_STEPS.index(step), first)
                if step in F_SUM_STEPS:
                    sums(n, F_SUM_STEPS.index(step), first)

            def mask(n, h, first):
                N = n * H + h
                dve.wait_ge(scored, count(N + 1))
                if not (first and h < 2):
                    dve.wait_ge(mixed, count(N - 1))
                dve.tensor_tensor(at[:, h % 2], sco[h % 2][:, 0:3 * P], tri[:], ALU.mult).then_inc(masked, 1)

            def drain_pair(n, r, first=False):
                Q = n * PAIRS + r
                dve.wait_ge(mixed, count(n * H + 2 * r + 2))
                a = acc[r % 2][:, 0:260].rearrange("p (h k d) -> p h k d", h=2, k=2)
                z, zi = zs[:, r % 2], zr[:, r % 2]
                dve.tensor_scalar(z.rearrange("p (h k) -> p h k", h=2), a[:, :, :, HD], 1e-12, None,
                                  ALU.add).then_inc(z_kept, 1)
                dve.wait_ge(z_kept, count(Q + 1))
                dve.reciprocal(zi, z).then_inc(z_recip, 1)
                dve.wait_ge(z_recip, count(Q + 1))
                if r % 2 == 0 and not first:
                    dve.wait_ge(o_turned, count(4 * n - 4 + r // 2 + 1))
                dve.tensor_tensor(on[:, :, 2 * r:2 * r + 2].rearrange("p k h d -> p h k d"), a[:, :, :, 0:HD],
                                  zi.rearrange("p (h k) -> p h k", h=2)[:, :, :, None].to_broadcast([P, 2, 2, HD]),
                                  ALU.mult).then_inc(head_out, 1)

            def add_attn(n):
                dve.wait_ge(projected, count(n + 1))
                x = X[:, bass.ds(2 * n, 2), :]
                dve.tensor_tensor(x, x, wop[:, 0:SEQ].rearrange("p (k d) -> p k d", k=2), ALU.add).then_inc(added, 1)

            def heads(n, par, first=False, ahead=2):
                for h in range(H):
                    if (h - F_DRAIN_LAG) % 2 == 0:
                        if h >= F_DRAIN_LAG:
                            drain_pair(n, (h - F_DRAIN_LAG) // 2, first)
                        elif not first:
                            drain_pair(n - 1, PAIRS + (h - F_DRAIN_LAG) // 2)
                    if ahead >= 1:
                        softmaxes(n + 1, h)
                    if ahead >= 2:
                        softmaxes(n + 2, h - H)
                    mask(n, h, first)
                    if ahead >= 1:
                        keep_features(n + 1, 1 - par, h)
                    if ahead >= 2:
                        keep_features(n + 2, par, h - H)
                    if h == F_ADD_STEP and not first:
                        add_attn(n - 1)

            dve.memset(V[:].rearrange("p a k h d -> p (a k h) d")[:, :, HD:HD + 1], 1.0).then_inc(ones_set, 1)
            dve.wait_ge(loaded, LOADED)
            for j in range(4):
                dve.wait_ge(folded, count(j + 1))
                part, a = divmod(j, 2)
                to = wf[:, part * INNER:(part + 1) * INNER].rearrange("p (r a f) -> p r a f", a=2, f=HD)
                dve.tensor_copy(to[:, :, a], sco[a][:].rearrange("p (r f) -> p r f", f=HD)).then_inc(fold_kept, 1)
            for step in range(F_FIRST, H):
                softmaxes(0, step, True)
                softmaxes(1, step - H)
                keep_features(0, 0, step)
            heads(0, 0, first=True)
            with dve.Fori(0, NSEQ // 2 - 2) as i:
                heads(2 * i + 1, 1)
                heads(2 * i + 2, 0)
            heads(NSEQ - 3, 1)
            heads(NSEQ - 2, 0, ahead=1)
            heads(NSEQ - 1, 1, ahead=0)
            for r in range(PAIRS - F_DRAIN_LAG // 2, PAIRS):
                drain_pair(NSEQ - 1, r)
            add_attn(NSEQ - 1)

        @block.gpsimd
        def _(pool):
            def heads_of(ap):
                return ap.rearrange("p (h f) -> p h f", f=HD)

            def shift(n, unit, first=False):
                j = n * 4 + unit
                k, part = divmod(unit, 2)
                pool.wait_ge(smallest, count(j + 1))
                if not (first and k == 0):
                    pool.wait_ge(exped, count(j - 1))
                f = heads_of(raw[:, k, part])
                pool.tensor_tensor(shifted[:, part, :, 0], f,
                                   hi[:, part, 0][:, :, None].to_broadcast([P, H, HD]), ALU.subtract)\
                    .then_inc(shift_done, 1)
                pool.tensor_tensor(shifted[:, part, :, 1],
                                   hi[:, part, 1][:, :, None].to_broadcast([P, H, HD]), f, ALU.subtract)\
                    .then_inc(shift_done, 1)

            def scale(n, unit):
                j = n * 4 + unit
                part = unit % 2
                pool.wait_ge(recips, count(j + 1))
                e = ex[:, part]
                pool.tensor_tensor(e, e, er[:, part][:, :, :, None].to_broadcast([P, H, 2, HD]), ALU.mult)\
                    .then_inc(featured, 1)

            def stage(n):
                pool.tensor_copy(xs[:], X[:, bass.ds(2 * n, 2), :]).then_inc(staged, 1)

            def project(n, first=False, last=False):
                shift(n, 0, first)
                if not first:
                    scale(n - 1, 3)
                shift(n, 1, first)
                scale(n, 0)
                if not last:
                    pool.wait_ge(proj_full, count(n * F_PROJ + 1))
                    stage(n + 1)
                shift(n, 2, first)
                scale(n, 1)
                shift(n, 3, first)
                scale(n, 2)

            stage(0)
            project(0, first=True)
            with pool.Fori(1, NSEQ - 1) as n:
                project(n)
            project(NSEQ - 1, last=True)
            scale(NSEQ - 1, 3)
PROJ = 13
TURN = 8
PROJ_ORDER = [(k, part, a) for k, part in ((0, 0), (0, 1), (1, 0), (1, 1), (0, 2), (1, 2)) for a in range(2)]
PROJ_STEPS = range(-6, 7)
TURN_STEPS = (1, 2, 5, 7, 8, 10, 12, 14)
FIRST_STEP = -6
TURN_LAG = 2
MIX_LAG = 3
DRAIN_LAG = 4
OUT_STEPS = (8, 9)
SPLIT_STEPS = (6, 8, 10)
ADD_STEP = 10


def slot_qkv(k, part):
    return 1 + PROJ_ORDER.index((k, part, 1))


def slot_turn(k, part):
    return 4 * k + 2 * part + 1


def beside_feed(g, t):
    step = FIRST_STEP + 3 * (g - 1) + t
    return () if g == 0 else (step,) if step < H - 2 else (step, step + 1)


def deep_stage(nc, X, c, w):
    with ExitStack() as ctx:
        def sb(name, shape, dt=F32):
            return ctx.enter_context(nc.sbuf_tensor(name, shape, dt))

        counters = []

        def sem(name):
            counters.append(ctx.enter_context(nc.semaphore(name)))
            return counters[-1]

        wqkv_hi = sb("wqkv_hi", [P, 3 * INNER], F32R)
        wqkv_lo = sb("wqkv_lo", [P, 3 * INNER], F32R)
        w1_hi = sb("w1_hi", [P, 2 * FH], F32R)
        w1_lo = sb("w1_lo", [P, 2 * FH], F32R)
        wo = sb("wo", [P, PAIRS, D])
        w1 = sb("w1", [P, 2 * FH])
        w2 = sb("w2", [P, 3, D])
        b1 = sb("b1", [P, 6])
        lng = sb("lng", [P, 1])
        lnb = sb("lnb", [P, 1])
        b2 = sb("b2", [P, D])
        qks = sb("qks", [P, 2, HD])
        rope = sb("rope", [P, 2, 2, 2, HD])
        table = sb("table", [P, 2, 2, 2, HD])
        band = sb("band", [P, 320], BF16)
        identb = sb("identb", [P, P], BF16)
        xs = sb("xs", [P, 2, D])
        xT_hi = sb("xT_hi", [P, SEQ + 1], F32R)
        xT_lo = sb("xT_lo", [P, SEQ + 1], F32R)
        raw = sb("raw", [P, 2, 2, INNER])
        sq = sb("sq", [P, 2, INNER])
        work = sb("work", [P, 4 * INNER])
        t1 = work[:, 0:2 * INNER].rearrange("p (a n) -> p a n", a=2)
        t2 = work[:, 2 * INNER:4 * INNER].rearrange("p (a n) -> p a n", a=2)
        wqkv = work[:, 0:3 * INNER]
        rot = sb("rot", [P, 2, INNER])
        ss = sb("ss", [P, 2, 2 * H])
        ssc = sb("ssc", [P, 2, 2 * H])
        rs = sb("rs", [P, 2, 2 * H])
        half = sb("half", [P, 2 * H])
        rq8 = sb("rq8", [P, 2, 2, H])
        V = sb("V", [P, 2, 2, INNER])
        qT = sb("qT", [P, 2, PAIRS, SEQ])
        kT = sb("kT", [P, 2, PAIRS, SEQ])
        mx = sb("mx", [P, 4, 2])
        nb = sb("nb", [P, 4, 2])
        den = sb("den", [P, 4, 2])
        rden = sb("rden", [P, 4, 2])
        pr = sb("pr", [P, 4, 3 * P])
        prT = sb("prT", [P, 2, 288])
        oT = sb("oT", [P, 2, PAIRS, SEQ])
        room = oT[:].rearrange("p a r t -> p (a r t)")

        def within(start, *shape):
            size = int(np.prod(shape))
            ap = room[:, start:start + size]
            return ap if len(shape) == 1 else ap.rearrange("p (a n) -> p a n", a=shape[0])

        band32 = within(0, 320)
        xs4 = within(0, 4, D)
        xn = within(512, 4, D)
        xnT = within(1024, 4 * P)
        gl = within(1536, 2, 4 * P)
        hT = within(2560, 3, 4 * P)
        xnT_hi = sb("xnT_hi", [P, 4 * P], F32R)
        xnT_lo = sb("xnT_lo", [P, 4 * P], F32R)
        xT4 = sb("xT4", [P, 2, SEQ + 1])
        st = sb("st", [P, 4, 6])
        mv = sb("mv", [P, 4, 2])
        zero = sb("zero", [P, D])
        tick = sb("tick", [P, 1])
        ve = sb("ve", [P, 4])
        rstd = sb("rstd", [P, 4])

        def psum(name):
            return ctx.enter_context(nc.psum_tensor(name, [P, 512], F32))

        sco = [psum("sco0"), psum("sco1")]
        tur = [psum("tur0"), psum("tur1")]
        acc = psum("acc")
        wop = psum("wop")
        gen = psum("gen")
        trn = psum("trn")
        gate_ps, up_ps, out_ps = sco, tur, acc
        trn_ps = back_ps = wop

        const_in = ctx.enter_context(nc.semaphore("const_in"))
        wqkv_in = ctx.enter_context(nc.semaphore("wqkv_in"))
        attn_w_in = ctx.enter_context(nc.semaphore("attn_w_in"))
        ffn_w_in = ctx.enter_context(nc.semaphore("ffn_w_in"))
        filled = sem("filled")
        wqkv_high = sem("wqkv_high")
        wqkv_low = sem("wqkv_low")
        w1_high = sem("w1_high")
        w1_low = sem("w1_low")
        x_high = sem("x_high")
        f_low = sem("f_low")
        tables = sem("tables")
        staged = sem("staged")
        proj_full = sem("proj_full")
        proj_drained = sem("proj_drained")
        turn_full = sem("turn_full")
        turn_kept = sem("turn_kept")
        squared = sem("squared")
        reduced = sem("reduced")
        clamped = sem("clamped")
        inv_norm = sem("inv_norm")
        cos_part = sem("cos_part")
        sin_part = sem("sin_part")
        summed = sem("summed")
        rotated = sem("rotated")
        q_scaled = sem("q_scaled")
        scored = sem("scored")
        maxed = sem("maxed")
        bias_ready = sem("bias_ready")
        exped = sem("exped")
        recips = sem("recips")
        normed = sem("normed")
        turned = sem("turned")
        turn_drained = sem("turn_drained")
        mixed = sem("mixed")
        head_out = sem("head_out")
        projected = sem("projected")
        attn_added = sem("attn_added")
        f_staged = sem("f_staged")
        f_bias = sem("f_bias")
        f_t1 = sem("f_t1")
        f_shifted = sem("f_shifted")
        f_back = sem("f_back")
        f_stats = sem("f_stats")
        f_mv = sem("f_mv")
        f_cleared = sem("f_cleared")
        f_ve = sem("f_ve")
        f_rstd = sem("f_rstd")
        f_xn = sem("f_xn")
        f_t3 = sem("f_t3")
        f_xnT = sem("f_xnT")
        f_gate = sem("f_gate")
        f_up = sem("f_up")
        f_gelu = sem("f_gelu")
        f_h = sem("f_h")
        f_out = sem("f_out")
        f_added = sem("f_added")

        block = ctx.enter_context(nc.Block())


        @block.sync
        def _(sp):
            for s in counters:
                sp.sem_inc(s, 1)
            sp.dma_start(rope[:], c["rope"]).then_inc(const_in, 16)
            sp.dma_start(band32, c["band"]).then_inc(const_in, 16)

            def load_attn(l):
                sp.wait_ge(rotated, count(l * NSEQ * 4))
                sp.wait_ge(const_in, 32)
                sp.dma_start(wqkv, w["Wqkv"][bass.ds(l, 1)].rearrange("o d n -> (o d) n")).then_inc(wqkv_in, 16)
                sp.wait_ge(tables, count(l))
                sp.wait_ge(const_in, 32)
                sp.dma_start(qks[:, 0], w["q_scale"][bass.ds(l, 1)].to_broadcast([P, HD])).then_inc(attn_w_in, 16)
                sp.dma_start(qks[:, 1], w["k_scale"][bass.ds(l, 1)].to_broadcast([P, HD])).then_inc(attn_w_in, 16)
                sp.wait_ge(projected, count(l * NSEQ))
                sp.wait_ge(const_in, 32)
                sp.dma_start(wo[:], w["Wo"][bass.ds(l, 1)].rearrange("o (r p) n -> p (o r) n", p=P)).then_inc(attn_w_in, 16)

            def load_ffn(l):
                sp.wait_ge(f_added, count(l * 8))
                sp.wait_ge(const_in, 32)
                sp.dma_start(w1[:], w["W1"][bass.ds(l, 1)].rearrange("o d n -> (o d) n")).then_inc(ffn_w_in, 16)
                sp.dma_start(w2[:, 0:2], w["W2"][bass.ds(l, 1), 0:256].rearrange("o (r p) n -> p (o r) n", p=P)).then_inc(ffn_w_in, 16)
                sp.dma_start(w2[0:85, 2], w["W2"][bass.ds(l, 1), 256:FH].rearrange("o p n -> (o p) n")).then_inc(ffn_w_in, 16)
                sp.dma_start(b1[:], w["b1"][bass.ds(l, 1)].rearrange("o p t -> (o p) t")).then_inc(ffn_w_in, 16)
                sp.dma_start(lng[:], w["ln_g"][bass.ds(l, 1)].rearrange("o (p i) -> (o p) i", i=1)).then_inc(ffn_w_in, 16)
                sp.dma_start(lnb[:], w["ln_b"][bass.ds(l, 1)].rearrange("o (p i) -> (o p) i", i=1)).then_inc(ffn_w_in, 16)
                sp.dma_start(b2[:], w["b2"][bass.ds(l, 1)].to_broadcast([P, D])).then_inc(ffn_w_in, 16)

            load_attn(0)
            load_ffn(0)
            if DEPTH > 1:
                with sp.Fori(1, DEPTH) as l:
                    load_attn(l)
                    load_ffn(l)

        WQKV, ATTN_W, FFN_W = 16, 48, 112

        @block.tensor
        def _(pe):
            def split_product(to, a_hi, a_lo, b_hi, b_lo):
                pe.matmul(to, a_hi, b_lo, start=True, stop=False)
                pe.matmul(to, a_lo, b_hi, start=False, stop=False)
                return pe.matmul(to, a_hi, b_hi, start=False, stop=True)

            def project(n, step):
                if step not in PROJ_STEPS:
                    return
                slot = PROJ_STEPS.index(step)
                pe.wait_ge(proj_drained, count(n * PROJ + slot))
                if slot == 0:
                    pe.wait_ge(staged, count(n + 1))
                    for k in range(2):
                        t = pe.transpose(gen[:, k * P:(k + 1) * P], xs[:, k], c["ident"][:])
                else:
                    k, part, a = PROJ_ORDER[slot - 1]
                    at = part * INNER + a * 512
                    t = split_product(gen[:], xT_hi[:, k * P:(k + 1) * P], xT_lo[:, k * P:(k + 1) * P],
                                      wqkv_hi[:, at:at + 512], wqkv_lo[:, at:at + 512])
                t.then_inc(proj_full, 1)

            def turn_qk(n, step):
                if step not in TURN_STEPS:
                    return
                slot = TURN_STEPS.index(step)
                k, rest = divmod(slot, 4)
                part, a = divmod(rest, 2)
                pe.wait_ge(turn_kept, count(n * TURN + slot))
                pe.wait_ge(rotated, count(n * 4 + 2 * k + part + 1))
                for r in range(4):
                    at = (4 * a + r) * P
                    t = pe.transpose(trn[:, r * P:(r + 1) * P], rot[:, part, at:at + P], c["ident"][:])
                t.then_inc(turn_full, 1)

            def scores(n, par, h, first):
                N = n * H + h
                if h == 0:
                    pe.wait_ge(turn_kept, count(n * TURN + TURN))
                    pe.wait_ge(proj_drained, count(n * PROJ + PROJ))
                if not (first and h < 2):
                    pe.wait_ge(exped, count(N - 1))
                r, lo = h // 2, 64 * (h % 2)
                s = sco[h % 2]
                pe.matmul(s[:, 0:320], identb[:], band[:], start=True, stop=True)
                pe.matmul(s[:, 32:160], qT[lo:lo + 64, par, r, 0:P], kT[lo:lo + 64, par, r, 0:P],
                          start=False, stop=True, skip_group_check=True)
                pe.matmul(s[:, 160:320], qT[lo:lo + 64, par, r, P:SEQ], kT[lo:lo + 64, par, r, P - WIN:SEQ],
                          start=False, stop=True, skip_group_check=True).then_inc(scored, 1)

            def turn(n, h, first):
                N = n * H + h
                pe.wait_ge(normed, count(N + 1))
                if not (first and h < 2):
                    pe.wait_ge(turn_drained, count(N - 1))
                p = pr[:, h % 4]
                t = tur[h % 2]
                pe.transpose(t[:, 0:P], p[:, 0:P], c["ident"][:])
                pe.transpose(t[:, P:P + WIN], p[0:WIN, P:2 * P], c["ident"][0:WIN, 0:WIN])
                pe.transpose(t[:, P + WIN:288], p[:, 2 * P:3 * P], c["ident"][:]).then_inc(turned, 1)

            def mix(n, par, h):
                N = n * H + h
                pe.wait_ge(turn_drained, count(N + 1))
                if h % 2 == 0:
                    pe.wait_ge(head_out, count(n * PAIRS + h // 2))
                lo = 64 * (h % 2)
                pe.matmul(acc[lo:lo + 64, 0:160], V[:, par, 0, h * HD:(h + 1) * HD], prT[:, h % 2, 0:160],
                          start=True, stop=True)
                pe.matmul(acc[lo:lo + 64, P:SEQ], V[:, par, 1, h * HD:(h + 1) * HD], prT[:, h % 2, 160:288],
                          start=False, stop=True, skip_group_check=True).then_inc(mixed, 1)

            def out_product(n, par, k):
                if k == 0:
                    pe.wait_ge(head_out, count(n * PAIRS + PAIRS))
                    pe.wait_ge(attn_added, count(n))
                for r in range(PAIRS):
                    t = pe.matmul(wop[:, k * P:(k + 1) * P], oT[:, par, r, k * P:(k + 1) * P], wo[:, r],
                                  start=(r == 0), stop=(r == PAIRS - 1))
                if k == 1:
                    t.then_inc(projected, 1)

            def heads(n, par, first=False, ahead=2):
                for h in range(H):
                    scores(n, par, h, first)
                    if ahead >= 1:
                        project(n + 1, h)
                    if ahead >= 2:
                        project(n + 2, h - H)
                    if h in OUT_STEPS and not first:
                        out_product(n - 1, 1 - par, OUT_STEPS.index(h))
                    if h >= TURN_LAG:
                        turn(n, h - TURN_LAG, first)
                    elif not first:
                        turn(n - 1, h + H - TURN_LAG, False)
                    if ahead >= 1:
                        turn_qk(n + 1, h)
                    if h >= MIX_LAG:
                        mix(n, par, h - MIX_LAG)
                    elif not first:
                        mix(n - 1, 1 - par, h + H - MIX_LAG)

            def prepare(l, step):
                n = l * NSEQ
                if step == FIRST_STEP:
                    pe.wait_ge(attn_w_in, (l + 1) * ATTN_W)
                    pe.wait_ge(wqkv_high, count(l + 1))
                    pe.wait_ge(wqkv_low, count(l + 1))
                project(n, step)
                project(n + 1, step - H)
                turn_qk(n, step)

            def attention(l):
                pe.wait_ge(f_added, count(l * 8))
                n = l * NSEQ
                heads(n, 0, first=True)
                with pe.Fori(0, NSEQ // 2 - 2) as i:
                    heads(n + 2 * i + 1, 1)
                    heads(n + 2 * i + 2, 0)
                heads(n + NSEQ - 3, 1)
                heads(n + NSEQ - 2, 0, ahead=1)
                heads(n + NSEQ - 1, 1, ahead=0)
                n = n + NSEQ - 1
                for h in range(H - MIX_LAG, H):
                    if h >= H - TURN_LAG:
                        turn(n, h, False)
                    mix(n, 1, h)
                out_product(n, 1, 0)
                out_product(n, 1, 1)

            def f_in(m):
                pe.wait_ge(f_staged, count(m + 1))
                for k in range(4):
                    t = pe.transpose(trn_ps[:, k * P:(k + 1) * P], xs4[:, k], c["ident"][:])
                t.then_inc(f_t1, 1)

            def f_return(m):
                pe.wait_ge(f_shifted, count(m + 1))
                for k in range(4):
                    t = pe.transpose(back_ps[:, k * P:(k + 1) * P],
                                     xT4[:, k // 2, (k % 2) * P:(k % 2) * P + P], c["ident"][:])
                t.then_inc(f_back, 1)

            def f_norm(m):
                pe.wait_ge(f_xn, count(4 * m + 4))
                for k in range(4):
                    t = pe.transpose(trn_ps[:, k * P:(k + 1) * P], xn[:, k], c["ident"][:])
                t.then_inc(f_t3, 1)

            def f_hidden(m, t):
                at, rows = FT[t]
                if t == 0:
                    pe.wait_ge(f_xnT, count(m + 1))
                    pe.wait_ge(f_low, count(m + 1))
                u = 3 * m + t
                if t >= 2:
                    pe.wait_ge(f_gelu, count(u - 1))
                    pe.wait_ge(f_h, count(u - 1))
                else:
                    pe.wait_ge(f_h, count(3 * m))
                split_product(gate_ps[t % 2][0:rows, :], w1_hi[:, FH + at:FH + at + rows],
                              w1_lo[:, FH + at:FH + at + rows], xnT_hi[:], xnT_lo[:]).then_inc(f_gate, 1)
                split_product(up_ps[t % 2][0:rows, :], w1_hi[:, at:at + rows], w1_lo[:, at:at + rows],
                              xnT_hi[:], xnT_lo[:]).then_inc(f_up, 1)

            def f_output(m):
                pe.wait_ge(f_h, count(3 * m + 3))
                pe.wait_ge(f_added, count(m))
                for k in range(4):
                    for t, (at, rows) in enumerate(FT):
                        i = pe.matmul(out_ps[:, k * P:(k + 1) * P], hT[0:rows, t, k * P:(k + 1) * P],
                                      w2[0:rows, t], start=(t == 0), stop=(t == 2))
                i.then_inc(f_out, 1)

            def feed(l, g, front, ahead):
                m = 8 * l + g
                for t in range(3):
                    f_hidden(m, t)
                    if front:
                        (f_in, f_return, f_norm)[t](m + 1)
                    if ahead:
                        for step in beside_feed(g, t):
                            prepare(l + 1, step)
                f_output(m)

            def layer(l, last):
                attention(l)
                pe.wait_ge(attn_added, count((l + 1) * NSEQ))
                pe.wait_ge(ffn_w_in, (l + 1) * FFN_W)
                pe.wait_ge(w1_high, count(l + 1))
                pe.wait_ge(w1_low, count(l + 1))
                f_in(8 * l)
                f_return(8 * l)
                f_norm(8 * l)
                if last:
                    with pe.Fori(0, 7) as g:
                        feed(l, g, True, False)
                    feed(l, 7, False, False)
                else:
                    for g in range(8):
                        feed(l, g, g < 7, True)

            pe.wait_ge(filled, count(9))
            for step in range(FIRST_STEP, H):
                prepare(0, step)
            if DEPTH > 1:
                with pe.Fori(0, DEPTH - 1) as l:
                    layer(l, last=False)
            layer(DEPTH - 1, last=True)

        @block.scalar
        def _(act):
            def project(n, par, step, first=False):
                if step not in PROJ_STEPS:
                    return
                slot = PROJ_STEPS.index(step)
                act.wait_ge(proj_full, count(n * PROJ + slot + 1))
                if slot == 0:
                    act.activation(xT_hi[0:64, 0:SEQ], gen[0:64, 0:SEQ], ACT.Copy)
                    act.activation(xT_hi[64:128, 1:SEQ + 1], gen[64:128, 0:SEQ], ACT.Copy).then_inc(x_high, 1)
                else:
                    k, part, a = PROJ_ORDER[slot - 1]
                    cols = slice(a * 512, a * 512 + 512)
                    if part == 2:
                        t = act.activation(V[:, par, k, cols], gen[:], ACT.Copy)
                    else:
                        if a == 0 and not first:
                            act.wait_ge(rotated, count(n * 4 - 4 + 2 * k + part + 1))
                        t = act.activation(raw[:, part, k, cols], gen[:], ACT.Copy)
                    t.then_inc(proj_drained, 1)

            def keep_turn(n, par, step):
                if step not in TURN_STEPS:
                    return
                slot = TURN_STEPS.index(step)
                k, rest = divmod(slot, 4)
                part, a = divmod(rest, 2)
                act.wait_ge(turn_full, count(n * TURN + slot + 1))
                act.activation((qT, kT)[part][:, par, 4 * a:4 * a + 4, k * P:(k + 1) * P],
                               trn[:].rearrange("p (r t) -> p r t", t=P), ACT.Copy).then_inc(turn_kept, 1)

            def exps(n, par, h, first):
                N = n * H + h
                act.wait_ge(bias_ready, count(N + 1))
                if not (first and h < 4):
                    act.wait_ge(turned, count(N - 3))
                p, s = pr[:, h % 4], sco[h % 2]
                act.activation(p[:, 0:P], s[:, 32:160], ACT.Exp, bias=nb[:, h % 4, 0:1],
                               scale=rq8[:, par, 0, h:h + 1], accum_out=den[:, h % 4, 0:1])
                act.activation(p[:, 2 * P - WIN:3 * P], s[:, 160:320], ACT.Exp, bias=nb[:, h % 4, 1:2],
                               scale=rq8[:, par, 1, h:h + 1], accum_out=den[:, h % 4, 1:2]).then_inc(exped, 1)

            def drain_turn(n, h, first):
                N = n * H + h
                act.wait_ge(turned, count(N + 1))
                if not (first and h < 2):
                    act.wait_ge(mixed, count(N - 1))
                act.activation(prT[:, h % 2], tur[h % 2][:, 0:288], ACT.Copy).then_inc(turn_drained, 1)

            def drain_pair(n, par, r):
                act.wait_ge(mixed, count(n * H + 2 * r + 2))
                act.activation(oT[:, par, r], acc[:, 0:SEQ], ACT.Copy).then_inc(head_out, 1)

            def split_wqkv(l, piece):
                if piece == 0:
                    act.wait_ge(wqkv_in, (l + 1) * WQKV)
                cols = slice(piece * INNER, (piece + 1) * INNER)
                t = act.activation(wqkv_hi[:, cols], wqkv[:, cols], ACT.Copy)
                if piece == 2:
                    t.then_inc(wqkv_high, 1)

            def split_w1(l):
                act.wait_ge(ffn_w_in, (l + 1) * FFN_W)
                act.activation(w1_hi[:], w1[:], ACT.Copy).then_inc(w1_high, 1)

            def heads(n, par, first=False, ahead=2, split=None):
                for h in range(H):
                    if ahead == 0 and split is not None and h in SPLIT_STEPS:
                        split_wqkv(split, SPLIT_STEPS.index(h))
                    if ahead >= 1:
                        project(n + 1, 1 - par, h)
                    if ahead >= 2:
                        project(n + 2, par, h - H)
                    if h >= TURN_LAG:
                        drain_turn(n, h - TURN_LAG, first)
                    elif not first:
                        drain_turn(n - 1, h + H - TURN_LAG, False)
                    exps(n, par, h, first)
                    if h >= DRAIN_LAG and (h - DRAIN_LAG) % 2 == 0:
                        drain_pair(n, par, (h - DRAIN_LAG) // 2)
                    elif not first and h < DRAIN_LAG and (h - DRAIN_LAG) % 2 == 0:
                        drain_pair(n - 1, 1 - par, PAIRS + (h - DRAIN_LAG) // 2)
                    if ahead >= 1:
                        keep_turn(n + 1, 1 - par, h)

            def prepare(l, step, first=False):
                n = l * NSEQ
                project(n, 0, step, first)
                project(n + 1, 1, step - H)
                keep_turn(n, 0, step)

            def attention(l, last):
                act.wait_ge(f_added, count(l * 8))
                n = l * NSEQ
                heads(n, 0, first=True)
                with act.Fori(0, NSEQ // 2 - 2) as i:
                    heads(n + 2 * i + 1, 1)
                    heads(n + 2 * i + 2, 0)
                heads(n + NSEQ - 3, 1)
                heads(n + NSEQ - 2, 0, ahead=1)
                heads(n + NSEQ - 1, 1, ahead=0, split=None if last else l + 1)
                for h in range(H - TURN_LAG, H):
                    drain_turn(n + NSEQ - 1, h, False)
                    drain_pair(n + NSEQ - 1, 1, h - H // 2)
                split_w1(l)

            def f_shift(m):
                act.wait_ge(f_t1, count(m + 1))
                for s in range(2):
                    act.activation(xT4[0:64, s, 0:SEQ], trn_ps[0:64, s * SEQ:(s + 1) * SEQ], ACT.Copy)
                    t = act.activation(xT4[64:128, s, 1:SEQ + 1], trn_ps[64:128, s * SEQ:(s + 1) * SEQ], ACT.Copy)
                t.then_inc(f_shifted, 1)

            def f_affine(m):
                act.wait_ge(f_t3, count(m + 1))
                act.activation(xnT_hi[:], trn_ps[:], ACT.Identity, bias=lnb[:], scale=lng[:])
                act.activation(xnT, trn_ps[:], ACT.Identity, bias=lnb[:], scale=lng[:]).then_inc(f_xnT, 1)

            def f_gelus(m, t):
                rows = FT[t][1]
                u = 3 * m + t
                act.wait_ge(f_gate, count(u + 1))
                if t == 2:
                    act.wait_ge(f_h, count(u - 1))
                act.activation(gl[0:rows, t % 2], gate_ps[t % 2][0:rows, :], ACT.Gelu,
                               bias=b1[0:rows, 3 + t:4 + t]).then_inc(f_gelu, 1)

            def feed(l, g, front, ahead):
                m = 8 * l + g
                for t in range(3):
                    f_gelus(m, t)
                    if front and t == 0:
                        f_shift(m + 1)
                    if front and t == 2:
                        f_affine(m + 1)
                    if ahead:
                        for step in beside_feed(g, t):
                            prepare(l + 1, step)

            def layer(l, last):
                act.preload_act_table(ACT.Exp)
                attention(l, last)
                act.preload_act_table(ACT.Gelu)
                act.wait_ge(attn_added, count((l + 1) * NSEQ))
                act.wait_ge(ffn_w_in, (l + 1) * FFN_W)
                f_shift(8 * l)
                f_affine(8 * l)
                if last:
                    with act.Fori(0, 7) as g:
                        feed(l, g, True, False)
                    feed(l, 7, False, False)
                else:
                    for g in range(8):
                        feed(l, g, g < 7, True)

            act.wait_ge(filled, count(6))
            act.activation(xT_hi[64:128, 0:1], zero[64:128, 0:1], ACT.Copy)
            act.activation(xT_lo[64:128, 0:1], zero[64:128, 0:1], ACT.Copy).then_inc(filled, 1)
            for piece in range(3):
                split_wqkv(0, piece)
            for step in range(FIRST_STEP, H):
                prepare(0, step, True)
            if DEPTH > 1:
                with act.Fori(0, DEPTH - 1) as l:
                    layer(l, last=False)
            layer(DEPTH - 1, last=True)

        @block.vector
        def _(dve):
            def heads_of(ap):
                return ap.rearrange("p (h d) -> p h d", d=HD)

            def reduce_sq(n, k, part):
                j = n * 4 + 2 * k + part
                dve.wait_ge(squared, count(j + 1))
                dve.tensor_reduce(ss[:, k, part * H:(part + 1) * H], heads_of(sq[:, part]), AX.X,
                                  ALU.add).then_inc(reduced, 1)

            def cosine(n, k, part, first):
                j = n * 4 + 2 * k + part
                dve.wait_ge(proj_drained, count(n * PROJ + slot_qkv(k, part) + 1))
                if not (first and k == 0):
                    dve.wait_ge(rotated, count(j - 1))
                dve.tensor_tensor(heads_of(t1[:, part]), heads_of(raw[:, part, k]),
                                  table[:, part, 0, k][:, None, :].to_broadcast([P, H, HD]),
                                  ALU.mult).then_inc(cos_part, 1)

            def add_parts(n, k, part, first):
                j = n * 4 + 2 * k + part
                dve.wait_ge(cos_part, count(j + 1))
                dve.wait_ge(sin_part, count(2 * j + 2))
                if k == 1:
                    dve.wait_ge(turn_full, count(n * TURN + slot_turn(0, part) + 1))
                elif not first:
                    dve.wait_ge(turn_full, count(n * TURN - TURN + slot_turn(1, part) + 1))
                dve.tensor_tensor(rot[:, part], t1[:, part], t2[:, part],
                                  ALU.add).then_inc(rotated if part == 0 else summed, 1)

            def clamp(n, k):
                dve.wait_ge(reduced, count(n * 4 + 2 * k + 2))
                dve.tensor_scalar(ssc[:, k], ss[:, k], 1e-24, None, ALU.max).then_inc(clamped, 1)

            def scale_block(n, par, k):
                dve.wait_ge(inv_norm, count(2 * n + k + 1))
                dve.tensor_scalar(rq8[:, par, k], rs[:, k, 0:H], 8.0, None, ALU.mult).then_inc(q_scaled, 1)
                dve.wait_ge(summed, count(2 * n + k + 1))
                dve.tensor_tensor(heads_of(rot[:, 1]), heads_of(rot[:, 1]),
                                  rs[:, k, H:2 * H][:, :, None].to_broadcast([P, H, HD]),
                                  ALU.mult).then_inc(rotated, 1)

            def project(n, par, step, first=False):
                if step == FIRST_STEP:
                    low_x(n)
                for k in range(2):
                    if step == (-3, 4)[k]:
                        reduce_sq(n, k, 0)
                    if step == (-4, 5)[k]:
                        cosine(n, k, 0, first)
                    if step == (-1, 7)[k]:
                        add_parts(n, k, 0, first)
                    if step == (0, 8)[k]:
                        reduce_sq(n, k, 1)
                        clamp(n, k)
                    if step == (0, 8)[k]:
                        cosine(n, k, 1, first)
                    if step == (2, 9)[k]:
                        add_parts(n, k, 1, first)
                    if step == (3, 11)[k]:
                        scale_block(n, par, k)

            def maxima(n, par, h, first):
                N = n * H + h
                dve.wait_ge(scored, count(N + 1))
                if h == 0:
                    dve.wait_ge(q_scaled, count(2 * n + 2))
                if not (first and h < 4):
                    dve.wait_ge(exped, count(N - 3))
                dve.tensor_reduce(mx[:, h % 4], sco[h % 2][:, 0:320].rearrange("p (k j) -> p k j", k=2),
                                  AX.X, ALU.max).then_inc(maxed, 1)
                dve.wait_ge(maxed, count(N + 1))
                dve.scalar_tensor_tensor(out=nb[:, h % 4], in0=mx[:, h % 4], scalar=-1.0,
                                         in1=rq8[:, par, :, h], op0=ALU.mult, op1=ALU.mult).then_inc(bias_ready, 1)

            def normalise(n, h):
                N = n * H + h
                dve.wait_ge(exped, count(N + 1))
                dve.reciprocal(rden[:, h % 4], den[:, h % 4]).then_inc(recips, 1)
                dve.wait_ge(recips, count(N + 1))
                p = pr[:, h % 4]
                dve.tensor_scalar(p[:, 0:P], p[:, 0:P], rden[:, h % 4, 0:1], None, ALU.mult)
                dve.tensor_scalar(p[:, 2 * P - WIN:3 * P], p[:, 2 * P - WIN:3 * P], rden[:, h % 4, 1:2], None,
                                  ALU.mult).then_inc(normed, 1)

            def add_attn(n, l, s):
                dve.wait_ge(projected, count(n + 1))
                x = X[:, bass.ds(2 * s, 2), :]
                dve.tensor_tensor(x, x, wop[:, 0:SEQ].rearrange("p (k d) -> p k d", k=2),
                                  ALU.add).then_inc(attn_added, 1)

            def heads(l, s, par, first=False, ahead=2):
                n = l * NSEQ + s
                for h in range(H):
                    maxima(n, par, h, first)
                    if h >= 1:
                        normalise(n, h - 1)
                    elif not first:
                        normalise(n - 1, H - 1)
                    if ahead >= 1:
                        project(n + 1, 1 - par, h)
                    if ahead >= 2:
                        project(n + 2, par, h - H)
                    if h == ADD_STEP and not first:
                        add_attn(n - 1, l, s - 1)

            def low_x(n):
                dve.wait_ge(x_high, count(n + 1))
                dve.tensor_tensor(xT_lo[0:64, 0:SEQ], gen[0:64, 0:SEQ], xT_hi[0:64, 0:SEQ].bitcast(F32), ALU.subtract)
                dve.tensor_tensor(xT_lo[64:128, 1:SEQ + 1], gen[64:128, 0:SEQ],
                                  xT_hi[64:128, 1:SEQ + 1].bitcast(F32), ALU.subtract).then_inc(proj_drained, 1)

            def make_tables(l):
                dve.wait_ge(attn_w_in, (l + 1) * ATTN_W)
                dve.wait_ge(wqkv_high, count(l + 1))
                dve.wait_ge(wqkv_low, count(l + 1))
                dve.wait_ge(cos_part, count(l * NSEQ * 4))
                dve.wait_ge(sin_part, count(l * NSEQ * 8))
                for part in range(2):
                    for k in range(2):
                        dve.tensor_tensor(table[:, part, 0, k], rope[:, part, 0, k], qks[:, part], ALU.mult)
                        for a in range(2):
                            i = dve.tensor_tensor(table[:, part, 1, k, 32 * a:32 * a + 32],
                                                  rope[:, part, 1, k, 32 * a:32 * a + 32],
                                                  qks[:, part, 32 - 32 * a:64 - 32 * a], ALU.mult)
                i.then_inc(tables, 1)
                dve.wait_ge(tables, count(l + 1))

            def prepare(l, step, first=False):
                n = l * NSEQ
                project(n, 0, step, first)
                project(n + 1, 1, step - H)

            def attention(l):
                dve.wait_ge(f_added, count(l * 8))
                n = l * NSEQ
                heads(l, 0, 0, first=True)
                with dve.Fori(0, NSEQ // 2 - 2) as i:
                    heads(l, 2 * i + 1, 1)
                    heads(l, 2 * i + 2, 0)
                heads(l, NSEQ - 3, 1)
                heads(l, NSEQ - 2, 0, ahead=1)
                heads(l, NSEQ - 1, 1, ahead=0)
                n = n + NSEQ - 1
                normalise(n, H - 1)
                add_attn(n, l, NSEQ - 1)

            def f_stat(m):
                dve.wait_ge(f_back, count(m + 1))
                dve.wait_ge(f_xn, count(4 * m))
                for k in range(4):
                    i = dve.bn_stats(st[:, k], back_ps[:, k * P:(k + 1) * P])
                i.then_inc(f_stats, 1)
                dve.wait_ge(f_cleared, count(m))
                dve.wait_ge(f_stats, count(m + 1))
                dve.memset(tick[:], 0.0).then_inc(f_cleared, 1)
                for k in range(4):
                    i = dve.bn_aggr(mv[:, k], st[:, k])
                i.then_inc(f_mv, 1)
                dve.wait_ge(f_mv, count(m + 1))
                dve.tensor_scalar(ve[:], mv[:, :, 1], EPS_LN, None, ALU.add).then_inc(f_ve, 1)

            def f_normal(m):
                dve.wait_ge(f_rstd, count(m + 1))
                for k in range(4):
                    dve.tensor_scalar(xn[:, k], back_ps[:, k * P:(k + 1) * P], mv[:, k, 0:1], rstd[:, k:k + 1],
                                      ALU.subtract, ALU.mult).then_inc(f_xn, 1)

            def f_gated(m, t):
                rows = FT[t][1]
                u = 3 * m + t
                dve.wait_ge(f_up, count(u + 1))
                dve.wait_ge(f_gelu, count(u + 1))
                if t == 0:
                    dve.wait_ge(f_out, count(m))
                dve.scalar_tensor_tensor(out=hT[0:rows, t], in0=up_ps[t % 2][0:rows, :],
                                         scalar=b1[0:rows, t:t + 1], in1=gl[0:rows, t % 2],
                                         op0=ALU.add, op1=ALU.mult).then_inc(f_h, 1)

            def f_add(m, g):
                dve.wait_ge(f_out, count(m + 1))
                dve.wait_ge(f_bias, count(m + 1))
                x = X[:, bass.ds(4 * g, 4), :]
                dve.tensor_tensor(x, x, out_ps[:].rearrange("p (k d) -> p k d", k=4), ALU.add).then_inc(f_added, 1)

            def f_low_part(m):
                dve.wait_ge(f_xnT, count(m + 1))
                dve.tensor_tensor(xnT_lo[:], xnT, xnT_hi[:].bitcast(F32), ALU.subtract).then_inc(f_low, 1)

            def feed(l, g, front, ahead):
                m = 8 * l + g
                for t in range(3):
                    f_gated(m, t)
                    if front and t == 1:
                        f_stat(m + 1)
                    if front and t == 2:
                        f_normal(m + 1)
                    if ahead:
                        for step in beside_feed(g, t):
                            prepare(l + 1, step)
                if front:
                    f_low_part(m + 1)
                f_add(m, g)

            def layer(l, last):
                attention(l)
                dve.wait_ge(ffn_w_in, (l + 1) * FFN_W)
                f_stat(8 * l)
                f_normal(8 * l)
                f_low_part(8 * l)
                if last:
                    with dve.Fori(0, 7) as g:
                        feed(l, g, True, False)
                    feed(l, 7, False, False)
                else:
                    for g in range(8):
                        feed(l, g, g < 7, True)
                        if g == 0:
                            make_tables(l + 1)

            dve.memset(half[:], -0.5).then_inc(filled, 1)
            dve.memset(xT4[64:128, :, 0:1], 0.0).then_inc(filled, 1)
            dve.memset(pr[:, :, P:2 * P], 0.0).then_inc(filled, 1)
            dve.memset(zero[:], 0.0).then_inc(filled, 1)
            dve.memset(den[:], 0.0).then_inc(filled, 1)
            dve.memset(mx[:], 0.0).then_inc(filled, 1)
            dve.wait_ge(filled, count(6))
            dve.wait_ge(const_in, 32)
            dve.tensor_copy(band[:], band32).then_inc(filled, 1)
            dve.tensor_copy(identb[:], c["ident"][:]).then_inc(filled, 1)
            make_tables(0)
            for step in range(FIRST_STEP, H):
                prepare(0, step, True)
            if DEPTH > 1:
                with dve.Fori(0, DEPTH - 1) as l:
                    layer(l, last=False)
            layer(DEPTH - 1, last=True)

        @block.gpsimd
        def _(pool):
            def square(n, k, part, first):
                j = n * 4 + 2 * k + part
                pool.wait_ge(proj_drained, count(n * PROJ + slot_qkv(k, part) + 1))
                if not (first and k == 0):
                    pool.wait_ge(reduced, count(j - 1))
                pool.tensor_tensor(sq[:, part], raw[:, part, k], raw[:, part, k], ALU.mult).then_inc(squared, 1)

            def sine(n, k, part, first):
                j = n * 4 + 2 * k + part
                if not (first and k == 0):
                    pool.wait_ge(rotated, count(j - 1))
                src = raw[:, part, k].rearrange("p (h a d) -> p h a d", h=H, a=2)
                dst = t2[:, part].rearrange("p (h a d) -> p h a d", h=H, a=2)
                for a in range(2):
                    pool.tensor_tensor(dst[:, :, a], src[:, :, 1 - a],
                                       table[:, part, 1, k, 32 * a:32 * a + 32][:, None, :].to_broadcast([P, H, 32]),
                                       ALU.mult).then_inc(sin_part, 1)

            def inverse(n, k):
                pool.wait_ge(clamped, count(2 * n + k + 1))
                pool.tensor_tensor(rs[:, k], ssc[:, k], half[:], ALU.pow).then_inc(inv_norm, 1)

            def stage(l, s):
                if isinstance(s, int):
                    if s > 0:
                        pool.wait_ge(proj_full, count((l * NSEQ + s - 1) * PROJ + 1))
                    pool.tensor_tensor(xs[:], X[:, 2 * s:2 * s + 2], zero[:, None, :].to_broadcast([P, 2, D]),
                                       ALU.add).then_inc(staged, 1)
                else:
                    pool.wait_ge(proj_full, count((l * NSEQ + s - 1) * PROJ + 1))
                    pool.tensor_copy(xs[:], X[:, bass.ds(2 * s, 2), :]).then_inc(staged, 1)

            def low_wqkv(l):
                pool.wait_ge(wqkv_high, count(l + 1))
                pool.tensor_tensor(wqkv_lo[:], wqkv, wqkv_hi[:].bitcast(F32), ALU.subtract).then_inc(wqkv_low, 1)

            def low_w1(l):
                pool.wait_ge(w1_high, count(l + 1))
                pool.tensor_tensor(w1_lo[:], w1[:], w1_hi[:].bitcast(F32), ALU.subtract).then_inc(w1_low, 1)

            def rotation(l, s, unit, first=False):
                square(l * NSEQ + s, unit // 2, unit % 2, first)
                sine(l * NSEQ + s, unit // 2, unit % 2, first)

            def project(l, s, first=False, last=False):
                rotation(l, s, 0, first)
                rotation(l, s, 1, first)
                inverse(l * NSEQ + s, 0)
                rotation(l, s, 2)
                if not last:
                    stage(l, s + 1)
                rotation(l, s, 3)
                inverse(l * NSEQ + s, 1)

            def f_stage(l, g):
                m = 8 * l + g
                pool.wait_ge(f_t1, count(m))
                x = X[:, bass.ds(4 * g, 4), :]
                if isinstance(g, int):
                    pool.tensor_tensor(xs4, x, zero[:, None, :].to_broadcast([P, 4, D]), ALU.add).then_inc(f_staged, 1)
                else:
                    pool.tensor_copy(xs4, x).then_inc(f_staged, 1)
                pool.wait_ge(f_ve, count(m + 1))
                pool.tensor_tensor(rstd[:], ve[:], half[:, 0:4], ALU.pow).then_inc(f_rstd, 1)
                pool.tensor_tensor(x, x, b2[:, None, :].to_broadcast([P, 4, D]), ALU.add).then_inc(f_bias, 1)

            def next_layer(l, g):
                if g == 1:
                    pool.wait_ge(f_added, count(8 * l + 1))
                    stage(l + 1, 0)
                    pool.wait_ge(tables, count(l + 2))
                if g in (2, 3, 5):
                    rotation(l + 1, 0, {2: 0, 3: 1, 5: 3}[g])
                if g == 4:
                    inverse((l + 1) * NSEQ, 0)
                    rotation(l + 1, 0, 2)
                if g == 5:
                    stage(l + 1, 1)
                if g == 6:
                    inverse((l + 1) * NSEQ, 1)

            def layer(l, last):
                with pool.Fori(1, NSEQ - 1) as s:
                    project(l, s)
                project(l, NSEQ - 1, last=True)
                if not last:
                    low_wqkv(l + 1)
                low_w1(l)
                pool.wait_ge(attn_added, count((l + 1) * NSEQ))
                pool.wait_ge(ffn_w_in, (l + 1) * FFN_W)
                f_stage(l, 0)
                if last:
                    with pool.Fori(1, 8) as g:
                        f_stage(l, g)
                else:
                    for g in range(1, 8):
                        f_stage(l, g)
                        next_layer(l, g)

            pool.wait_ge(filled, count(7))
            low_wqkv(0)
            pool.wait_ge(tables, count(1))
            stage(0, 0)
            project(0, 0, True)
            if DEPTH > 1:
                with pool.Fori(0, DEPTH - 1) as l:
                    layer(l, last=False)
            layer(DEPTH - 1, last=True)

def network(nc, c, w, out):
    with ExitStack() as ctx:
        X = ctx.enter_context(nc.sbuf_tensor("X", [P, NBLK, D], F32))
        ident = ctx.enter_context(nc.sbuf_tensor("ident", [P, P], F32))
        x_in = ctx.enter_context(nc.semaphore("x_in"))
        x_out = ctx.enter_context(nc.semaphore("x_out"))
        with nc.Block() as block:
            @block.sync
            def _(sp):
                for s in range(NSEQ):
                    sp.dma_start(X[:, 2 * s:2 * s + 2, :],
                                 w["L0_attn_x"][s].rearrange("(k p) d -> p k d", p=P)).then_inc(x_in, 16)
                sp.dma_start(ident[:], c["ident"]).then_inc(x_in, 16)
                sp.wait_ge(x_in, 16 * (NSEQ + 1))
        c = dict(c, ident=ident)

        def part(prefix):
            return {k[len(prefix):]: v for k, v in w.items() if k.startswith(prefix)}

        linear_stage(nc, X, c, part("L0_attn_"))
        norm_stage(nc, X, "_n0")
        expert_stage(nc, X, c, part("L0_ffn_"))
        norm_stage(nc, X, "_n1")
        feature_stage(nc, X, c, part("L1_attn_"))
        X0 = ctx.enter_context(nc.sbuf_tensor("X0", [P, NBLK, D], F32))
        norm_stage(nc, X, "_n2", keep=X0)
        deep_stage(nc, X, c, part("L1_ffn_"))
        norm_stage(nc, X, "_n3", residual=X0)
        with nc.Block() as block:
            @block.sync
            def _(sp):
                for s in range(NSEQ):
                    sp.dma_start(out[s].rearrange("(k p) d -> p k d", p=P),
                                 X[:, 2 * s:2 * s + 2, :]).then_inc(x_out, 16)
                sp.wait_ge(x_out, 16 * NSEQ)


def shape_constants():
    f = np.float32
    half = np.arange(0, HD, 2, dtype=f)
    inv_freq = (f(1.0) / f(10000.0) ** (half / f(HD))).astype(f)
    t = np.arange(SEQ, dtype=f)
    freqs = t[:, None] * inv_freq[None, :]
    base = (half + f(0.4 * HD)) / f(1.4 * HD)
    scale = (base[None, :] ** ((t - SEQ // 2) / f(WIN // 2))[:, None]).astype(f)
    cos, sin = np.cos(freqs), np.sin(freqs)
    rope = np.zeros((P, 2, 2, 2, HD), f)
    for part, s in enumerate((scale, f(1.0) / scale)):
        for kind, table in enumerate(([cos * s, cos * s], [-sin * s, sin * s])):
            rope[:, part, kind] = np.concatenate(table, 1).reshape(2, P, HD).transpose(1, 0, 2)
    i = np.arange(P)[:, None]
    band = np.full((P, 320), NEG, f)
    for at, j in ((WIN, np.arange(P)), (P + WIN, np.arange(P + WIN) - WIN)):
        band[:, at:at + len(j)] = np.where((i >= j) & (i <= j + WIN), 0.0, NEG)
    j = np.arange(P)[None, :]
    upper = (i <= j).astype(f)
    return {
        "ident": np.eye(P, dtype=f),
        "rope": rope,
        "band": band,
        "causal": np.concatenate([upper, np.ones((P, P), f), upper], 1),
        "heads32": (i // 32 == j // 32).astype(f),
        "rank8": np.tile(np.arange(8, 0, -1, dtype=f), (P, 1)),
    }


def laid_out(inputs):
    a = {k: np.asarray(v) for k, v in inputs.items()}
    turn = {"L0_ffn_gate_w": (1, 0), "L0_ffn_sw1": (1, 0), "L0_ffn_sw2": (1, 0), "L0_ffn_sw3": (1, 0),
            "L0_ffn_w1": (2, 0, 1), "L0_ffn_w2": (2, 0, 1), "L0_ffn_w3": (2, 0, 1)}
    for k, axes in turn.items():
        a[k] = a[k].transpose(axes)
    a["L1_attn_WqT"] = a.pop("L1_attn_Wq").T
    a["L1_attn_WkT"] = a.pop("L1_attn_Wk").T
    b1 = a["L1_ffn_b1"]
    tiles = np.zeros((DEPTH, P, 6), b1.dtype)
    for side in range(2):
        for t, (at, rows) in enumerate(FT):
            tiles[:, :rows, 3 * side + t] = b1[:, FH * side + at:FH * side + at + rows]
    a["L1_ffn_b1"] = tiles
    return {k: np.ascontiguousarray(v) for k, v in a.items()}


def kernel(**inputs):
    import concourse.bacc as bacc
    from concourse.bass_utils import run_bass_kernel_spmd

    nc = bacc.Bacc("TRN2", target_bir_lowering=False, num_devices=1)
    arrays = {}

    def declare(name, a):
        arrays["in_" + name] = a
        return nc.dram_tensor("in_" + name, a.shape, mybir.dt.from_np(a.dtype), kind="ExternalInput").ap()

    w = {k: declare(k, a) for k, a in laid_out(inputs).items()}
    c = {k: declare("const_" + k, a) for k, a in shape_constants().items()}
    out = nc.dram_tensor("out_0", (NSEQ, SEQ, D), F32, kind="ExternalOutput").ap()
    network(nc, c, w, out)
    r = run_bass_kernel_spmd(nc, [arrays], core_ids=[0])
    return r.results[0]["out_0"]
```
